# Optimizing a Trainium2 kernel written in Bass

```python
import numpy as np
import jax
import jax.numpy as jnp

def _softmax(x, axis=-1):
    return jax.nn.softmax(x, axis=axis)

def _gelu(x):
    return jax.nn.gelu(x, approximate=True)

def _silu(x):
    return jax.nn.silu(x)

def _sigmoid(x):
    return jax.nn.sigmoid(x)

def _layernorm(x, axis=-1, eps=1e-05):
    m = jnp.mean(x, axis=axis, keepdims=True)
    v = jnp.var(x, axis=axis, keepdims=True)
    return (x - m) / jnp.sqrt(v + eps)

def _scatter_add(tgt, idx, src, axis=0):
    return tgt.at[idx].add(src)

def _segment_sum(src, seg, n):
    return jax.ops.segment_sum(src, seg, n)
kernel_name = 'mk_gnn_resnorm_d1_gnn_r8_0c11a3'

def setup_inputs(seed: int=0):
    np.random.seed(seed)
    _w = jnp.asarray

    def _rec_inputs():
        import jax
        import jax.numpy as jnp
        _gk = jax.random.key(seed)
        x = -8.776e-05 + 1 * jax.random.normal(jax.random.fold_in(_gk, 1), (6250, 256), jnp.float32)
        src = jax.random.randint(jax.random.fold_in(_gk, 2), (100000,), 0, 6250, jnp.int32)
        dst = jnp.minimum((6250 * jax.random.uniform(jax.random.fold_in(_gk, 3), (100000,)) ** 2.0).astype(jnp.int32), 49999)
        _o = jnp.argsort(dst, stable=True)
        src = src[_o]
        dst = dst[_o]
        edge_attr_64 = 1.36993e-05 + 0.999972 * jax.random.normal(jax.random.fold_in(_gk, 11), (100000, 64), jnp.float32)
        edge_weight = jax.random.uniform(jax.random.fold_in(_gk, 13), (100000,), jnp.float32, 0.0, 0.999998)
        return (x, src, dst, edge_attr_64, edge_weight)
    x, src, dst, edge_attr_64, edge_weight = _rec_inputs()

    def _L0_gnn_setup():
        import jax, jax.numpy as jnp
        import numpy as np
        N = 2500
        E = 40000
        D = 256
        H = 8
        DH = D // H
        ED = 64
        FF = 4 * D
        EPS = 1e-05

        def _layernorm(x, g, b):
            m = jnp.mean(x, axis=-1, keepdims=True)
            v = jnp.var(x, axis=-1, keepdims=True)
            return (x - m) * jax.lax.rsqrt(v + EPS) * g + b

        def _edge_attention(xn, edge_index, ef, ew, Wq, bq, Wk, bk, Wv, bv, We, be, Wo, bo):
            n = xn.shape[0]
            scale = DH ** (-0.5)
            q = (xn @ Wq + bq).reshape(n, H, DH)
            k = (xn @ Wk + bk).reshape(n, H, DH)
            v = (xn @ Wv + bv).reshape(n, H, DH)
            src, dst = (edge_index[0], edge_index[1])
            ep = ef @ We + be
            scores = jnp.einsum('ehd,ehd->eh', q[dst], k[src] + ep[:, None, :]) * scale
            scores = scores * ew[:, None]
            m = jax.ops.segment_max(scores, dst, num_segments=n)
            m = jnp.where(jnp.isfinite(m), m, 0.0)
            ex = jnp.exp(scores - m[dst])
            s = jax.ops.segment_sum(ex, dst, num_segments=n)
            attn = ex / s[dst]
            out = jax.ops.segment_sum(attn[:, :, None] * v[src], dst, num_segments=n)
            out = out.reshape(n, D) @ Wo + bo
            return out
        key = jax.random.key(seed)
        ks = jax.random.split(key, 32)

        def lin_w(k, i, o):
            return (jax.random.normal(k, (i, o), jnp.float32) / np.sqrt(i)).astype(jnp.float32)
        return {'x': jax.random.normal(ks[0], (N, D), jnp.float32), 'edge_features': jax.random.normal(ks[1], (E, ED), jnp.float32), 'edge_weights': jax.random.uniform(ks[2], (E,), jnp.float32), 'edge_index': jax.random.randint(ks[3], (2, E), 0, N, dtype=jnp.int32), 'Wq': lin_w(ks[4], D, D), 'bq': jnp.zeros((D,), jnp.float32), 'Wk': lin_w(ks[5], D, D), 'bk': jnp.zeros((D,), jnp.float32), 'Wv': lin_w(ks[6], D, D), 'bv': jnp.zeros((D,), jnp.float32), 'We': lin_w(ks[7], ED, DH), 'be': jnp.zeros((DH,), jnp.float32), 'Wo': lin_w(ks[8], D, D), 'bo': jnp.zeros((D,), jnp.float32), 'ln1_g': jnp.ones((D,), jnp.float32), 'ln1_b': jnp.zeros((D,), jnp.float32), 'ln2_g': jnp.ones((D,), jnp.float32), 'ln2_b': jnp.zeros((D,), jnp.float32), 'W1': lin_w(ks[9], D, FF), 'b1': jnp.zeros((FF,), jnp.float32), 'W2': lin_w(ks[10], FF, D), 'b2': jnp.zeros((D,), jnp.float32), 'alpha': jnp.ones((1,), jnp.float32), 'beta': jnp.ones((1,), jnp.float32)}
    _L0_gnn_all = _L0_gnn_setup()
    _L0_gnn_in = {k: v for k, v in _L0_gnn_all.items() if k in ('Wq', 'bq', 'Wk', 'bk', 'Wv', 'bv', 'We', 'be', 'Wo', 'bo', 'ln1_g', 'ln1_b', 'ln2_g', 'ln2_b', 'W1', 'b1', 'W2', 'b2', 'alpha', 'beta')}
    del _L0_gnn_all
    return {'x': x, 'src': src, 'dst': dst, 'edge_attr_64': edge_attr_64, 'edge_weight': edge_weight, 'L0_gnn_Wq': _L0_gnn_in['Wq'], 'L0_gnn_bq': _L0_gnn_in['bq'], 'L0_gnn_Wk': _L0_gnn_in['Wk'], 'L0_gnn_bk': _L0_gnn_in['bk'], 'L0_gnn_Wv': _L0_gnn_in['Wv'], 'L0_gnn_bv': _L0_gnn_in['bv'], 'L0_gnn_We': _L0_gnn_in['We'], 'L0_gnn_be': _L0_gnn_in['be'], 'L0_gnn_Wo': _L0_gnn_in['Wo'], 'L0_gnn_bo': _L0_gnn_in['bo'], 'L0_gnn_ln1_g': _L0_gnn_in['ln1_g'], 'L0_gnn_ln1_b': _L0_gnn_in['ln1_b'], 'L0_gnn_ln2_g': _L0_gnn_in['ln2_g'], 'L0_gnn_ln2_b': _L0_gnn_in['ln2_b'], 'L0_gnn_W1': _L0_gnn_in['W1'], 'L0_gnn_b1': _L0_gnn_in['b1'], 'L0_gnn_W2': _L0_gnn_in['W2'], 'L0_gnn_b2': _L0_gnn_in['b2'], 'L0_gnn_alpha': _L0_gnn_in['alpha'], 'L0_gnn_beta': _L0_gnn_in['beta']}

def reference(x, src, dst, edge_attr_64, edge_weight, L0_gnn_Wq, L0_gnn_bq, L0_gnn_Wk, L0_gnn_bk, L0_gnn_Wv, L0_gnn_bv, L0_gnn_We, L0_gnn_be, L0_gnn_Wo, L0_gnn_bo, L0_gnn_ln1_g, L0_gnn_ln1_b, L0_gnn_ln2_g, L0_gnn_ln2_b, L0_gnn_W1, L0_gnn_b1, L0_gnn_W2, L0_gnn_b2, L0_gnn_alpha, L0_gnn_beta):
    import jax
    import jax.numpy as jnp

    def _L0_gnn_ref(x, edge_features, edge_weights, edge_index, Wq, bq, Wk, bk, Wv, bv, We, be, Wo, bo, ln1_g, ln1_b, ln2_g, ln2_b, W1, b1, W2, b2, alpha, beta):
        import jax, jax.numpy as jnp
        import numpy as np
        N = 2500
        E = 40000
        D = 256
        H = 8
        DH = D // H
        ED = 64
        FF = 4 * D
        EPS = 1e-05

        def _layernorm(x, g, b):
            m = jnp.mean(x, axis=-1, keepdims=True)
            v = jnp.var(x, axis=-1, keepdims=True)
            return (x - m) * jax.lax.rsqrt(v + EPS) * g + b

        def _edge_attention(xn, edge_index, ef, ew, Wq, bq, Wk, bk, Wv, bv, We, be, Wo, bo):
            n = xn.shape[0]
            scale = DH ** (-0.5)
            q = (xn @ Wq + bq).reshape(n, H, DH)
            k = (xn @ Wk + bk).reshape(n, H, DH)
            v = (xn @ Wv + bv).reshape(n, H, DH)
            src, dst = (edge_index[0], edge_index[1])
            ep = ef @ We + be
            scores = jnp.einsum('ehd,ehd->eh', q[dst], k[src] + ep[:, None, :]) * scale
            scores = scores * ew[:, None]
            m = jax.ops.segment_max(scores, dst, num_segments=n)
            m = jnp.where(jnp.isfinite(m), m, 0.0)
            ex = jnp.exp(scores - m[dst])
            s = jax.ops.segment_sum(ex, dst, num_segments=n)
            attn = ex / s[dst]
            out = jax.ops.segment_sum(attn[:, :, None] * v[src], dst, num_segments=n)
            out = out.reshape(n, D) @ Wo + bo
            return out
        xn = _layernorm(x, ln1_g, ln1_b)
        attn_out = _edge_attention(xn, edge_index, edge_features, edge_weights, Wq, bq, Wk, bk, Wv, bv, We, be, Wo, bo)
        x = x + alpha * attn_out
        xn = _layernorm(x, ln2_g, ln2_b)
        ff = jax.nn.gelu(xn @ W1 + b1, approximate=False) @ W2 + b2
        x = x + beta * ff
        return x
    edge_index = jnp.stack([src, dst])
    x = _layernorm(x + _L0_gnn_ref(x, edge_attr_64, edge_weight, edge_index, L0_gnn_Wq, L0_gnn_bq, L0_gnn_Wk, L0_gnn_bk, L0_gnn_Wv, L0_gnn_bv, L0_gnn_We, L0_gnn_be, L0_gnn_Wo, L0_gnn_bo, L0_gnn_ln1_g, L0_gnn_ln1_b, L0_gnn_ln2_g, L0_gnn_ln2_b, L0_gnn_W1, L0_gnn_b1, L0_gnn_W2, L0_gnn_b2, L0_gnn_alpha, L0_gnn_beta), axis=-1)
    return x

_drawn_inputs = setup_inputs


def setup_inputs(seed=0):
    import zlib

    import numpy as np

    out = dict(_drawn_inputs(seed))
    spreads = {'L0_gnn_bq': (0.0, 0.468),
     'L0_gnn_bk': (0.0, 0.8),
     'L0_gnn_bv': (0.0, 0.1),
     'L0_gnn_be': (0.0, 0.8),
     'L0_gnn_bo': (0.0, 0.1),
     'L0_gnn_ln1_g': (1.0, 0.2),
     'L0_gnn_ln1_b': (0.0, 0.1),
     'L0_gnn_ln2_g': (1.0, 0.2),
     'L0_gnn_ln2_b': (0.0, 0.1),
     'L0_gnn_b1': (0.0, 0.1),
     'L0_gnn_b2': (0.0, 0.1)}
    factors = {}
    for name, (base, spread) in spreads.items():
        noise = np.random.default_rng([zlib.crc32(name.encode()), seed]).standard_normal(out[name].shape)
        drawn = base * np.exp(spread * noise) if base else spread * noise
        out[name] = jnp.asarray(drawn.astype(out[name].dtype))
    for name, factor in factors.items():
        out[name] = (out[name] * factor).astype(out[name].dtype)
    return out
```

```python
from contextlib import ExitStack

import concourse.bass as bass
from concourse import mybir
import numpy as np

P = 128
ITEM_GROUP = 4
CHUNKS = 16
GROUPS = CHUNKS // ITEM_GROUP
BIG = 1.0e30
EPS = 1.0e-5


def ceil_div(a, b):
    return -(-a // b)


def sizes(n_nodes, n_edges):
    blocks = ceil_div(n_nodes, P)
    tiles = ceil_div(n_edges, P)
    items = tiles + blocks - 1
    steps = ceil_div(items, CHUNKS)
    return dict(blocks=blocks, tiles=tiles, items=items, steps=steps, pairs=ceil_div(blocks, 2),
                tile_chunks=ceil_div(max(tiles, steps * CHUNKS) + 1, P),
                col_chunks=ceil_div((steps + 1) * CHUNKS, P))


def graph_layer(nc, A, n_nodes, n_edges, dims):
    D, H, ED, FF = dims
    DH = D // H
    DC = D // P
    FC = FF // P
    ROW = D + H
    Z = sizes(n_nodes, n_edges)
    BLOCKS, STEPS, PAIRS = Z["blocks"], Z["steps"], Z["pairs"]
    TCH, CCH = Z["tile_chunks"], Z["col_chunks"]
    COLS = STEPS * CHUNKS
    WIDE = CCH * P
    NTILES = 2 * PAIRS
    LINE = STEPS * P
    NEDGE = BLOCKS - 1
    fp32, bf16, i32 = mybir.dt.float32, mybir.dt.bfloat16, mybir.dt.int32
    ALU, ACT, AX = mybir.AluOpType, mybir.ActivationFunctionType, mybir.AxisListType
    ENG = mybir.EngineType
    ds = bass.ds

    ctx = ExitStack()
    with ctx:
        def sb(name, shape, dt):
            return ctx.enter_context(nc.sbuf_tensor("sb_" + name, shape, dt))

        def sem(name):
            return ctx.enter_context(nc.semaphore(name))

        def carve(region, at, shape, dt):
            n = int(np.prod(shape)) * (2 if dt == bf16 else 4)
            v = region[:, at // 4:(at + n) // 4]
            if dt != fp32:
                v = v.bitcast(dt)
            if len(shape) == 2:
                v = v.rearrange("p (a b) -> p a b", a=shape[0])
            if len(shape) == 3:
                v = v.rearrange("p (a b c) -> p a b c", a=shape[0], b=shape[1])
            return v, at + n

        r_q = sb("r_q", [P, max(NTILES * 3 * D // 2, NTILES * ROW)], fp32)
        r_line = sb("r_line", [P, max(NTILES * D, 2 * LINE)], fp32)
        r_item = sb("r_item", [P, 5 * WIDE], fp32)
        r_kt = sb("r_kt", [P, max(5 * WIDE, CHUNKS * ROW)], fp32)
        r_w = sb("r_w", [P, DC * D + DC * FF + FC * D], fp32)
        r_tmp = sb("r_tmp", [P, max(4608, COLS, LINE // 2 + 4 * P)], fp32)

        q3, _ = carve(r_q, 0, (NTILES, 3, D), bf16)
        sums, _ = carve(r_q, 0, (NTILES, ROW), fp32)
        QB = NTILES * 3 * D * 2
        reach = r_q[:, NTILES * ROW - LINE:NTILES * ROW]
        KEEP = (NTILES * ROW - LINE) // ROW
        x_all, _ = carve(r_line, 0, (NTILES, D), fp32)
        line = r_line[:, 0:LINE]
        fline = r_line[:, LINE:LINE + LINE // 2].bitcast(bf16)
        gline = r_line[:, LINE + LINE // 2:2 * LINE].bitcast(bf16)
        ex_all = r_line[:, LINE:2 * LINE]
        src_item, at = carve(r_item, 0, (WIDE,), i32)
        rel_item, at = carve(r_item, at, (WIDE,), fp32)
        ews_item, at = carve(r_item, at, (WIDE,), fp32)
        off_item, at = carve(r_item, at, (WIDE,), fp32)
        f_item, at = carve(r_item, at, (WIDE,), bf16)
        g_item, at = carve(r_item, at, (WIDE,), bf16)
        kt, _ = carve(r_kt, 0, (CHUNKS, ROW), fp32)
        g_dst, at = carve(r_kt, 0, (CCH, P), i32)
        rel_f, _ = carve(r_kt, 0, (CCH, P), fp32)
        g_prev, at1 = carve(r_kt, at, (CCH, P), i32)
        f_f, _ = carve(r_kt, at, (CCH, P), fp32)
        g_next, at2 = carve(r_kt, at1, (CCH, P), i32)
        g_f, _ = carve(r_kt, at1, (CCH, P), fp32)
        g_src, at3 = carve(r_kt, at2, (CCH, P), i32)
        src_f, _ = carve(r_kt, at2, (CCH, P), fp32)
        g_w, at4 = carve(r_kt, at3, (CCH, P), fp32)
        tail = QB - 4 * (2 * WIDE + TCH * NEDGE)
        assert tail > 0
        icol, at = carve(r_q, tail, (WIDE,), fp32)
        past, at = carve(r_q, at, (WIDE,), fp32)
        valid, _ = carve(r_item, 8 * WIDE, (CCH, P), fp32)
        off_f, _ = carve(r_item, 12 * WIDE, (CCH, P), fp32)
        ended, at = carve(r_q, at, (TCH, NEDGE), fp32)
        w_qkv, at = carve(r_w, 0, (DC, 3 * D), fp32)
        b_qkv, at = carve(r_w, at, (3 * D,), fp32)
        w_o, at = carve(r_w, 0, (DC, D), fp32)
        w_1, at = carve(r_w, at, (DC, FF), fp32)
        w_2, at = carve(r_w, at, (FC, D), fp32)
        xn, at = carve(r_tmp, 0, (2, D), fp32)
        xnT, at = carve(r_tmp, at, (2, DC, P), fp32)
        q32, at = carve(r_tmp, at, (2, D), fp32)
        qrest, at = carve(r_tmp, at, (2, D), fp32)
        kv, at = carve(r_tmp, at, (2, 2 * D), fp32)
        moments, at = carve(r_tmp, at, (NTILES, 2), fp32)
        rstd, at = carve(r_tmp, at, (NTILES,), fp32)
        shift, at = carve(r_tmp, at, (NTILES,), fp32)
        vare, at = carve(r_tmp, at, (NTILES,), fp32)
        efT, at = carve(r_tmp, 0, (CHUNKS, P), fp32)
        hot, at = carve(r_tmp, at, (CHUNKS, P), bf16)
        hotT, at = carve(r_tmp, at, (CHUNKS, P), bf16)
        raw, at = carve(r_tmp, at, (CHUNKS, H), fp32)
        scaled, at = carve(r_tmp, at, (CHUNKS, H), fp32)
        masked, at = carve(r_tmp, at, (CHUNKS, H), fp32)
        fwide, at = carve(r_tmp, at, (CHUNKS, H), bf16)
        gwide, at = carve(r_tmp, at, (CHUNKS, H), bf16)
        hot32, at = carve(r_tmp, 0, (CHUNKS, P), fp32)
        exslice, at = carve(r_tmp, at, (P,), fp32)
        junk, at = carve(r_tmp, 0, (LINE,), bf16)
        edge_row, at = carve(r_tmp, at, (2, P), fp32)
        carry_row, at = carve(r_tmp, at, (P + 2 * H,), fp32)
        tile_rowf, _ = carve(r_tmp, 0, (COLS,), fp32)
        att, at = carve(r_kt, 0, (2, D), fp32)
        attT, at = carve(r_kt, at, (DC, 2 * P), fp32)
        x_in, at = carve(r_kt, at, (2, D), fp32)
        x1, at = carve(r_kt, at, (2, D), fp32)
        both, at = carve(r_kt, at, (2, D), fp32)
        xn2, at = carve(r_kt, at, (2, D), fp32)
        xn2T, at = carve(r_kt, at, (DC, 2 * P), fp32)
        gelu, at = carve(r_tmp, 0, (FC, 2 * P), fp32)
        y_sum, at = carve(r_tmp, at, (2, D), fp32)
        y_out, at = carve(r_tmp, at, (2, D), fp32)
        bo_row, at = carve(r_tmp, at, (D,), fp32)
        b2_row, at = carve(r_tmp, at, (D,), fp32)
        bo_a, at = carve(r_tmp, at, (D,), fp32)
        b2_b, at = carve(r_tmp, at, (D,), fp32)

        ident = sb("ident", [P, P], fp32)
        identb = sb("identb", [P, P], bf16)
        iota = sb("iota", [P, P], fp32)
        iotab = sb("iotab", [P, P], bf16)
        ones = sb("ones", [P, 1], fp32)
        index = sb("index", [P, CHUNKS], i32)
        tile_index = sb("tile_index", [P, CCH], i32)
        b7 = sb("b7", [P, CCH], fp32)
        b128 = sb("b128", [P, CCH], fp32)
        t7 = sb("t7", [P, CCH], fp32)
        last_i = sb("last_i", [P, TCH], i32)
        last_f = sb("last_f", [P, TCH], fp32)
        thr = sb("thr", [P, NEDGE], fp32)
        ends = sb("ends", [P, 1], fp32)
        bcol = sb("bcol", [P, 1], fp32)
        block_row = sb("block_row", [1, COLS + CHUNKS], i32)
        tile_row = sb("tile_row", [1, COLS + CHUNKS], i32)
        halfneg = sb("halfneg", [P, NTILES], fp32)
        cols = sb("cols", [P, 4 * DC + FC + 2], fp32)
        we = sb("we", [ED + 1, DH], fp32)
        flag_sum = sb("flag_sum", [P, 2], fp32)
        carry = sb("carry", [P, 1], fp32)
        den = sb("den", [P, 2, H], fp32)
        ln_a = sb("ln_a", [P, 2, 6], fp32)
        ln_b = sb("ln_b", [P, 2, 6], fp32)
        mom_a = sb("mom_a", [P, 2, 2], fp32)
        mom_b = sb("mom_b", [P, 2, 2], fp32)
        var_a = sb("var_a", [P, 2], fp32)
        var_b = sb("var_b", [P, 2], fp32)
        inv_a = sb("inv_a", [P, 2], fp32)
        inv_b = sb("inv_b", [P, 2], fp32)
        g1, b1v, g2, b2v = (cols[:, i * DC:(i + 1) * DC] for i in range(4))
        bias1 = cols[:, 4 * DC:4 * DC + FC]
        alpha = cols[:, 4 * DC + FC:4 * DC + FC + 1]
        beta = cols[:, 4 * DC + FC + 1:4 * DC + FC + 2]

        ps = ctx.enter_context(nc.psum_tensor("ps", [P, 4096], fp32))

        def bank(i, n=512, off=0):
            return ps[:, i * 512 + off:i * 512 + off + n]

        k_table = nc.dram_tensor("k_table", (NTILES * P, D), fp32).ap()
        v_table = nc.dram_tensor("v_table", (NTILES * P, D), fp32).ap()


        HALF = COLS // 2
        cut = [2 * (PAIRS * i // 5) for i in range(6)]

        def hot_ps(g):
            return bank(4, 256).bitcast(bf16).rearrange("p (a b) -> p a b", b=P)

        def ep_ps(g):
            return bank(5 + 2 * (g % 2), ITEM_GROUP * DH)

        def flag_ps(i):
            return bank(6, 64, P + i * 64).bitcast(bf16)

        s_const = sem("consts_made")
        s_credit = sem("credits_given")
        s_held = sem("waits_carried")
        s_load = sem("params_loaded")
        s_last = sem("last_dst_loaded")
        s_x = [sem(f"x_loaded{i}") for i in range(5)]
        s_w = sem("finish_weights_loaded")
        gates = [sem(f"gate{i}") for i in range(4)]
        s_step = sem("vector_step")
        s_ended = sem("ended_ready")
        s_ends_ps = sem("ends_summed")
        s_past = sem("past_ready")
        s_item_ps = sem("items_placed")
        s_tidx = sem("tile_index_ready")
        s_rows = [sem(f"tile_rows_gathered{i}") for i in range(5)]
        s_derived = sem("derived_rows_ready")
        s_rows_T = sem("rows_transposed")
        s_item = sem("item_columns_ready")
        s_bn = sem("tile_stats_ready")
        s_mom = sem("tile_moments_ready")
        s_moms = sem("moments_kept")
        s_vare = sem("variances_ready")
        s_rstd = sem("rstd_ready")
        s_shift = sem("shift_ready")
        s_xn = sem("xn_ready")
        s_xT_ps = sem("xn_transposed")
        s_xT = sem("xnT_ready")
        s_q_ps = sem("q_projected")
        s_kv_ps = sem("kv_projected")
        s_q32 = sem("q_biased")
        s_q1 = sem("q_part1_ready")
        s_rest1 = sem("q_rest_ready")
        s_q2 = sem("q_part2_ready")
        s_q3 = sem("q_part3_ready")
        s_kv = sem("kv_biased")
        s_kv_out = [sem(f"kv_stored{i}") for i in range(2)]
        s_idx = sem("index_ready")
        s_in = [sem(f"rows_gathered{g}") for g in range(GROUPS)]
        s_ef = [sem(f"edge_features_loaded{g}") for g in range(GROUPS)]
        s_efone = sem("ones_row_ready")
        s_hot = sem("onehot_ready")
        s_hot_T = sem("onehot_transposed")
        s_hotT = sem("onehotT_ready")
        s_q_e = sem("q_of_edges_ready")
        s_ep = sem("edge_projection_ready")
        s_added = sem("edge_projection_added")
        s_prod = sem("q_times_k_ready")
        s_raw = sem("scores_raw")
        s_scaled = sem("scores_scaled")
        s_masked = sem("scores_masked")
        s_wide = sem("flags_widened")
        s_flags_T = sem("flags_transposed")
        s_flags = sem("flags_stored")
        s_scores_T = sem("scores_transposed")
        s_scores = sem("scores_stored")
        s_fsum = sem("flags_summed")
        s_scan = sem("chunks_scanned")
        s_edge = sem("chunk_ends_in_a_row")
        s_rows_c = sem("carry_row_ready")
        s_carry = sem("carry_column_ready")
        s_sub = sem("maximum_subtracted")
        s_exp = sem("exponentials_ready")
        s_zero = sem("sums_zeroed")
        s_slice = sem("slice_copied")
        s_slice_T = sem("slice_transposed")
        s_ex = sem("softmax_terms_ready")
        s_hot32 = sem("onehot32_ready")
        s_wv = sem("v_weighed")
        s_wex = sem("terms_beside_v")
        s_y = sem("item_summed")
        s_acc = sem("item_added")
        f_bias = sem("bias_rows_loaded")
        f_rows = sem("bias_rows_scaled")
        f_x = sem("finish_x_loaded")
        f_den0 = sem("denominators_guarded")
        f_den = sem("denominators_inverted")
        f_att = sem("attention_normalised")
        f_attT_ps = sem("attention_transposed")
        f_attT = sem("attentionT_ready")
        f_wo = sem("attention_projected")
        f_x1a = sem("x1_without_bias")
        f_x1 = sem("x1_ready")
        f_bn1 = sem("x1_stats")
        f_mom1 = sem("x1_moments")
        f_var1 = sem("x1_variance")
        f_inv1 = sem("x1_rstd")
        f_half = sem("x_plus_x1")
        f_both = sem("residuals_ready")
        f_xn2 = sem("xn2_ready")
        f_xn2T_ps = sem("xn2_transposed")
        f_xn2T = sem("xn2T_ready")
        f_h = sem("hidden_ready")
        f_gelu = sem("gelu_ready")
        f_ff = sem("mlp_ready")
        f_y = sem("y_ready")
        f_bn2 = sem("y_stats")
        f_mom2 = sem("y_moments")
        f_var2 = sem("y_variance")
        f_inv2 = sem("y_rstd")
        f_out = sem("out_ready")
        f_store = sem("out_stored")

        credit = {s_q32: 1, s_kv: 1, s_rest1: 2, s_ep: 4, s_added: 2, s_hotT: 2, s_prod: 2, s_q_e: 4,
                  s_hot_T: 4, s_scores_T: 1, s_scores: 2, s_flags_T: 1, s_flags: 1, s_slice_T: 1, s_ex: 1,
                  s_y: 16, s_acc: 4, f_attT_ps: 2, f_attT: 4, f_x1a: 2, f_xn2T: 4, f_xn2T_ps: 2,
                  f_gelu: 2, f_y: 2, f_half: 1}

        def need(eng, semaphore, count):
            eng.wait_ge(semaphore, count + credit.get(semaphore, 0))

        def hold(eng, *needs):
            for semaphore, count in needs:
                need(eng, semaphore, count)
            eng.sem_inc(s_held, 1)

        def gate(eng, i):
            eng.drain().then_inc(gates[i], 1)
            eng.wait_ge(gates[i], 5)

        def load16(engine, row, s, top):
            return nc.values_load_multi_w_load_instructions(
                row[0:1, ds(s * CHUNKS, CHUNKS)], engines=(engine,), min_val=0, max_val=top)[1]

        def tile_of(view, n):
            return view[:, ds(n, 1), :].rearrange("p t d -> p (t d)")

        def part_of(n, part):
            return q3[:, ds(n, 1), part, :].rearrange("p t d -> p (t d)")

        def items_of(g):
            return slice(g * ITEM_GROUP, (g + 1) * ITEM_GROUP)

        block = ctx.enter_context(nc.Block())

        @block.sync
        def _(sp):
            for semaphore, count in credit.items():
                sp.sem_inc(semaphore, count)
            sp.sem_inc(s_credit, 1)

            def load(dst, src):
                sp.dma_start(dst, src).then_inc(s_load, 16)

            sp.dma_start(last_i[:, :], A["dst_last"]).then_inc(s_last, 16)
            xv = A["x"].rearrange("(t p) d -> p t d", p=P)
            for i in range(5):
                sp.dma_start(x_all[:, cut[i]:cut[i + 1], :], xv[:, cut[i]:cut[i + 1], :]).then_inc(s_x[i], 16)
            load(w_qkv[:, :, 0:D], A["Wq"].rearrange("(c p) n -> p c n", p=P))
            load(w_qkv[:, :, D:2 * D], A["Wk"].rearrange("(c p) n -> p c n", p=P))
            load(w_qkv[:, :, 2 * D:3 * D], A["Wv"].rearrange("(c p) n -> p c n", p=P))
            load(b_qkv[:, :], A["b_qkv"].partition_broadcast(P))
            load(cols[:, 0:4 * DC + FC], A["cols"])
            load(alpha, A["alpha"].partition_broadcast(P))
            load(beta, A["beta"].partition_broadcast(P))
            load(we[:, :], A["We_be"])

            kv_k = k_table.rearrange("(t p) d -> t p d", p=P)
            kv_v = v_table.rearrange("(t p) d -> t p d", p=P)
            with sp.Fori(0, PAIRS) as it:
                for u in range(2):
                    hold(sp, (s_kv, 2 * it + u + 1))
                    sp.dma_start(kv_k[ds(2 * it + u, 1), :, :].rearrange("t p d -> (t p) d"),
                                 kv[:, u, 0:D]).then_inc(s_kv_out[u], 16)
                    sp.dma_start(kv_v[ds(2 * it + u, 1), :, :].rearrange("t p d -> (t p) d"),
                                 kv[:, u, D:2 * D]).then_inc(s_kv_out[u], 16)
            for u in range(2):
                sp.wait_ge(s_kv_out[u], 32 * PAIRS)
            gate(sp, 0)

            sp.dma_start(w_o[:, :, :], A["Wo"].rearrange("(c p) n -> p c n", p=P)).then_inc(s_w, 16)
            sp.dma_start(w_1[:, :, :], A["W1"].rearrange("(c p) n -> p c n", p=P)).then_inc(s_w, 16)
            sp.dma_start(w_2[:, :, :], A["W2"].rearrange("(c p) n -> p c n", p=P)).then_inc(s_w, 16)
            with sp.Fori(0, STEPS) as s:
                first = load16(ENG.SP, tile_row, s, (TCH * P - 1) * P)
                for g in range(GROUPS):
                    hold(sp, (s_ep, s * GROUPS + g - 3))
                    for j in range(g * ITEM_GROUP, (g + 1) * ITEM_GROUP):
                        sp.dma_start(efT[0:ED, j, :], A["efT"][:, ds(first[j], P)]).then_inc(s_ef[g], 16)
            gate(sp, 1)
            gate(sp, 2)
            gate(sp, 3)

            sp.dma_start(bo_row[:, :], A["bo"].partition_broadcast(P)).then_inc(f_bias, 16)
            sp.dma_start(b2_row[:, :], A["b2"].partition_broadcast(P)).then_inc(f_bias, 16)
            xt = A["x"].rearrange("(t p) d -> p t d", p=P)
            ot = A["out"].rearrange("(t p) d -> p t d", p=P)
            sp.dma_start(x_in[:, :, :], xt[:, 0:2, :]).then_inc(f_x, 16)
            with sp.Fori(0, PAIRS - 1) as it:
                hold(sp, (f_both, it + 1))
                sp.dma_start(x_in[:, :, :], xt[:, ds(2 * it + 2, 2), :]).then_inc(f_x, 16)
                hold(sp, (f_out, 2 * it + 2))
                sp.dma_start(ot[:, ds(2 * it, 2), :], y_out[:, :, :]).then_inc(f_store, 16)
            sp.wait_ge(f_out, 2 * PAIRS)
            sp.dma_start(ot[:, NTILES - 2:NTILES, :], y_out[:, :, :]).then_inc(f_store, 16)
            sp.wait_ge(f_store, 16 * PAIRS)

        @block.gpsimd
        def _(pool):
            loose = dict(allow_small_or_imprecise_dtypes=True)
            pool.memset(ones[:, :], 1.0).then_inc(s_const, 1)
            pool.memset(ident[:, :], 0.0).then_inc(s_const, 1)
            pool.iota(iota[:, :], [[1, P]], base=0, channel_multiplier=0, **loose).then_inc(s_const, 1)
            pool.iota(iotab[:, :], [[1, P]], base=0, channel_multiplier=0, **loose).then_inc(s_const, 1)
            pool.iota(thr[:, :], [[P, NEDGE]], base=P, channel_multiplier=0, **loose).then_inc(s_const, 1)
            pool.iota(bcol[:, :], [[0, 1]], base=0, channel_multiplier=1, **loose).then_inc(s_const, 1)
            pool.memset(icol[:, COLS:WIDE], 0.0).then_inc(s_const, 1)
            pool.iota(icol[:, 0:COLS], [[1, STEPS], [STEPS, CHUNKS]], base=0, channel_multiplier=0,
                      **loose).then_inc(s_const, 1)
            pool.memset(halfneg[:, :], -0.5).then_inc(s_const, 1)
            pool.wait_ge(s_const, 9)
            pool.affine_select(out=ident[:, :], in_=ident[:, :], compare_op=ALU.not_equal, fill=1.0,
                               base=0, pattern=[[-1, P]], channel_multiplier=1).then_inc(s_const, 1)
            pool.wait_ge(s_const, 10)
            pool.tensor_copy(identb[:, :], ident[:, :]).then_inc(s_const, 1)

            pool.wait_ge(s_tidx, 1)
            for n, (rows, table) in enumerate(((g_dst, "dst_rows"), (g_prev, "prev_rows"),
                                               (g_next, "next_rows"), (g_src, "src_rows"),
                                               (g_w, "w_rows"))):
                for m in range(CCH):
                    pool.indirect_dma_start(
                        out=rows[:, m, :], out_offset=None, in_=A[table],
                        in_offset=bass.IndirectOffsetOnAxis(ap=tile_index[:, m:m + 1], axis=0))\
                        .then_inc(s_rows[n], 16)

            pool.wait_ge(s_vare, 1)
            pool.tensor_tensor(rstd[:, :], vare[:, :], halfneg[:, :], ALU.pow).then_inc(s_rstd, 1)
            with pool.Fori(0, PAIRS) as it:
                for u in range(2):
                    n = 2 * it + u
                    hold(pool, (s_q1, n + 1))
                    pool.tensor_tensor(qrest[:, u, :], q32[:, u, :], part_of(n, 0), ALU.subtract)\
                        .then_inc(s_rest1, 1)
                    hold(pool, (s_q2, n + 1))
                    pool.tensor_tensor(part_of(n, 2), qrest[:, u, :], part_of(n, 1), ALU.subtract)\
                        .then_inc(s_q3, 1)
            gate(pool, 0)

            def gathers(table, done):
                with pool.Fori(0, STEPS) as s:
                    for g in range(GROUPS):
                        hold(pool, (s_idx, s * GROUPS + done * (STEPS + 1) * GROUPS + g + 1))
                        for j in range(g * ITEM_GROUP, (g + 1) * ITEM_GROUP):
                            pool.indirect_dma_start(
                                out=kt[:, j, 0:D], out_offset=None, in_=table,
                                in_offset=bass.IndirectOffsetOnAxis(ap=index[:, j:j + 1], axis=0))\
                                .then_inc(s_in[g], 16)

            gathers(k_table, 0)
            gate(pool, 1)
            pool.memset(sums[:, 0:KEEP, :], 0.0).then_inc(s_zero, 1)
            gate(pool, 2)
            pool.memset(sums[:, KEEP:NTILES, :], 0.0).then_inc(s_zero, 1)
            gathers(v_table, 1)
            gate(pool, 3)

            def root1(p):
                hold(pool, (f_var1, p + 1))
                pool.tensor_tensor(inv_a[:, :], var_a[:, :], halfneg[:, 0:2], ALU.pow).then_inc(f_inv1, 1)

            def residuals(p):
                hold(pool, (f_y, 2 * p))
                pool.tensor_tensor(both[:, :, :], x1[:, :, :], x_in[:, :, :], ALU.add).then_inc(f_half, 1)
                hold(pool, (f_half, p + 1))
                pool.tensor_tensor(both[:, :, :], both[:, :, :],
                                   b2_b.unsqueeze(1).to_broadcast([P, 2, D]), ALU.add).then_inc(f_both, 1)

            def root2(p):
                hold(pool, (f_var2, p + 1))
                pool.tensor_tensor(inv_b[:, :], var_b[:, :], halfneg[:, 0:2], ALU.pow).then_inc(f_inv2, 1)

            pool.wait_ge(f_rows, 2)
            root1(0)
            residuals(0)
            with pool.Fori(0, PAIRS - 1) as it:
                root1(it + 1)
                root2(it)
                residuals(it + 1)
            root2(PAIRS - 1)

        @block.scalar
        def _(act):
            def mv(out, in_, **kw):
                return nc.scalar.activation(out, in_, ACT.Copy, **kw)

            act.wait_ge(s_credit, 1)
            act.wait_ge(s_shift, 1)
            act.wait_ge(s_load, 16 * 8)

            def normalise(n, u):
                hold(act, (s_xT_ps, n - 1))
                nc.scalar.activation(xn[:, u, :], tile_of(x_all, n), ACT.Identity,
                                     scale=rstd[:, ds(n, 1)], bias=shift[:, ds(n, 1)]).then_inc(s_xn, 1)

            def place_xT(n, u, first=False):
                if first:
                    act.wait_ge(s_xT_ps, n + 1)
                else:
                    hold(act, (s_kv_ps, n - 1), (s_xT_ps, n + 1))
                for c in range(DC):
                    nc.scalar.activation(xnT[:, u, c, :], bank(u, P, c * P), ACT.Identity,
                                         scale=g1[:, c:c + 1], bias=b1v[:, c:c + 1]).then_inc(s_xT, 1)

            def parts(n, u):
                hold(act, (s_q32, n + 1))
                mv(part_of(n, 0), q32[:, u, :]).then_inc(s_q1, 1)
                hold(act, (s_rest1, n + 1))
                mv(part_of(n, 1), qrest[:, u, :]).then_inc(s_q2, 1)

            for n in range(2):
                nc.scalar.activation(xn[:, n, :], x_all[:, n, :], ACT.Identity, scale=rstd[:, n:n + 1],
                                     bias=shift[:, n:n + 1]).then_inc(s_xn, 1)
            place_xT(0, 0, True)
            place_xT(1, 1, True)
            with act.Fori(0, PAIRS - 1) as it:
                for u in range(2):
                    normalise(2 * it + 2 + u, u)
                    parts(2 * it + u, u)
                    place_xT(2 * it + 2 + u, u)
            for u in range(2):
                parts(NTILES - 2 + u, u)
            gate(act, 0)

            def store_scores(s):
                hold(act, (s_scores_T, s + 1))
                mv(line[:, ds(s * P, P)], bank(6, P)).then_inc(s_scores, 1)

            def score_step(s, first=False):
                hold(act, (s_flags_T, s))
                for wide, item in ((fwide, f_item), (gwide, g_item)):
                    mv(wide[:, :, :], item[:, ds(s * CHUNKS, CHUNKS)].unsqueeze(2)
                       .to_broadcast([P, CHUNKS, H])).then_inc(s_wide, 1)
                for g in range(GROUPS):
                    n = s * GROUPS + g
                    hold(act, (s_q_e, n - 3), (s_hot_T, n + 1))
                    mv(hotT[:, items_of(g), :], hot_ps(g)).then_inc(s_hotT, 1)
                    if g == 0:
                        hold(act, (s_flags_T, s + 1))
                        mv(fline[:, ds(s * P, P)], flag_ps(0)).then_inc(s_flags, 1)
                        mv(gline[:, ds(s * P, P)], flag_ps(1)).then_inc(s_flags, 1)
                    if g == 1 and not first:
                        store_scores(s - 1)

            score_step(0, True)
            with act.Fori(1, STEPS) as s:
                score_step(s)
            store_scores(STEPS - 1)
            gate(act, 1)

            nc.scalar.activation(junk, fline, ACT.Copy, accum_out=flag_sum[:, 0:1]).then_inc(s_fsum, 1)
            act.wait_ge(s_fsum, 1)
            nc.scalar.activation(junk, gline, ACT.Copy, accum_out=flag_sum[:, 1:2]).then_inc(s_fsum, 1)
            for i in range(4):
                a, b = LINE * i // 4, LINE * (i + 1) // 4
                act.wait_ge(s_sub, i + 1)
                nc.scalar.activation(line[:, a:b], line[:, a:b], ACT.Exp).then_inc(s_exp, 1)
            gate(act, 2)

            with act.Fori(0, STEPS) as s:
                hold(act, (s_slice_T, s))
                mv(exslice[:, :], line[:, ds(s * P, P)]).then_inc(s_slice, 1)
                hold(act, (s_slice_T, s + 1))
                mv(ex_all[:, ds(s * P, P)], bank(6, P)).then_inc(s_ex, 1)
            gate(act, 3)

            def place_att(p):
                for u in range(2):
                    hold(act, (f_attT_ps, 2 * p + u + 1))
                    for c in range(DC):
                        mv(attT[:, c, u * P:(u + 1) * P], bank(u, P, c * P)).then_inc(f_attT, 1)

            def place_xn2(p):
                for u in range(2):
                    hold(act, (f_xn2T_ps, 2 * p + u + 1))
                    for c in range(DC):
                        nc.scalar.activation(xn2T[:, c, u * P:(u + 1) * P], bank(u, P, 256 + c * P),
                                             ACT.Identity, scale=g2[:, c:c + 1], bias=b2v[:, c:c + 1])\
                            .then_inc(f_xn2T, 1)

            def hidden(p):
                for f in range(FC):
                    hold(act, (f_h, p * FC + f + 1))
                    nc.scalar.activation(gelu[:, f, :], bank(4 + f % 2, 2 * P), ACT.Gelu,
                                         bias=bias1[:, f:f + 1]).then_inc(f_gelu, 1)

            place_att(0)
            place_xn2(0)
            with act.Fori(0, PAIRS - 1) as it:
                place_att(it + 1)
                hidden(it)
                place_xn2(it + 1)
            hidden(PAIRS - 1)

        @block.tensor
        def _(pe):
            mm = nc.tensor.matmul
            tr = nc.tensor.transpose
            pe.wait_ge(s_const, 11)
            pe.wait_ge(s_ended, TCH)
            for c in range(TCH):
                last = mm(bank(6)[0:NEDGE, 0:1], ended[:, c, :], ones[:, 0:1], start=(c == 0), stop=(c == TCH - 1))
            last.then_inc(s_ends_ps, 1)
            pe.wait_ge(s_past, 1)
            for m in range(CCH):
                mm(bank(6, 1, m), past[0:NEDGE, m * P:(m + 1) * P], ones[0:NEDGE, 0:1], start=True, stop=True)
                mm(bank(6, 1, 64 + m), icol[0:1, m * P:(m + 1) * P], ones[0:1, 0:1], start=True, stop=True)
            mm(bank(7)[0:1, 0:HALF], ones[0:NEDGE, 0:1], past[0:NEDGE, 0:HALF], start=True, stop=True)
            mm(bank(5)[0:1, 0:COLS - HALF], ones[0:NEDGE, 0:1], past[0:NEDGE, HALF:COLS], start=True, stop=True)\
                .then_inc(s_item_ps, 1)

            def transpose_x(n, u, first=False):
                if not first:
                    need(pe, s_xT, (n - 1) * DC)
                need(pe, s_xn, n + 1)
                for c in range(DC):
                    last = tr(bank(u, P, c * P), xn[:, u, c * P:(c + 1) * P], ident[:, :])
                last.then_inc(s_xT_ps, 1)

            def project(n, u):
                need(pe, s_xT, n * DC + DC)
                need(pe, s_q32, n - 1) if not (isinstance(n, int) and n < 2) else None
                for c in range(DC):
                    last = mm(bank(2 + u, D), xnT[:, u, c, :], w_qkv[:, c, 0:D],
                              start=(c == 0), stop=(c == DC - 1))
                last.then_inc(s_q_ps, 1)
                need(pe, s_kv, n - 1) if not (isinstance(n, int) and n < 2) else None
                for c in range(DC):
                    last = mm(bank(4 + u), xnT[:, u, c, :], w_qkv[:, c, D:3 * D],
                              start=(c == 0), stop=(c == DC - 1))
                last.then_inc(s_kv_ps, 1)

            pe.wait_ge(s_load, 16 * 8)
            transpose_x(0, 0, True)
            transpose_x(1, 1, True)
            pe.wait_ge(s_tidx, 1)
            project(0, 0)
            with pe.Fori(0, PAIRS - 1) as it:
                transpose_x(2 * it + 2, 0)
                project(2 * it + 1, 1)
                transpose_x(2 * it + 3, 1)
                project(2 * it + 2, 0)
            project(NTILES - 1, 1)
            for n, rows in enumerate((rel_f, f_f, g_f, src_f, g_w, off_f)):
                pe.wait_ge(s_derived, n + 1)
                if n:
                    pe.wait_ge(s_item, n)
                for m in range(CCH):
                    last = tr(ps[:, 6 * 512 + m * P:6 * 512 + (m + 1) * P], rows[:, m, :], ident[:, :])
                last.then_inc(s_rows_T, 1)
            gate(pe, 0)

            def transpose_scores(s, flags_stored):
                need(pe, s_flags, flags_stored)
                need(pe, s_masked, s + 1)
                tr(bank(6, P), masked.rearrange("p a b -> p (a b)"), ident[:, :]).then_inc(s_scores_T, 1)

            def score_step(s, first=False):
                blocks = load16(ENG.PE, block_row, s, BLOCKS - 1)
                for g in range(GROUPS):
                    n = s * GROUPS + g
                    need(pe, s_added, n - 1)
                    need(pe, s_ef[g], (s + 1) * 16 * ITEM_GROUP)
                    for i in range(ITEM_GROUP):
                        last = mm(ep_ps(g)[:, i * DH:(i + 1) * DH], efT[0:ED + 1, g * ITEM_GROUP + i, :],
                                  we[:, :], start=True, stop=True)
                    last.then_inc(s_ep, 1)
                    need(pe, s_hotT, n)
                    need(pe, s_hot, n + 1)
                    for i in range(ITEM_GROUP):
                        last = tr(hot_ps(g)[:, i, :], hot[:, g * ITEM_GROUP + i, :], identb[:, :])
                    last.then_inc(s_hot_T, 1)
                    if g == 0:
                        need(pe, s_scores, s - 1)
                        need(pe, s_wide, 2 * s + 2)
                        tr(flag_ps(0), fwide.rearrange("p a b -> p (a b)"), identb[:, :])
                        tr(flag_ps(1), gwide.rearrange("p a b -> p (a b)"), identb[:, :])\
                            .then_inc(s_flags_T, 1)
                    need(pe, s_prod, n - 1)
                    need(pe, s_hotT, n + 1)
                    for i in range(ITEM_GROUP):
                        j = g * ITEM_GROUP + i
                        for part in range(3):
                            last = mm(ps[:, (g % 2) * 1024 + i * D:(g % 2) * 1024 + (i + 1) * D],
                                      hotT[:, j, :], part_of(blocks[j], part), start=(part == 0), stop=(part == 2))
                    last.then_inc(s_q_e, 1)
                    if g == 1 and not first:
                        transpose_scores(s - 1, 2 * s + 2)

            pe.wait_ge(s_efone, 1)
            score_step(0, True)
            with pe.Fori(1, STEPS) as s:
                score_step(s)
            transpose_scores(STEPS - 1, 2 * STEPS)
            gate(pe, 1)

            for back in range(2):
                pe.wait_ge(s_scan, back + 1)
                pe.wait_ge(s_fsum, 2)
                at_end = reach[:, LINE - 1:LINE] if not back else reach[:, 0:1]
                mm(bank(0)[0:1, 0:P], at_end, ident[:, :], start=True, stop=True)
                mm(bank(0)[0:1, P:2 * P], flag_sum[:, back:back + 1], ident[:, :], start=True, stop=True)\
                    .then_inc(s_edge, 1)
                pe.wait_ge(s_rows_c, back + 1)
                row = carry_row[0:1, 0:P] if not back else carry_row[0:1, H:H + P]
                mm(bank(1, 1), row, ones[0:1, 0:1], start=True, stop=True).then_inc(s_carry, 1)
            gate(pe, 2)

            def transpose_slice(s):
                need(pe, s_ex, s)
                need(pe, s_slice, s + 1)
                tr(bank(6, P), exslice[:, :], ident[:, :]).then_inc(s_slice_T, 1)

            def sum_step(s, ahead=True):
                for g in range(GROUPS):
                    n = s * GROUPS + g
                    need(pe, s_hot32, n + 1)
                    need(pe, s_wv, n + 1)
                    need(pe, s_wex, n + 1)
                    for j in range(g * ITEM_GROUP, (g + 1) * ITEM_GROUP):
                        need(pe, s_acc, s * CHUNKS + j - 3)
                        mm(bank(j % 4, ROW), hot32[:, j, :], kt[:, j, :], start=True, stop=True)\
                            .then_inc(s_y, 1)
                    if g == 1 and ahead:
                        transpose_slice(s + 1)

            transpose_slice(0)
            with pe.Fori(0, STEPS - 1) as s:
                sum_step(s)
            sum_step(STEPS - 1, False)
            gate(pe, 3)

            def attention(p):
                for u in range(2):
                    need(pe, f_attT, p * 2 * DC + u * DC - DC)
                    need(pe, f_xn2T, p * 2 * DC + u * DC - DC)
                    need(pe, f_att, 2 * p + u + 1)
                    for c in range(DC):
                        last = tr(bank(u, P, c * P), att[:, u, c * P:(c + 1) * P], ident[:, :])
                    last.then_inc(f_attT_ps, 1)
                for u in range(2):
                    need(pe, f_x1a, 2 * p + u - 1)
                    need(pe, f_attT, p * 2 * DC + u * DC + DC)
                    for c in range(DC):
                        last = mm(bank(2 + u, D), attT[:, c, u * P:(u + 1) * P], w_o[:, c, :],
                                  start=(c == 0), stop=(c == DC - 1))
                    last.then_inc(f_wo, 1)

            def transpose_xn2(p):
                for u in range(2):
                    need(pe, f_xn2T, p * 2 * DC + u * DC - DC)
                    need(pe, f_xn2, 2 * p + u + 1)
                    for c in range(DC):
                        last = tr(bank(u, P, 256 + c * P), xn2[:, u, c * P:(c + 1) * P], ident[:, :])
                    last.then_inc(f_xn2T_ps, 1)

            def hidden(p):
                need(pe, f_xn2T, (p + 1) * 2 * DC)
                for f in range(FC):
                    need(pe, f_gelu, p * FC + f - 1)
                    for c in range(DC):
                        last = mm(bank(4 + f % 2, 2 * P), w_1[:, c, f * P:(f + 1) * P], xn2T[:, c, :],
                                  start=(c == 0), stop=(c == DC - 1))
                    last.then_inc(f_h, 1)

            def mlp(p):
                need(pe, f_gelu, (p + 1) * FC)
                for u in range(2):
                    need(pe, f_y, 2 * p + u - 1)
                    for f in range(FC):
                        last = mm(bank(6 + u, D), gelu[:, f, u * P:(u + 1) * P], w_2[:, f, :],
                                  start=(f == 0), stop=(f == FC - 1))
                    last.then_inc(f_ff, 1)

            pe.wait_ge(s_w, 48)
            attention(0)
            transpose_xn2(0)
            with pe.Fori(0, PAIRS - 1) as it:
                attention(it + 1)
                hidden(it)
                transpose_xn2(it + 1)
                mlp(it)
            hidden(PAIRS - 1)
            mlp(PAIRS - 1)

        @block.vector
        def _(dve):
            v = nc.vector
            steps = [0]

            def step(ins):
                steps[0] += 1
                ins.then_inc(s_step, 1)
                dve.wait_ge(s_step, steps[0])

            dve.wait_ge(s_last, 16)
            dve.wait_ge(s_const, 11)
            step(v.tensor_copy(last_f[:, :], last_i[:, :]))
            for c in range(TCH):
                v.tensor_scalar(ended[:, c, :], thr[:, :], last_f[:, c:c + 1], None, ALU.is_gt)\
                    .then_inc(s_ended, 1)
            dve.wait_ge(s_ends_ps, 1)
            step(v.tensor_tensor(ends[0:NEDGE, :], bank(6)[0:NEDGE, 0:1], bcol[0:NEDGE, :], ALU.add))
            v.tensor_scalar(past[0:NEDGE, :], icol[0:NEDGE, :], ends[0:NEDGE, 0:1], None, ALU.is_gt)\
                .then_inc(s_past, 1)
            dve.wait_ge(s_item_ps, 1)
            step(v.tensor_copy(b7[:, :], bank(6, CCH)))
            step(v.tensor_scalar(b128[:, :], b7[:, :], float(P), None, ALU.mult))
            step(v.tensor_tensor(t7[:, :], bank(6, CCH, 64), b7[:, :], ALU.subtract))
            step(v.tensor_copy(tile_index[:, :], t7[:, :]))
            for a, b, source in ((0, HALF, bank(7)), (HALF, COLS, bank(5))):
                step(v.tensor_copy(block_row[0:1, a:b], source[0:1, 0:b - a]))
                step(v.tensor_tensor(tile_rowf[0:1, a:b], icol[0:1, a:b], source[0:1, 0:b - a], ALU.subtract))
            step(v.tensor_scalar(tile_row[0:1, 0:COLS], tile_rowf[0:1, :], float(P), None, ALU.mult))
            v.tensor_copy(t7[:, 0:1], b7[:, 0:1]).then_inc(s_tidx, 1)

            for i in range(5):
                dve.wait_ge(s_x[i], 16)
                with dve.Fori(cut[i] // 2, cut[i + 1] // 2) as p:
                    for u in range(2):
                        v.bn_stats(ln_a[:, u, :], tile_of(x_all, 2 * p + u)).then_inc(s_bn, 1)
                    hold(dve, (s_bn, 2 * p + 2))
                    for u in range(2):
                        v.bn_aggr(mom_a[:, u, :], ln_a[:, u, :]).then_inc(s_mom, 1)
                    need(dve, s_mom, 2 * p + 2)
                    v.tensor_copy(moments[:, ds(2 * p, 2), :], mom_a[:, :, :]).then_inc(s_moms, 1)
            dve.wait_ge(s_moms, PAIRS)
            v.tensor_scalar(vare[:, :], moments[:, :, 1], EPS, None, ALU.add).then_inc(s_vare, 1)
            dve.wait_ge(s_rstd, 1)
            v.scalar_tensor_tensor(shift[:, :], moments[:, :, 0], -1.0, rstd[:, :], ALU.mult, ALU.mult)\
                .then_inc(s_shift, 1)

            for n in range(5):
                dve.wait_ge(s_rows[n], 16 * CCH)
            step(v.tensor_tensor(f_f, g_prev, g_dst, ALU.not_equal))
            step(v.tensor_tensor(g_f, g_next, g_dst, ALU.not_equal))
            step(v.tensor_tensor(rel_f, g_dst, b128[:, :].unsqueeze(2).to_broadcast([P, CCH, P]),
                                 ALU.subtract))
            step(v.tensor_scalar(off_f, rel_f, 0.0, None, ALU.is_ge))
            step(v.scalar_tensor_tensor(valid, rel_f, float(P), off_f, ALU.is_lt, ALU.mult))
            step(v.scalar_tensor_tensor(f_f, f_f, -BIG, valid, ALU.mult, ALU.mult))
            step(v.scalar_tensor_tensor(g_f, g_f, -BIG, valid, ALU.mult, ALU.mult))
            step(v.tensor_copy(src_f, g_src))
            step(v.scalar_tensor_tensor(g_w, g_w, float(DH) ** -0.5, valid, ALU.mult, ALU.mult))
            step(v.tensor_scalar(off_f, valid, BIG, -BIG, ALU.mult, ALU.add))
            v.tensor_copy(t7[:, 0:1], b7[:, 0:1]).then_inc(s_derived, 6)

            def biased(n, u, it=None):
                need(dve, s_rest1, n - 1)
                need(dve, s_q_ps, n + 1)
                v.tensor_tensor(q32[:, u, :], bank(2 + u, D), b_qkv[:, 0:D], ALU.add).then_inc(s_q32, 1)
                if it is not None:
                    dve.wait_ge(s_kv_out[u], it * 32)
                need(dve, s_kv_ps, n + 1)
                v.tensor_tensor(kv[:, u, :], bank(4 + u), b_qkv[:, D:3 * D], ALU.add).then_inc(s_kv, 1)

            dve.wait_ge(s_load, 16 * 8)
            biased(0, 0)
            biased(1, 1)
            with dve.Fori(1, PAIRS) as it:
                for u in range(2):
                    biased(2 * it + u, u, it)
            for n, column in enumerate((rel_item, f_item, g_item, src_item, ews_item, off_item)):
                dve.wait_ge(s_rows_T, n + 1)
                v.tensor_copy(column[:, :], ps[:, 6 * 512:6 * 512 + WIDE]).then_inc(s_item, 1)
            dve.wait_ge(s_item, 6)
            gate(dve, 0)

            def indices(s, g):
                v.tensor_copy(index[:, items_of(g)], src_item[:, ds(s * CHUNKS + g * ITEM_GROUP, ITEM_GROUP)])\
                    .then_inc(s_idx, 1)

            def onehots(s, g):
                need(dve, s_hot_T, s * GROUPS + g - 3)
                for j in range(g * ITEM_GROUP, (g + 1) * ITEM_GROUP):
                    last = v.tensor_scalar(hot[:, j, :], iotab[:, :], rel_item[:, ds(s * CHUNKS + j, 1)],
                                           None, ALU.is_equal)
                last.then_inc(s_hot, 1)

            v.memset(efT[ED:ED + 1, :, :], 1.0).then_inc(s_efone, 1)
            for g in range(GROUPS):
                indices(0, g)
            onehots(0, 0)
            with dve.Fori(0, STEPS) as s:
                for g in range(GROUPS):
                    n = s * GROUPS + g
                    onehots(s + (g + 1) // GROUPS, (g + 1) % GROUPS)
                    rows = kt[:, items_of(g), 0:D]
                    heads = rows.rearrange("p a (h d) -> p a h d", h=H)
                    dve.wait_ge(s_in[g], (s + 1) * 16 * ITEM_GROUP)
                    need(dve, s_ep, n + 1)
                    v.tensor_tensor(heads, heads,
                                    ep_ps(g).rearrange("p (a d) -> p a d", d=DH)
                                    .unsqueeze(2).to_broadcast([P, ITEM_GROUP, H, DH]), ALU.add)\
                        .then_inc(s_added, 1)
                    need(dve, s_added, n + 1)
                    need(dve, s_q_e, n + 1)
                    v.tensor_tensor(rows, rows, ps[:, (g % 2) * 1024:(g % 2 + 1) * 1024]
                                    .rearrange("p (a d) -> p a d", d=D), ALU.mult).then_inc(s_prod, 1)
                    need(dve, s_prod, n + 1)
                    v.tensor_reduce(raw[:, items_of(g), :], heads, AX.X, ALU.add).then_inc(s_raw, 1)
                    need(dve, s_raw, n + 1)
                    indices(s + 1, g)
                step_cols = ds(s * CHUNKS, CHUNKS)
                need(dve, s_raw, (s + 1) * GROUPS)
                v.tensor_tensor(scaled[:, :, :], raw[:, :, :], ews_item[:, step_cols].unsqueeze(2)
                                .to_broadcast([P, CHUNKS, H]), ALU.mult).then_inc(s_scaled, 1)
                need(dve, s_scaled, s + 1)
                need(dve, s_scores_T, s)
                v.tensor_tensor(masked[:, :, :], scaled[:, :, :], off_item[:, step_cols].unsqueeze(2)
                                .to_broadcast([P, CHUNKS, H]), ALU.add).then_inc(s_masked, 1)
            gate(dve, 1)

            def backwards(view, back):
                return view[:, ::-1] if back else view

            def scan(out, flags, values, start):
                return v.tensor_tensor_scan(out, flags, values, start, ALU.add, ALU.max)

            for back in range(2):
                flags = backwards((fline, gline)[back], back)
                out = backwards(reach, back)
                scan(out, flags, backwards((line, reach)[back], back), -BIG).then_inc(s_scan, 1)
                dve.wait_ge(s_scan, back + 1)
                dve.wait_ge(s_edge, back + 1)
                step(v.tensor_copy(edge_row[0:1, :, :], bank(0)[0:1, 0:2 * P].rearrange("p (a b) -> p a b", a=2)))
                step(v.memset(carry_row[0:1, :], -BIG))
                for h in range(H):
                    ends_h = edge_row[0:1, 0, h:P:H]
                    sums_h = edge_row[0:1, 1, h:P:H]
                    out_h = carry_row[0:1, h:P:H] if back else carry_row[0:1, H + h:H + P:H]
                    last = scan(backwards(out_h, back), backwards(sums_h, back), backwards(ends_h, back), -BIG)
                last.then_inc(s_rows_c, 1)
                dve.wait_ge(s_carry, back + 1)
                step(v.tensor_copy(carry[:, :], bank(1, 1)))
                step(scan(out, flags, out, carry[:, 0:1]))
            for i in range(4):
                a, b = LINE * i // 4, LINE * (i + 1) // 4
                v.tensor_tensor(line[:, a:b], line[:, a:b], reach[:, a:b], ALU.subtract).then_inc(s_sub, 1)
            gate(dve, 2)

            for g in range(GROUPS):
                indices(0, g)
            dve.wait_ge(s_zero, 2)
            with dve.Fori(0, STEPS) as s:
                blocks = load16(ENG.DVE, block_row, s, BLOCKS - 1)

                def weigh(g):
                    n = s * GROUPS + g
                    need(dve, s_y, s * CHUNKS + g * ITEM_GROUP - 12)
                    for j in range(g * ITEM_GROUP, (g + 1) * ITEM_GROUP):
                        last = v.tensor_scalar(hot32[:, j, :], iota[:, :], rel_item[:, ds(s * CHUNKS + j, 1)],
                                               None, ALU.is_equal)
                    last.then_inc(s_hot32, 1)
                    ex = ex_all[:, ds(s * P + g * ITEM_GROUP * H, ITEM_GROUP * H)]
                    ex = ex.rearrange("p (a h) -> p a h", h=H)
                    heads = kt[:, items_of(g), 0:D].rearrange("p a (h d) -> p a h d", h=H)
                    dve.wait_ge(s_in[g], (s + STEPS + 1) * 16 * ITEM_GROUP)
                    need(dve, s_ex, s + 1)
                    v.tensor_tensor(heads, heads, ex.unsqueeze(3).to_broadcast([P, ITEM_GROUP, H, DH]),
                                    ALU.mult).then_inc(s_wv, 1)
                    v.tensor_copy(kt[:, items_of(g), D:ROW], ex).then_inc(s_wex, 1)

                def add_up(g):
                    for j in range(g * ITEM_GROUP, (g + 1) * ITEM_GROUP):
                        m = s * CHUNKS + j
                        need(dve, s_y, m + 1)
                        need(dve, s_acc, m)
                        v.tensor_tensor(tile_of(sums, blocks[j]), tile_of(sums, blocks[j]),
                                        bank(j % 4, ROW), ALU.add).then_inc(s_acc, 1)
                    indices(s + 1, g)

                weigh(0)
                for g in range(1, GROUPS):
                    weigh(g)
                    add_up(g - 1)
                add_up(GROUPS - 1)
            need(dve, s_acc, COLS)
            gate(dve, 3)

            dve.wait_ge(f_bias, 32)
            v.tensor_scalar(bo_a, bo_row, alpha, None, ALU.mult).then_inc(f_rows, 1)
            v.tensor_scalar(b2_b, b2_row, beta, None, ALU.mult).then_inc(f_rows, 1)
            dve.wait_ge(f_rows, 2)

            def attention(p):
                need(dve, f_attT_ps, 2 * p)
                v.tensor_scalar(den[:, :, :], sums[:, ds(2 * p, 2), D:ROW], 0.5, None, ALU.max)\
                    .then_inc(f_den0, 1)
                need(dve, f_den0, p + 1)
                v.reciprocal(den[:, :, :], den[:, :, :]).then_inc(f_den, 1)
                need(dve, f_den, p + 1)
                for u in range(2):
                    v.tensor_tensor(att[:, u, :].rearrange("p (h d) -> p h d", h=H),
                                    sums[:, ds(2 * p + u, 1), 0:D].rearrange("p t (h d) -> p (t h) d", h=H),
                                    den[:, u, :].unsqueeze(2).to_broadcast([P, H, DH]), ALU.mult)\
                        .then_inc(f_att, 1)

            def normalised(values, p, side, out, done):
                stat, mom, var, inv, bn, moms, vars_, invs = side
                for u in range(2):
                    v.bn_stats(stat[:, u, :], values[:, u, :]).then_inc(bn, 1)
                hold(dve, (bn, 2 * p + 2))
                for u in range(2):
                    v.bn_aggr(mom[:, u, :], stat[:, u, :]).then_inc(moms, 1)
                need(dve, moms, 2 * p + 2)
                v.tensor_scalar(var[:, :], mom[:, :, 1], EPS, None, ALU.add).then_inc(vars_, 1)
                need(dve, invs, p + 1)
                for u in range(2):
                    v.tensor_scalar(out[:, u, :], values[:, u, :], mom[:, u, 0:1], inv[:, u:u + 1],
                                    ALU.subtract, ALU.mult).then_inc(done, 1)

            side_a = (ln_a, mom_a, var_a, inv_a, f_bn1, f_mom1, f_var1, f_inv1)
            side_b = (ln_b, mom_b, var_b, inv_b, f_bn2, f_mom2, f_var2, f_inv2)

            def residual(p):
                need(dve, f_half, p)
                dve.wait_ge(f_x, (p + 1) * 16)
                for u in range(2):
                    need(dve, f_wo, 2 * p + u + 1)
                    v.scalar_tensor_tensor(x1[:, u, :], bank(2 + u, D), alpha, x_in[:, u, :],
                                           ALU.mult, ALU.add).then_inc(f_x1a, 1)
                for u in range(2):
                    need(dve, f_x1a, 2 * p + u + 1)
                    v.tensor_tensor(x1[:, u, :], x1[:, u, :], bo_a, ALU.add).then_inc(f_x1, 1)
                need(dve, f_x1, 2 * p + 2)
                need(dve, f_xn2T_ps, 2 * p)
                normalised(x1, p, side_a, xn2, f_xn2)

            def result(p, first=False):
                need(dve, f_both, p + 1)
                if not first:
                    need(dve, f_out, 2 * p)
                for u in range(2):
                    need(dve, f_ff, 2 * p + u + 1)
                    v.scalar_tensor_tensor(y_sum[:, u, :], bank(6 + u, D), beta, both[:, u, :],
                                           ALU.mult, ALU.add).then_inc(f_y, 1)
                need(dve, f_y, 2 * p + 2)
                if not first:
                    dve.wait_ge(f_store, p * 16)
                normalised(y_sum, p, side_b, y_out, f_out)

            attention(0)
            residual(0)
            attention(1)
            residual(1)
            result(0, True)
            with dve.Fori(1, PAIRS - 1) as it:
                attention(it + 1)
                residual(it + 1)
                result(it)
            result(PAIRS - 1)


_OUT = "out"


def kernel(**inputs):
    import concourse.bacc as bacc
    from concourse.bass_utils import run_bass_kernel_spmd

    a = {k.removeprefix("L0_gnn_"): np.asarray(v) for k, v in inputs.items()}
    n_nodes, D = a["x"].shape
    n_edges = a["src"].shape[0]
    ED, DH = a["We"].shape
    FF = a["W1"].shape[1]
    Z = sizes(n_nodes, n_edges)
    rows, tiles = 2 * Z["pairs"] * P, Z["tile_chunks"] * P

    x = np.zeros((rows, D), a["x"].dtype)
    x[:n_nodes] = a["x"]
    beyond = Z["blocks"] * P
    dst = np.full(tiles * P + 2, beyond, np.int32)
    dst[0] = -1
    dst[1:n_edges + 1] = a["dst"]
    src = np.zeros(tiles * P, np.int32)
    src[:n_edges] = a["src"]
    ew = np.zeros(tiles * P, a["edge_weight"].dtype)
    ew[:n_edges] = a["edge_weight"]
    ef = np.zeros((ED, tiles * P), a["edge_attr_64"].dtype)
    ef[:, :n_edges] = a["edge_attr_64"].T

    def columns(v):
        return v.reshape(-1, P).T

    arrays = {
        "x": x, "dst_rows": dst[1:-1].reshape(tiles, P), "prev_rows": dst[:-2].reshape(tiles, P),
        "next_rows": dst[2:].reshape(tiles, P), "src_rows": src.reshape(tiles, P),
        "w_rows": ew.reshape(tiles, P), "dst_last": columns(dst[1:-1].reshape(tiles, P)[:, P - 1]),
        "efT": ef, "Wq": a["Wq"], "Wk": a["Wk"], "Wv": a["Wv"],
        "b_qkv": np.concatenate([a["bq"], a["bk"], a["bv"]]),
        "cols": np.concatenate([columns(a[k]) for k in ("ln1_g", "ln1_b", "ln2_g", "ln2_b", "b1")], axis=1),
        "alpha": a["alpha"], "beta": a["beta"], "We_be": np.concatenate([a["We"], a["be"][None]]),
        "Wo": a["Wo"], "W1": a["W1"], "W2": a["W2"], "bo": a["bo"], "b2": a["b2"],
    }
    nc = bacc.Bacc("TRN2", target_bir_lowering=False, num_devices=1)
    A, ins = {}, {}
    for name, v in arrays.items():
        v = np.ascontiguousarray(v)
        ins["in_" + name] = v
        A[name] = nc.dram_tensor("in_" + name, v.shape, mybir.dt.from_np(v.dtype), kind="ExternalInput").ap()
    A["out"] = nc.dram_tensor("out", (rows, D), mybir.dt.float32, kind="ExternalOutput").ap()
    graph_layer(nc, A, n_nodes, n_edges, (D, D // DH, ED, FF))
    r = run_bass_kernel_spmd(nc, [ins], core_ids=[0])
    return r.results[0]["out"][:n_nodes]
```

```python
from contextlib import ExitStack

import concourse.bass as bass
from concourse import mybir
import numpy as np

P = 128
ITEM_GROUP = 4
CHUNKS = 16
GROUPS = CHUNKS // ITEM_GROUP
BIG = 1.0e30
EPS = 1.0e-5


def ceil_div(a, b):
    return -(-a // b)


def sizes(n_nodes, n_edges):
    blocks = ceil_div(n_nodes, P)
    tiles = ceil_div(n_edges, P)
    items = tiles + blocks - 1
    steps = 4 * ceil_div(items, 4 * CHUNKS)
    return dict(blocks=blocks, tiles=tiles, items=items, steps=steps, pairs=ceil_div(blocks, 2),
                tile_chunks=ceil_div(max(tiles, steps * CHUNKS) + 1, P),
                col_chunks=ceil_div((steps + 1) * CHUNKS, P))


def graph_layer(nc, A, n_nodes, n_edges, dims):
    D, H, ED, FF = dims
    DH = D // H
    DC = D // P
    FC = FF // P
    ROW = D + H
    Z = sizes(n_nodes, n_edges)
    BLOCKS, STEPS, PAIRS = Z["blocks"], Z["steps"], Z["pairs"]
    TCH, CCH = Z["tile_chunks"], Z["col_chunks"]
    COLS = STEPS * CHUNKS
    WIDE = CCH * P
    NTILES = 2 * PAIRS
    LINE = STEPS * P
    NEDGE = BLOCKS - 1
    fp32, bf16, i32 = mybir.dt.float32, mybir.dt.bfloat16, mybir.dt.int32
    ALU, ACT, AX = mybir.AluOpType, mybir.ActivationFunctionType, mybir.AxisListType
    ENG = mybir.EngineType
    ds = bass.ds

    ctx = ExitStack()
    with ctx:
        def sb(name, shape, dt):
            return ctx.enter_context(nc.sbuf_tensor("sb_" + name, shape, dt))

        def sem(name):
            return ctx.enter_context(nc.semaphore(name))

        def carve(region, at, shape, dt):
            n = int(np.prod(shape)) * (2 if dt == bf16 else 4)
            v = region[:, at // 4:(at + n) // 4]
            if dt != fp32:
                v = v.bitcast(dt)
            if len(shape) == 2:
                v = v.rearrange("p (a b) -> p a b", a=shape[0])
            if len(shape) == 3:
                v = v.rearrange("p (a b c) -> p a b c", a=shape[0], b=shape[1])
            return v, at + n

        r_q = sb("r_q", [P, max(NTILES * 3 * D // 2, NTILES * ROW)], fp32)
        r_line = sb("r_line", [P, max(NTILES * D, 2 * LINE)], fp32)
        r_item = sb("r_item", [P, 5 * WIDE], fp32)
        r_kt = sb("r_kt", [P, max(5 * WIDE, CHUNKS * ROW)], fp32)
        r_w = sb("r_w", [P, DC * D + DC * FF + FC * D], fp32)
        r_tmp = sb("r_tmp", [P, max(4608, COLS, LINE // 2 + 4 * P)], fp32)

        q3, _ = carve(r_q, 0, (NTILES, 3, D), bf16)
        sums, _ = carve(r_q, 0, (NTILES, ROW), fp32)
        QB = NTILES * 3 * D * 2
        reach = r_q[:, NTILES * ROW - LINE:NTILES * ROW]
        KEEP = (NTILES * ROW - LINE) // ROW
        x_all, _ = carve(r_line, 0, (NTILES, D), fp32)
        line = r_line[:, 0:LINE]
        fline = r_line[:, LINE:LINE + LINE // 2].bitcast(bf16)
        gline = r_line[:, LINE + LINE // 2:2 * LINE].bitcast(bf16)
        ex_all = r_line[:, LINE:2 * LINE]
        src_item, at = carve(r_item, 0, (WIDE,), i32)
        rel_item, at = carve(r_item, at, (WIDE,), fp32)
        ews_item, at = carve(r_item, at, (WIDE,), fp32)
        off_item, at = carve(r_item, at, (WIDE,), fp32)
        f_item, at = carve(r_item, at, (WIDE,), bf16)
        g_item, at = carve(r_item, at, (WIDE,), bf16)
        kt, _ = carve(r_kt, 0, (CHUNKS, ROW), fp32)
        g_dst, at = carve(r_kt, 0, (CCH, P), i32)
        rel_f, _ = carve(r_kt, 0, (CCH, P), fp32)
        g_prev, at1 = carve(r_kt, at, (CCH, P), i32)
        f_f, _ = carve(r_kt, at, (CCH, P), fp32)
        g_next, at2 = carve(r_kt, at1, (CCH, P), i32)
        g_f, _ = carve(r_kt, at1, (CCH, P), fp32)
        g_src, at3 = carve(r_kt, at2, (CCH, P), i32)
        src_f, _ = carve(r_kt, at2, (CCH, P), fp32)
        g_w, at4 = carve(r_kt, at3, (CCH, P), fp32)
        tail = QB - 4 * (2 * WIDE + TCH * NEDGE)
        assert tail > 0
        icol, at = carve(r_q, tail, (WIDE,), fp32)
        past, at = carve(r_q, at, (WIDE,), fp32)
        valid, _ = carve(r_item, 8 * WIDE, (CCH, P), fp32)
        off_f, _ = carve(r_item, 12 * WIDE, (CCH, P), fp32)
        ended, at = carve(r_q, at, (TCH, NEDGE), fp32)
        w_qkv, at = carve(r_w, 0, (DC, 3 * D), fp32)
        b_qkv, at = carve(r_w, at, (3 * D,), fp32)
        w_o, at = carve(r_w, 0, (DC, D), fp32)
        w_1, at = carve(r_w, at, (DC, FF), fp32)
        w_2, at = carve(r_w, at, (FC, D), fp32)
        xn, at = carve(r_tmp, 0, (2, D), fp32)
        xnT, at = carve(r_tmp, at, (2, DC, P), fp32)
        q32, at = carve(r_tmp, at, (2, D), fp32)
        qrest, at = carve(r_tmp, at, (2, D), fp32)
        kv, at = carve(r_tmp, at, (2, 2 * D), fp32)
        moments, at = carve(r_tmp, at, (NTILES, 2), fp32)
        rstd, at = carve(r_tmp, at, (NTILES,), fp32)
        shift, at = carve(r_tmp, at, (NTILES,), fp32)
        vare, at = carve(r_tmp, at, (NTILES,), fp32)
        efT, at = carve(r_tmp, 0, (CHUNKS, P), fp32)
        hot, at = carve(r_tmp, at, (CHUNKS, P), bf16)
        hotT, at = carve(r_tmp, at, (CHUNKS, P), bf16)
        raw, at = carve(r_tmp, at, (CHUNKS, H), fp32)
        scaled, at = carve(r_tmp, at, (CHUNKS, H), fp32)
        masked, at = carve(r_tmp, at, (CHUNKS, H), fp32)
        fwide, at = carve(r_tmp, at, (CHUNKS, H), bf16)
        gwide, at = carve(r_tmp, at, (CHUNKS, H), bf16)
        hot32, at = carve(r_tmp, 0, (CHUNKS, P), fp32)
        junk, at = carve(r_tmp, 0, (LINE,), bf16)
        edge_row, at = carve(r_tmp, at, (2, P), fp32)
        carry_row, at = carve(r_tmp, at, (P + 2 * H,), fp32)
        exslice, _ = carve(r_tmp, 0, (2, P), fp32)
        tile_rowf, _ = carve(r_tmp, 0, (COLS,), fp32)
        att, at = carve(r_kt, 0, (2, D), fp32)
        attT, at = carve(r_kt, at, (DC, 2 * P), fp32)
        x_in, at = carve(r_kt, at, (2, D), fp32)
        x1, at = carve(r_kt, at, (2, D), fp32)
        xn2, at = carve(r_kt, at, (2, D), fp32)
        xn2T, at = carve(r_kt, at, (DC, 2 * P), fp32)
        both_a, at = carve(r_kt, at, (2, D), fp32)
        gelu, at = carve(r_tmp, 0, (FC, 2 * P), fp32)
        y_sum, at = carve(r_tmp, at, (2, D), fp32)
        both_b, at = carve(r_tmp, at, (2, D), fp32)
        both = (both_a, both_b)
        y_out, at = carve(r_tmp, at, (2, D), fp32)
        bo_row, at = carve(r_tmp, at, (D,), fp32)
        b2_row, at = carve(r_tmp, at, (D,), fp32)
        bo_a, at = carve(r_tmp, at, (D,), fp32)
        b2_b, at = carve(r_tmp, at, (D,), fp32)

        ident = sb("ident", [P, P], fp32)
        identb = sb("identb", [P, P], bf16)
        iota = sb("iota", [P, P], fp32)
        iotab = sb("iotab", [P, P], bf16)
        ones = sb("ones", [P, 1], fp32)
        index = sb("index", [P, CHUNKS], i32)
        tile_index = sb("tile_index", [P, CCH], i32)
        b7 = sb("b7", [P, CCH], fp32)
        b128 = sb("b128", [P, CCH], fp32)
        t7 = sb("t7", [P, CCH], fp32)
        last_i = sb("last_i", [P, TCH], i32)
        last_f = sb("last_f", [P, TCH], fp32)
        thr = sb("thr", [P, NEDGE], fp32)
        ends = sb("ends", [P, 1], fp32)
        bcol = sb("bcol", [P, 1], fp32)
        block_row = sb("block_row", [1, COLS + CHUNKS], i32)
        tile_row = sb("tile_row", [1, COLS + CHUNKS], i32)
        halfneg = sb("halfneg", [P, NTILES], fp32)
        cols = sb("cols", [P, 4 * DC + FC + 2], fp32)
        we = sb("we", [ED + 1, DH], fp32)
        flag_sum = sb("flag_sum", [P, 2], fp32)
        carry = sb("carry", [P, 1], fp32)
        den = sb("den", [P, 2, H], fp32)
        ln_a = sb("ln_a", [P, 2, 6], fp32)
        ln_b = sb("ln_b", [P, 2, 6], fp32)
        mom_a = sb("mom_a", [P, 2, 2], fp32)
        mom_b = sb("mom_b", [P, 2, 2], fp32)
        var_a = sb("var_a", [P, 2], fp32)
        var_b = sb("var_b", [P, 2], fp32)
        inv_a = sb("inv_a", [P, 2], fp32)
        inv_b = sb("inv_b", [P, 2], fp32)
        g1, b1v, g2, b2v = (cols[:, i * DC:(i + 1) * DC] for i in range(4))
        bias1 = cols[:, 4 * DC:4 * DC + FC]
        alpha = cols[:, 4 * DC + FC:4 * DC + FC + 1]
        beta = cols[:, 4 * DC + FC + 1:4 * DC + FC + 2]

        ps = ctx.enter_context(nc.psum_tensor("ps", [P, 4096], fp32))

        def bank(i, n=512, off=0):
            return ps[:, i * 512 + off:i * 512 + off + n]

        k_table = nc.dram_tensor("k_table", (NTILES * P, D), fp32).ap()
        v_table = nc.dram_tensor("v_table", (NTILES * P, D), fp32).ap()


        HALF = COLS // 2
        cut = [2 * (PAIRS * i // 5) for i in range(6)]

        def hot_ps(g):
            return bank(4, 256).bitcast(bf16).rearrange("p (a b) -> p a b", b=P)

        def ep_ps(g):
            return bank(5 + 2 * (g % 2), ITEM_GROUP * DH)

        def flag_ps(i):
            return bank(6, 64, P + i * 64).bitcast(bf16)

        s_const = sem("consts_made")
        s_credit = sem("credits_given")
        s_held = sem("waits_carried")
        s_load = sem("params_loaded")
        s_last = sem("last_dst_loaded")
        s_x = [sem(f"x_loaded{i}") for i in range(5)]
        s_w = sem("finish_weights_loaded")
        gates = [sem(f"gate{i}") for i in range(4)]
        s_step = sem("vector_step")
        s_ended = sem("ended_ready")
        s_ends_ps = sem("ends_summed")
        s_past = sem("past_ready")
        s_item_ps = sem("items_placed")
        s_tidx = sem("tile_index_ready")
        s_rows = [sem(f"tile_rows_gathered{i}") for i in range(5)]
        s_derived = sem("derived_rows_ready")
        s_rows_T = sem("rows_transposed")
        s_item = sem("item_columns_ready")
        s_bn = sem("tile_stats_ready")
        s_mom = sem("tile_moments_ready")
        s_moms = sem("moments_kept")
        s_vare = sem("variances_ready")
        s_rstd = sem("rstd_ready")
        s_shift = sem("shift_ready")
        s_xn = sem("xn_ready")
        s_xT_ps = sem("xn_transposed")
        s_xT = sem("xnT_ready")
        s_q_ps = sem("q_projected")
        s_kv_ps = sem("kv_projected")
        s_q32 = sem("q_biased")
        s_q1 = sem("q_part1_ready")
        s_rest1 = sem("q_rest_ready")
        s_q2 = sem("q_part2_ready")
        s_q3 = sem("q_part3_ready")
        s_kv = sem("kv_biased")
        s_kv_out = [sem(f"kv_stored{i}") for i in range(2)]
        s_idx = sem("index_ready")
        s_in = [sem(f"rows_gathered{g}") for g in range(GROUPS)]
        s_ef = [sem(f"edge_features_loaded{g}") for g in range(GROUPS)]
        s_efone = sem("ones_row_ready")
        s_hot = sem("onehot_ready")
        s_hot_T = sem("onehot_transposed")
        s_hotT = sem("onehotT_ready")
        s_q_e = sem("q_of_edges_ready")
        s_ep = sem("edge_projection_ready")
        s_added = sem("edge_projection_added")
        s_prod = sem("q_times_k_ready")
        s_raw = sem("scores_raw")
        s_scaled = sem("scores_scaled")
        s_masked = sem("scores_masked")
        s_wide = sem("flags_widened")
        s_flags_T = sem("flags_transposed")
        s_flags = sem("flags_stored")
        s_scores_T = sem("scores_transposed")
        s_scores = sem("scores_stored")
        s_fsum = sem("flags_summed")
        s_scan = sem("chunks_scanned")
        s_edge = sem("chunk_ends_in_a_row")
        s_rows_c = sem("carry_row_ready")
        s_carry = sem("carry_column_ready")
        s_sub = sem("maximum_subtracted")
        s_exp = sem("exponentials_ready")
        s_zero = sem("sums_zeroed")
        s_slice = sem("slice_copied")
        s_slice_T = sem("slice_transposed")
        s_ex = sem("softmax_terms_ready")
        s_hot32 = sem("onehot32_ready")
        s_wv = sem("v_weighed")
        s_wex = sem("terms_beside_v")
        s_y = sem("item_summed")
        s_acc = sem("item_added")
        f_bias = sem("bias_rows_loaded")
        f_rows = sem("bias_rows_scaled")
        f_x = sem("finish_x_loaded")
        f_den0 = sem("denominators_guarded")
        f_den = sem("denominators_inverted")
        f_att = sem("attention_normalised")
        f_attT_ps = sem("attention_transposed")
        f_attT = sem("attentionT_ready")
        f_wo = sem("attention_projected")
        f_x1a = sem("x1_without_bias")
        f_x1 = sem("x1_ready")
        f_bn1 = sem("x1_stats")
        f_mom1 = sem("x1_moments")
        f_var1 = sem("x1_variance")
        f_inv1 = sem("x1_rstd")
        f_half = sem("x_plus_x1")
        f_both = sem("residuals_ready")
        f_xn2 = sem("xn2_ready")
        f_xn2T_ps = sem("xn2_transposed")
        f_xn2T = sem("xn2T_ready")
        f_h = sem("hidden_ready")
        f_gelu = sem("gelu_ready")
        f_ff = sem("mlp_ready")
        f_y = sem("y_ready")
        f_bn2 = sem("y_stats")
        f_mom2 = sem("y_moments")
        f_var2 = sem("y_variance")
        f_inv2 = sem("y_rstd")
        f_out = sem("out_ready")
        f_store = sem("out_stored")

        credit = {s_q32: 1, s_kv: 1, s_rest1: 2, s_ep: 4, s_added: 2, s_hotT: 2, s_prod: 2, s_q_e: 4,
                  s_hot_T: 4, s_scores_T: 1, s_scores: 2, s_flags_T: 1, s_flags: 1, s_slice_T: 2, s_ex: 2,
                  s_y: 16, s_acc: 8, f_attT_ps: 1, f_attT: 1, f_x1a: 2, f_xn2T: 1, f_xn2T_ps: 1,
                  f_gelu: 2, f_y: 4, f_half: 1, f_wo: 1, f_h: 1}

        def need(eng, semaphore, count):
            eng.wait_ge(semaphore, count + credit.get(semaphore, 0))

        def hold(eng, *needs):
            for semaphore, count in needs:
                need(eng, semaphore, count)
            eng.sem_inc(s_held, 1)

        def gate(eng, i):
            eng.drain().then_inc(gates[i], 1)
            eng.wait_ge(gates[i], 5)

        def load_group(engine, row, s, g, top):
            return nc.values_load_multi_w_load_instructions(
                row[0:1, ds(s * CHUNKS + g * ITEM_GROUP, ITEM_GROUP)], engines=(engine,), min_val=0, max_val=top,
                skip_runtime_bounds_check_because="the prepare stage counts at most BLOCKS - 1 ends, and no "
                                                  "more ends than items, whatever the edges are")[1]

        def tile_of(view, n):
            return view[:, ds(n, 1), :].rearrange("p t d -> p (t d)")

        def part_of(n, part):
            return q3[:, ds(n, 1), part, :].rearrange("p t d -> p (t d)")

        def items_of(g):
            return slice(g * ITEM_GROUP, (g + 1) * ITEM_GROUP)

        block = ctx.enter_context(nc.Block())

        @block.sync
        def _(sp):
            for semaphore, count in credit.items():
                sp.sem_inc(semaphore, count)
            sp.sem_inc(s_credit, 1)

            def load(dst, src):
                sp.dma_start(dst, src).then_inc(s_load, 16)

            sp.dma_start(last_i[:, :], A["dst_last"]).then_inc(s_last, 16)
            xv = A["x"].rearrange("(t p) d -> p t d", p=P)
            for i in range(5):
                sp.dma_start(x_all[:, cut[i]:cut[i + 1], :], xv[:, cut[i]:cut[i + 1], :]).then_inc(s_x[i], 16)
            load(w_qkv[:, :, 0:D], A["Wq"].rearrange("(c p) n -> p c n", p=P))
            load(w_qkv[:, :, D:2 * D], A["Wk"].rearrange("(c p) n -> p c n", p=P))
            load(w_qkv[:, :, 2 * D:3 * D], A["Wv"].rearrange("(c p) n -> p c n", p=P))
            load(b_qkv[:, :], A["b_qkv"].partition_broadcast(P))
            load(cols[:, 0:4 * DC + FC], A["cols"])
            load(alpha, A["alpha"].partition_broadcast(P))
            load(beta, A["beta"].partition_broadcast(P))
            load(we[:, :], A["We_be"])

            kv_k = k_table.rearrange("(t p) d -> t p d", p=P)
            kv_v = v_table.rearrange("(t p) d -> t p d", p=P)
            with sp.Fori(0, PAIRS) as it:
                for u in range(2):
                    hold(sp, (s_kv, 2 * it + u + 1))
                    sp.dma_start(kv_k[ds(2 * it + u, 1), :, :].rearrange("t p d -> (t p) d"),
                                 kv[:, u, 0:D]).then_inc(s_kv_out[u], 16)
                    sp.dma_start(kv_v[ds(2 * it + u, 1), :, :].rearrange("t p d -> (t p) d"),
                                 kv[:, u, D:2 * D]).then_inc(s_kv_out[u], 16)
            for u in range(2):
                sp.wait_ge(s_kv_out[u], 32 * PAIRS)
            gate(sp, 0)

            sp.dma_start(w_o[:, :, :], A["Wo"].rearrange("(c p) n -> p c n", p=P)).then_inc(s_w, 16)
            sp.dma_start(w_1[:, :, :], A["W1"].rearrange("(c p) n -> p c n", p=P)).then_inc(s_w, 16)
            sp.dma_start(w_2[:, :, :], A["W2"].rearrange("(c p) n -> p c n", p=P)).then_inc(s_w, 16)
            with sp.Fori(0, STEPS) as s:
                for g in range(GROUPS):
                    first = load_group(ENG.SP, tile_row, s, g, (TCH * P - 1) * P)
                    hold(sp, (s_ep, s * GROUPS + g - 3))
                    for j in range(g * ITEM_GROUP, (g + 1) * ITEM_GROUP):
                        sp.dma_start(efT[0:ED, j, :], A["efT"][:, ds(first[j % ITEM_GROUP], P)]).then_inc(s_ef[g], 16)
            gate(sp, 1)
            gate(sp, 2)
            gate(sp, 3)

            sp.dma_start(bo_row[:, :], A["bo"].partition_broadcast(P)).then_inc(f_bias, 16)
            sp.dma_start(b2_row[:, :], A["b2"].partition_broadcast(P)).then_inc(f_bias, 16)
            xt = A["x"].rearrange("(t p) d -> p t d", p=P)
            ot = A["out"].rearrange("(t p) d -> p t d", p=P)
            sp.dma_start(x_in[:, :, :], xt[:, 0:2, :]).then_inc(f_x, 16)
            sp.wait_ge(f_both, 1)
            sp.dma_start(x_in[:, :, :], xt[:, 2:4, :]).then_inc(f_x, 16)
            with sp.Fori(0, PAIRS - 2) as it:
                hold(sp, (f_both, it + 2))
                sp.dma_start(x_in[:, :, :], xt[:, ds(2 * it + 4, 2), :]).then_inc(f_x, 16)
                hold(sp, (f_out, 2 * it + 2))
                sp.dma_start(ot[:, ds(2 * it, 2), :], y_out[:, :, :]).then_inc(f_store, 16)
            for p in range(PAIRS - 2, PAIRS):
                sp.wait_ge(f_out, 2 * p + 2)
                sp.dma_start(ot[:, 2 * p:2 * p + 2, :], y_out[:, :, :]).then_inc(f_store, 16)
            sp.wait_ge(f_store, 16 * PAIRS)

        @block.gpsimd
        def _(pool):
            loose = dict(allow_small_or_imprecise_dtypes=True)
            pool.memset(ones[:, :], 1.0).then_inc(s_const, 1)
            pool.memset(ident[:, :], 0.0).then_inc(s_const, 1)
            pool.iota(iota[:, :], [[1, P]], base=0, channel_multiplier=0, **loose).then_inc(s_const, 1)
            pool.iota(iotab[:, :], [[1, P]], base=0, channel_multiplier=0, **loose).then_inc(s_const, 1)
            pool.iota(thr[:, :], [[P, NEDGE]], base=P, channel_multiplier=0, **loose).then_inc(s_const, 1)
            pool.iota(bcol[:, :], [[0, 1]], base=0, channel_multiplier=1, **loose).then_inc(s_const, 1)
            pool.memset(icol[:, COLS:WIDE], 0.0).then_inc(s_const, 1)
            pool.iota(icol[:, 0:COLS], [[1, STEPS], [STEPS, CHUNKS]], base=0, channel_multiplier=0,
                      **loose).then_inc(s_const, 1)
            pool.memset(halfneg[:, :], -0.5).then_inc(s_const, 1)
            pool.wait_ge(s_const, 9)
            pool.affine_select(out=ident[:, :], in_=ident[:, :], compare_op=ALU.not_equal, fill=1.0,
                               base=0, pattern=[[-1, P]], channel_multiplier=1).then_inc(s_const, 1)
            pool.wait_ge(s_const, 10)
            pool.tensor_copy(identb[:, :], ident[:, :]).then_inc(s_const, 1)

            pool.wait_ge(s_tidx, 1)
            for n, (rows, table) in enumerate(((g_dst, "dst_rows"), (g_prev, "prev_rows"),
                                               (g_next, "next_rows"), (g_src, "src_rows"),
                                               (g_w, "w_rows"))):
                for m in range(CCH):
                    pool.indirect_dma_start(
                        out=rows[:, m, :], out_offset=None, in_=A[table],
                        in_offset=bass.IndirectOffsetOnAxis(ap=tile_index[:, m:m + 1], axis=0))\
                        .then_inc(s_rows[n], 16)

            pool.wait_ge(s_vare, 1)
            pool.tensor_tensor(rstd[:, :], vare[:, :], halfneg[:, :], ALU.pow).then_inc(s_rstd, 1)
            with pool.Fori(0, PAIRS) as it:
                for u in range(2):
                    n = 2 * it + u
                    hold(pool, (s_q1, n + 1))
                    pool.tensor_tensor(qrest[:, u, :], q32[:, u, :], part_of(n, 0), ALU.subtract)\
                        .then_inc(s_rest1, 1)
                    hold(pool, (s_q2, n + 1))
                    pool.tensor_tensor(part_of(n, 2), qrest[:, u, :], part_of(n, 1), ALU.subtract)\
                        .then_inc(s_q3, 1)
            gate(pool, 0)

            def gathers(table, s, before):
                for g in range(GROUPS):
                    hold(pool, (s_idx, s * GROUPS + before + g + 1))
                    for j in range(g * ITEM_GROUP, (g + 1) * ITEM_GROUP):
                        pool.indirect_dma_start(
                            out=kt[:, j, 0:D], out_offset=None, in_=table,
                            in_offset=bass.IndirectOffsetOnAxis(ap=index[:, j:j + 1], axis=0))\
                            .then_inc(s_in[g], 16)

            with pool.Fori(0, STEPS) as s:
                gathers(k_table, s, 0)
            gate(pool, 1)
            gathers(v_table, 0, (STEPS + 1) * GROUPS)
            pool.memset(sums[:, 0:KEEP, :], 0.0).then_inc(s_zero, 1)
            pool.wait_ge(s_sub, 2)
            pool.memset(sums[:, KEEP:NTILES, :], 0.0).then_inc(s_zero, 1)
            gate(pool, 2)
            with pool.Fori(1, STEPS) as s:
                gathers(v_table, s, (STEPS + 1) * GROUPS)
            gate(pool, 3)

            def root1(p):
                hold(pool, (f_var1, p + 1))
                pool.tensor_tensor(inv_a[:, :], var_a[:, :], halfneg[:, 0:2], ALU.pow).then_inc(f_inv1, 1)

            def residuals(p, odd):
                hold(pool, (f_y, 2 * p - 2))
                pool.tensor_tensor(both[odd][:, :, :], x1[:, :, :], x_in[:, :, :], ALU.add).then_inc(f_half, 1)
                hold(pool, (f_half, p + 1))
                pool.tensor_tensor(both[odd][:, :, :], both[odd][:, :, :],
                                   b2_b.unsqueeze(1).to_broadcast([P, 2, D]), ALU.add).then_inc(f_both, 1)

            def root2(p):
                hold(pool, (f_var2, p + 1))
                pool.tensor_tensor(inv_b[:, :], var_b[:, :], halfneg[:, 0:2], ALU.pow).then_inc(f_inv2, 1)

            def roots_of_pair(p, odd):
                root1(p + 1)
                root2(p - 1)
                residuals(p + 1, 1 - odd)

            pool.wait_ge(f_rows, 2)
            for p in range(2):
                root1(p)
                residuals(p, p)
            with pool.Fori(0, (PAIRS - 3) // 2) as two:
                roots_of_pair(2 * two + 1, 1)
                roots_of_pair(2 * two + 2, 0)
            for p in range(1 + (PAIRS - 3) // 2 * 2, PAIRS - 1):
                roots_of_pair(p, p % 2)
            root2(PAIRS - 2)
            root2(PAIRS - 1)

        @block.scalar
        def _(act):
            def mv(out, in_, **kw):
                return nc.scalar.activation(out, in_, ACT.Copy, **kw)

            act.wait_ge(s_credit, 1)
            act.wait_ge(s_shift, 1)
            act.wait_ge(s_load, 16 * 8)

            def normalise(n, u):
                hold(act, (s_xT_ps, n - 1))
                nc.scalar.activation(xn[:, u, :], tile_of(x_all, n), ACT.Identity,
                                     scale=rstd[:, ds(n, 1)], bias=shift[:, ds(n, 1)]).then_inc(s_xn, 1)

            def place_xT(n, u, first=False):
                if first:
                    act.wait_ge(s_xT_ps, n + 1)
                else:
                    hold(act, (s_kv_ps, n - 1), (s_xT_ps, n + 1))
                for c in range(DC):
                    nc.scalar.activation(xnT[:, u, c, :], bank(u, P, c * P), ACT.Identity,
                                         scale=g1[:, c:c + 1], bias=b1v[:, c:c + 1]).then_inc(s_xT, 1)

            def parts(n, u):
                hold(act, (s_q32, n + 1))
                mv(part_of(n, 0), q32[:, u, :]).then_inc(s_q1, 1)
                hold(act, (s_rest1, n + 1))
                mv(part_of(n, 1), qrest[:, u, :]).then_inc(s_q2, 1)

            for n in range(2):
                nc.scalar.activation(xn[:, n, :], x_all[:, n, :], ACT.Identity, scale=rstd[:, n:n + 1],
                                     bias=shift[:, n:n + 1]).then_inc(s_xn, 1)
            place_xT(0, 0, True)
            place_xT(1, 1, True)
            with act.Fori(0, PAIRS - 1) as it:
                for u in range(2):
                    normalise(2 * it + 2 + u, u)
                    parts(2 * it + u, u)
                    place_xT(2 * it + 2 + u, u)
            for u in range(2):
                parts(NTILES - 2 + u, u)
            gate(act, 0)

            def store_scores(s):
                hold(act, (s_scores_T, s + 1))
                mv(line[:, ds(s * P, P)], bank(6, P)).then_inc(s_scores, 1)

            def score_step(s, first=False):
                hold(act, (s_flags_T, s))
                for wide, item in ((fwide, f_item), (gwide, g_item)):
                    mv(wide[:, :, :], item[:, ds(s * CHUNKS, CHUNKS)].unsqueeze(2)
                       .to_broadcast([P, CHUNKS, H])).then_inc(s_wide, 1)
                for g in range(GROUPS):
                    n = s * GROUPS + g
                    hold(act, (s_q_e, n - 3), (s_hot_T, n + 1))
                    mv(hotT[:, items_of(g), :], hot_ps(g)).then_inc(s_hotT, 1)
                    if g == 0:
                        hold(act, (s_flags_T, s + 1))
                        mv(fline[:, ds(s * P, P)], flag_ps(0)).then_inc(s_flags, 1)
                        mv(gline[:, ds(s * P, P)], flag_ps(1)).then_inc(s_flags, 1)
                if not first:
                    store_scores(s - 1)

            score_step(0, True)
            with act.Fori(1, STEPS) as s:
                score_step(s)
            store_scores(STEPS - 1)
            gate(act, 1)

            nc.scalar.activation(junk, fline, ACT.Copy, accum_out=flag_sum[:, 0:1]).then_inc(s_fsum, 1)
            act.wait_ge(s_fsum, 1)
            nc.scalar.activation(junk, gline, ACT.Copy, accum_out=flag_sum[:, 1:2]).then_inc(s_fsum, 1)
            for half in range(2):
                act.wait_ge(s_sub, half + 1)
                with act.Fori(half * STEPS // 4, (half + 1) * STEPS // 4) as two:
                    for u in range(2):
                        hold(act, (s_slice_T, 2 * two + u - 1))
                        nc.scalar.activation(exslice[:, u, :], line[:, ds((2 * two + u) * P, P)], ACT.Exp)\
                            .then_inc(s_slice, 1)
            gate(act, 2)

            with act.Fori(0, STEPS) as s:
                for g in range(GROUPS):
                    hold(act, (s_y, s * CHUNKS + g * ITEM_GROUP - 12))
                    mv(kt[:, items_of(g), D:ROW], ex_all[:, ds(s * P + g * ITEM_GROUP * H, ITEM_GROUP * H)]
                       .rearrange("p (a h) -> p a h", h=H)).then_inc(s_wex, 1)
            gate(act, 3)

            with act.Fori(0, PAIRS) as p:
                for f in range(FC):
                    hold(act, (f_h, p * FC + f + 1))
                    nc.scalar.activation(gelu[:, f, :], bank(4 + f % 2, 2 * P), ACT.Gelu,
                                         bias=bias1[:, f:f + 1]).then_inc(f_gelu, 1)

        @block.tensor
        def _(pe):
            mm = nc.tensor.matmul
            tr = nc.tensor.transpose
            pe.wait_ge(s_const, 11)
            pe.wait_ge(s_ended, TCH)
            for c in range(TCH):
                last = mm(bank(6)[0:NEDGE, 0:1], ended[:, c, :], ones[:, 0:1], start=(c == 0), stop=(c == TCH - 1))
            last.then_inc(s_ends_ps, 1)
            pe.wait_ge(s_past, 1)
            for m in range(CCH):
                mm(bank(6, 1, m), past[0:NEDGE, m * P:(m + 1) * P], ones[0:NEDGE, 0:1], start=True, stop=True)
                mm(bank(6, 1, 64 + m), icol[0:1, m * P:(m + 1) * P], ones[0:1, 0:1], start=True, stop=True)
            mm(bank(7)[0:1, 0:HALF], ones[0:NEDGE, 0:1], past[0:NEDGE, 0:HALF], start=True, stop=True)
            mm(bank(5)[0:1, 0:COLS - HALF], ones[0:NEDGE, 0:1], past[0:NEDGE, HALF:COLS], start=True, stop=True)\
                .then_inc(s_item_ps, 1)

            def transpose_x(n, u, first=False):
                if not first:
                    need(pe, s_xT, (n - 1) * DC)
                need(pe, s_xn, n + 1)
                for c in range(DC):
                    last = tr(bank(u, P, c * P), xn[:, u, c * P:(c + 1) * P], ident[:, :])
                last.then_inc(s_xT_ps, 1)

            def project(n, u):
                need(pe, s_xT, n * DC + DC)
                need(pe, s_q32, n - 1) if not (isinstance(n, int) and n < 2) else None
                for c in range(DC):
                    last = mm(bank(2 + u, D), xnT[:, u, c, :], w_qkv[:, c, 0:D],
                              start=(c == 0), stop=(c == DC - 1))
                last.then_inc(s_q_ps, 1)
                need(pe, s_kv, n - 1) if not (isinstance(n, int) and n < 2) else None
                for c in range(DC):
                    last = mm(bank(4 + u), xnT[:, u, c, :], w_qkv[:, c, D:3 * D],
                              start=(c == 0), stop=(c == DC - 1))
                last.then_inc(s_kv_ps, 1)

            pe.wait_ge(s_load, 16 * 8)
            transpose_x(0, 0, True)
            transpose_x(1, 1, True)
            pe.wait_ge(s_tidx, 1)
            project(0, 0)
            with pe.Fori(0, PAIRS - 1) as it:
                transpose_x(2 * it + 2, 0)
                project(2 * it + 1, 1)
                transpose_x(2 * it + 3, 1)
                project(2 * it + 2, 0)
            project(NTILES - 1, 1)
            for n, rows in enumerate((rel_f, f_f, g_f, src_f, g_w, off_f)):
                pe.wait_ge(s_derived, n + 1)
                if n:
                    pe.wait_ge(s_item, n)
                for m in range(CCH):
                    last = tr(ps[:, 6 * 512 + m * P:6 * 512 + (m + 1) * P], rows[:, m, :], ident[:, :])
                last.then_inc(s_rows_T, 1)
            gate(pe, 0)

            def transpose_scores(s, flags_stored):
                need(pe, s_flags, flags_stored)
                need(pe, s_scores, s)
                need(pe, s_masked, s + 1)
                tr(bank(6, P), masked.rearrange("p a b -> p (a b)"), ident[:, :]).then_inc(s_scores_T, 1)

            def project_edges(n, g, step):
                need(pe, s_added, n - 1)
                need(pe, s_ef[g], (step + 1) * 16 * ITEM_GROUP)
                for i in range(ITEM_GROUP):
                    last = mm(ep_ps(g)[:, i * DH:(i + 1) * DH], efT[0:ED + 1, g * ITEM_GROUP + i, :],
                              we[:, :], start=True, stop=True)
                last.then_inc(s_ep, 1)

            def transpose_hot(n, g):
                need(pe, s_hotT, n)
                need(pe, s_hot, n + 1)
                for i in range(ITEM_GROUP):
                    last = tr(hot_ps(g)[:, i, :], hot[:, g * ITEM_GROUP + i, :], identb[:, :])
                last.then_inc(s_hot_T, 1)

            def score_step(s, first=False, final=False):
                for g in range(GROUPS):
                    n = s * GROUPS + g
                    blocks = load_group(ENG.PE, block_row, s, g, BLOCKS - 1)
                    if not (final and g == GROUPS - 1):
                        project_edges(n + 1, (g + 1) % GROUPS, s + (g + 1) // GROUPS)
                    if g == 0:
                        need(pe, s_scores, s - 1)
                        need(pe, s_wide, 2 * s + 2)
                        tr(flag_ps(0), fwide.rearrange("p a b -> p (a b)"), identb[:, :])
                        tr(flag_ps(1), gwide.rearrange("p a b -> p (a b)"), identb[:, :])\
                            .then_inc(s_flags_T, 1)
                    if not (final and g == GROUPS - 1):
                        transpose_hot(n + 1, (g + 1) % GROUPS)
                    if g == 2 and not first:
                        transpose_scores(s - 1, 2 * s + 2)
                    need(pe, s_prod, n - 1)
                    need(pe, s_hotT, n + 1)
                    for i in range(ITEM_GROUP):
                        j = g * ITEM_GROUP + i
                        for part in range(3):
                            last = mm(ps[:, (g % 2) * 1024 + i * D:(g % 2) * 1024 + (i + 1) * D],
                                      hotT[:, j, :], part_of(blocks[i], part), start=(part == 0), stop=(part == 2))
                    last.then_inc(s_q_e, 1)

            pe.wait_ge(s_efone, 1)
            project_edges(0, 0, 0)
            transpose_hot(0, 0)
            score_step(0, True)
            with pe.Fori(1, STEPS - 1) as s:
                score_step(s)
            score_step(STEPS - 1, final=True)
            transpose_scores(STEPS - 1, 2 * STEPS)
            gate(pe, 1)

            for back in range(2):
                pe.wait_ge(s_scan, back + 1)
                pe.wait_ge(s_fsum, 2)
                at_end = reach[:, LINE - 1:LINE] if not back else reach[:, 0:1]
                mm(bank(0)[0:1, 0:P], at_end, ident[:, :], start=True, stop=True)
                mm(bank(0)[0:1, P:2 * P], flag_sum[:, back:back + 1], ident[:, :], start=True, stop=True)\
                    .then_inc(s_edge, 1)
                pe.wait_ge(s_rows_c, back + 1)
                row = carry_row[0:1, 0:P] if not back else carry_row[0:1, H:H + P]
                mm(bank(1, 1), row, ones[0:1, 0:1], start=True, stop=True).then_inc(s_carry, 1)
            with pe.Fori(0, STEPS // 2) as two:
                for u in range(2):
                    need(pe, s_ex, 2 * two + u - 1)
                    need(pe, s_slice, 2 * two + u + 1)
                    tr(bank(6 + u, P), exslice[:, u, :], ident[:, :]).then_inc(s_slice_T, 1)
            gate(pe, 2)

            with pe.Fori(0, STEPS) as s:
                for g in range(GROUPS):
                    n = s * GROUPS + g
                    need(pe, s_hot32, n + 1)
                    need(pe, s_wex, n + 1)
                    need(pe, s_wv, n + 1)
                    for j in range(g * ITEM_GROUP, (g + 1) * ITEM_GROUP):
                        need(pe, s_acc, s * CHUNKS + j - 7)
                        mm(bank(j % 8, ROW), hot32[:, j, :], kt[:, j, :], start=True, stop=True)\
                            .then_inc(s_y, 1)
            gate(pe, 3)

            def transpose_att(p):
                need(pe, f_attT, p)
                need(pe, f_att, 2 * p + 2)
                for u in range(2):
                    for c in range(DC):
                        last = tr(bank(0, P, c * 2 * P + u * P), att[:, u, c * P:(c + 1) * P], ident[:, :])
                last.then_inc(f_attT_ps, 1)

            def project_att(p):
                for u in range(2):
                    need(pe, f_x1a, 2 * p + u - 1)
                    need(pe, f_attT, p + 1)
                    for c in range(DC):
                        last = mm(bank(2 + u, D), attT[:, c, u * P:(u + 1) * P], w_o[:, c, :],
                                  start=(c == 0), stop=(c == DC - 1))
                    last.then_inc(f_wo, 1)

            def transpose_xn2(p):
                need(pe, f_xn2T, p)
                need(pe, f_xn2, 2 * p + 2)
                for u in range(2):
                    for c in range(DC):
                        last = tr(bank(1, P, c * 2 * P + u * P), xn2[:, u, c * P:(c + 1) * P], ident[:, :])
                last.then_inc(f_xn2T_ps, 1)

            def hidden(p):
                need(pe, f_xn2T, p + 1)
                for f in range(FC):
                    need(pe, f_gelu, p * FC + f - 1)
                    for c in range(DC):
                        last = mm(bank(4 + f % 2, 2 * P), w_1[:, c, f * P:(f + 1) * P], xn2T[:, c, :],
                                  start=(c == 0), stop=(c == DC - 1))
                    last.then_inc(f_h, 1)

            def mlp(p):
                need(pe, f_gelu, (p + 1) * FC)
                for u in range(2):
                    need(pe, f_y, 2 * p + u - 1)
                    for f in range(FC):
                        last = mm(bank(6 + u, D), gelu[:, f, u * P:(u + 1) * P], w_2[:, f, :],
                                  start=(f == 0), stop=(f == FC - 1))
                    last.then_inc(f_ff, 1)

            def pair(p, ahead=2):
                if ahead >= 1:
                    project_att(p + 1)
                hidden(p)
                if ahead >= 1:
                    transpose_xn2(p + 1)
                if ahead >= 2:
                    transpose_att(p + 2)
                mlp(p)

            pe.wait_ge(s_w, 48)
            transpose_att(0)
            project_att(0)
            transpose_xn2(0)
            transpose_att(1)
            with pe.Fori(0, PAIRS - 2) as p:
                pair(p)
            pair(PAIRS - 2, 1)
            pair(PAIRS - 1, 0)

        @block.vector
        def _(dve):
            v = nc.vector
            steps = [0]

            def step(ins):
                steps[0] += 1
                ins.then_inc(s_step, 1)
                dve.wait_ge(s_step, steps[0])

            dve.wait_ge(s_last, 16)
            dve.wait_ge(s_const, 11)
            step(v.tensor_copy(last_f[:, :], last_i[:, :]))
            for c in range(TCH):
                v.tensor_scalar(ended[:, c, :], thr[:, :], last_f[:, c:c + 1], None, ALU.is_gt)\
                    .then_inc(s_ended, 1)
            dve.wait_ge(s_ends_ps, 1)
            step(v.tensor_tensor(ends[0:NEDGE, :], bank(6)[0:NEDGE, 0:1], bcol[0:NEDGE, :], ALU.add))
            v.tensor_scalar(past[0:NEDGE, :], icol[0:NEDGE, :], ends[0:NEDGE, 0:1], None, ALU.is_gt)\
                .then_inc(s_past, 1)
            dve.wait_ge(s_item_ps, 1)
            step(v.tensor_copy(b7[:, :], bank(6, CCH)))
            step(v.tensor_scalar(b128[:, :], b7[:, :], float(P), None, ALU.mult))
            step(v.tensor_tensor(t7[:, :], bank(6, CCH, 64), b7[:, :], ALU.subtract))
            step(v.tensor_copy(tile_index[:, :], t7[:, :]))
            for a, b, source in ((0, HALF, bank(7)), (HALF, COLS, bank(5))):
                step(v.tensor_copy(block_row[0:1, a:b], source[0:1, 0:b - a]))
                step(v.tensor_tensor(tile_rowf[0:1, a:b], icol[0:1, a:b], source[0:1, 0:b - a], ALU.subtract))
            step(v.tensor_scalar(tile_row[0:1, 0:COLS], tile_rowf[0:1, :], float(P), None, ALU.mult))
            v.tensor_copy(t7[:, 0:1], b7[:, 0:1]).then_inc(s_tidx, 1)

            for i in range(5):
                dve.wait_ge(s_x[i], 16)
                with dve.Fori(cut[i] // 2, cut[i + 1] // 2) as p:
                    for u in range(2):
                        v.bn_stats(ln_a[:, u, :], tile_of(x_all, 2 * p + u)).then_inc(s_bn, 1)
                    hold(dve, (s_bn, 2 * p + 2))
                    for u in range(2):
                        v.bn_aggr(mom_a[:, u, :], ln_a[:, u, :]).then_inc(s_mom, 1)
                    need(dve, s_mom, 2 * p + 2)
                    v.tensor_copy(moments[:, ds(2 * p, 2), :], mom_a[:, :, :]).then_inc(s_moms, 1)
            dve.wait_ge(s_moms, PAIRS)
            v.tensor_scalar(vare[:, :], moments[:, :, 1], EPS, None, ALU.add).then_inc(s_vare, 1)
            dve.wait_ge(s_rstd, 1)
            v.scalar_tensor_tensor(shift[:, :], moments[:, :, 0], -1.0, rstd[:, :], ALU.mult, ALU.mult)\
                .then_inc(s_shift, 1)

            for n in range(5):
                dve.wait_ge(s_rows[n], 16 * CCH)
            step(v.tensor_tensor(f_f, g_prev, g_dst, ALU.not_equal))
            step(v.tensor_tensor(g_f, g_next, g_dst, ALU.not_equal))
            step(v.tensor_tensor(rel_f, g_dst, b128[:, :].unsqueeze(2).to_broadcast([P, CCH, P]),
                                 ALU.subtract))
            step(v.tensor_scalar(off_f, rel_f, 0.0, None, ALU.is_ge))
            step(v.scalar_tensor_tensor(valid, rel_f, float(P), off_f, ALU.is_lt, ALU.mult))
            step(v.scalar_tensor_tensor(f_f, f_f, -BIG, valid, ALU.mult, ALU.mult))
            step(v.scalar_tensor_tensor(g_f, g_f, -BIG, valid, ALU.mult, ALU.mult))
            step(v.tensor_copy(src_f, g_src))
            step(v.scalar_tensor_tensor(g_w, g_w, float(DH) ** -0.5, valid, ALU.mult, ALU.mult))
            step(v.tensor_scalar(off_f, valid, BIG, -BIG, ALU.mult, ALU.add))
            v.tensor_copy(t7[:, 0:1], b7[:, 0:1]).then_inc(s_derived, 6)

            def biased(n, u, it=None):
                need(dve, s_rest1, n - 1)
                need(dve, s_q_ps, n + 1)
                v.tensor_tensor(q32[:, u, :], bank(2 + u, D), b_qkv[:, 0:D], ALU.add).then_inc(s_q32, 1)
                if it is not None:
                    dve.wait_ge(s_kv_out[u], it * 32)
                need(dve, s_kv_ps, n + 1)
                v.tensor_tensor(kv[:, u, :], bank(4 + u), b_qkv[:, D:3 * D], ALU.add).then_inc(s_kv, 1)

            dve.wait_ge(s_load, 16 * 8)
            biased(0, 0)
            biased(1, 1)
            with dve.Fori(1, PAIRS) as it:
                for u in range(2):
                    biased(2 * it + u, u, it)
            for n, column in enumerate((rel_item, f_item, g_item, src_item, ews_item, off_item)):
                dve.wait_ge(s_rows_T, n + 1)
                v.tensor_copy(column[:, :], ps[:, 6 * 512:6 * 512 + WIDE]).then_inc(s_item, 1)
            dve.wait_ge(s_item, 6)
            gate(dve, 0)

            def indices(s, g):
                v.tensor_copy(index[:, items_of(g)], src_item[:, ds(s * CHUNKS + g * ITEM_GROUP, ITEM_GROUP)])\
                    .then_inc(s_idx, 1)

            def onehots(s, g):
                need(dve, s_hot_T, s * GROUPS + g - 3)
                for j in range(g * ITEM_GROUP, (g + 1) * ITEM_GROUP):
                    last = v.tensor_scalar(hot[:, j, :], iotab[:, :], rel_item[:, ds(s * CHUNKS + j, 1)],
                                           None, ALU.is_equal)
                last.then_inc(s_hot, 1)

            def heads_of(g):
                return kt[:, items_of(g), 0:D].rearrange("p a (h d) -> p a h d", h=H)

            def add_edges(s, g):
                dve.wait_ge(s_in[g], (s + 1) * 16 * ITEM_GROUP)
                need(dve, s_ep, s * GROUPS + g + 1)
                v.tensor_tensor(heads_of(g), heads_of(g),
                                ep_ps(g).rearrange("p (a d) -> p a d", d=DH)
                                .unsqueeze(2).to_broadcast([P, ITEM_GROUP, H, DH]), ALU.add)\
                    .then_inc(s_added, 1)

            def score_step(s, final=False):
                for g in range(GROUPS):
                    n = s * GROUPS + g
                    rows = kt[:, items_of(g), 0:D]
                    need(dve, s_added, n + 1)
                    need(dve, s_q_e, n + 1)
                    v.tensor_tensor(rows, rows, ps[:, (g % 2) * 1024:(g % 2 + 1) * 1024]
                                    .rearrange("p (a d) -> p a d", d=D), ALU.mult).then_inc(s_prod, 1)
                    if not (final and g == GROUPS - 1):
                        add_edges(s + (g + 1) // GROUPS, (g + 1) % GROUPS)
                    need(dve, s_prod, n + 1)
                    v.tensor_reduce(raw[:, items_of(g), :], heads_of(g), AX.X, ALU.add).then_inc(s_raw, 1)
                    if not (final and g >= 1):
                        onehots(s + (g + 3) // GROUPS, (g + 3) % GROUPS)
                    need(dve, s_raw, n + 1)
                    indices(s + 1, g)
                step_cols = ds(s * CHUNKS, CHUNKS)
                v.tensor_tensor(scaled[:, :, :], raw[:, :, :], ews_item[:, step_cols].unsqueeze(2)
                                .to_broadcast([P, CHUNKS, H]), ALU.mult).then_inc(s_scaled, 1)
                need(dve, s_scaled, s + 1)
                need(dve, s_scores_T, s)
                v.tensor_tensor(masked[:, :, :], scaled[:, :, :], off_item[:, step_cols].unsqueeze(2)
                                .to_broadcast([P, CHUNKS, H]), ALU.add).then_inc(s_masked, 1)

            v.memset(efT[ED:ED + 1, :, :], 1.0).then_inc(s_efone, 1)
            for g in range(GROUPS):
                indices(0, g)
            for g in range(3):
                onehots(0, g)
            add_edges(0, 0)
            with dve.Fori(0, STEPS - 1) as s:
                score_step(s)
            score_step(STEPS - 1, True)
            gate(dve, 1)
            for g in range(GROUPS):
                indices(0, g)

            def backwards(view, back):
                return view[:, ::-1] if back else view

            def scan(out, flags, values, start):
                return v.tensor_tensor_scan(out, flags, values, start, ALU.add, ALU.max)

            for back in range(2):
                flags = backwards((fline, gline)[back], back)
                out = backwards(reach, back)
                scan(out, flags, backwards((line, reach)[back], back), -BIG).then_inc(s_scan, 1)
                dve.wait_ge(s_scan, back + 1)
                dve.wait_ge(s_edge, back + 1)
                step(v.tensor_copy(edge_row[0:1, :, :], bank(0)[0:1, 0:2 * P].rearrange("p (a b) -> p a b", a=2)))
                step(v.memset(carry_row[0:1, :], -BIG))
                for h in range(H):
                    ends_h = edge_row[0:1, 0, h:P:H]
                    sums_h = edge_row[0:1, 1, h:P:H]
                    out_h = carry_row[0:1, h:P:H] if back else carry_row[0:1, H + h:H + P:H]
                    last = scan(backwards(out_h, back), backwards(sums_h, back), backwards(ends_h, back), -BIG)
                last.then_inc(s_rows_c, 1)
                dve.wait_ge(s_carry, back + 1)
                step(v.tensor_copy(carry[:, :], bank(1, 1)))
                step(scan(out, flags, out, carry[:, 0:1]))
            for half in range(2):
                a, b = LINE * half // 2, LINE * (half + 1) // 2
                v.tensor_tensor(line[:, a:b], line[:, a:b], reach[:, a:b], ALU.subtract).then_inc(s_sub, 1)
            with dve.Fori(0, STEPS // 2) as two:
                for u in range(2):
                    need(dve, s_slice_T, 2 * two + u + 1)
                    v.tensor_copy(ex_all[:, ds((2 * two + u) * P, P)], bank(6 + u, P)).then_inc(s_ex, 1)
            dve.wait_ge(s_ex, STEPS + credit[s_ex])
            gate(dve, 2)

            def onehot32(s, g, i):
                j = g * ITEM_GROUP + i
                if i == 0:
                    need(dve, s_y, s * CHUNKS + j - 12)
                ins = v.tensor_scalar(hot32[:, j, :], iota[:, :], rel_item[:, ds(s * CHUNKS + j, 1)],
                                      None, ALU.is_equal)
                if i == ITEM_GROUP - 1:
                    ins.then_inc(s_hot32, 1)

            def weigh(s, g):
                ex = ex_all[:, ds(s * P + g * ITEM_GROUP * H, ITEM_GROUP * H)].rearrange("p (a h) -> p a h", h=H)
                dve.wait_ge(s_in[g], (s + STEPS + 1) * 16 * ITEM_GROUP)
                v.tensor_tensor(heads_of(g), heads_of(g), ex.unsqueeze(3).to_broadcast([P, ITEM_GROUP, H, DH]),
                                ALU.mult).then_inc(s_wv, 1)

            def sum_step(s, final=False):
                for g in range(GROUPS):
                    blocks = load_group(ENG.DVE, block_row, s, g, BLOCKS - 1)
                    if not (final and g == GROUPS - 1):
                        weigh(s + (g + 1) // GROUPS, (g + 1) % GROUPS)
                    for i in range(ITEM_GROUP):
                        j = g * ITEM_GROUP + i
                        need(dve, s_y, s * CHUNKS + j + 1)
                        need(dve, s_acc, s * CHUNKS + j)
                        v.tensor_tensor(tile_of(sums, blocks[i]), tile_of(sums, blocks[i]),
                                        bank(j % 8, ROW), ALU.add).then_inc(s_acc, 1)
                        if not (final and g >= GROUPS - 2):
                            onehot32(s + (g + 2) // GROUPS, (g + 2) % GROUPS, i)
                    indices(s + 1, g)

            for g in range(2):
                for i in range(ITEM_GROUP):
                    onehot32(0, g, i)
            weigh(0, 0)
            dve.wait_ge(s_zero, 2)
            with dve.Fori(0, STEPS - 1) as s:
                sum_step(s)
            sum_step(STEPS - 1, True)
            need(dve, s_acc, COLS)
            gate(dve, 3)

            dve.wait_ge(f_bias, 32)
            v.tensor_scalar(bo_a, bo_row, alpha, None, ALU.mult).then_inc(f_rows, 1)
            v.tensor_scalar(b2_b, b2_row, beta, None, ALU.mult).then_inc(f_rows, 1)
            dve.wait_ge(f_rows, 2)

            def attention(p):
                v.tensor_scalar(den[:, :, :], sums[:, ds(2 * p, 2), D:ROW], 0.5, None, ALU.max)\
                    .then_inc(f_den0, 1)
                need(dve, f_den0, p + 1)
                v.reciprocal(den[:, :, :], den[:, :, :]).then_inc(f_den, 1)
                need(dve, f_den, p + 1)
                need(dve, f_attT_ps, p)
                for u in range(2):
                    v.tensor_tensor(att[:, u, :].rearrange("p (h d) -> p h d", h=H),
                                    sums[:, ds(2 * p + u, 1), 0:D].rearrange("p t (h d) -> p (t h) d", h=H),
                                    den[:, u, :].unsqueeze(2).to_broadcast([P, H, DH]), ALU.mult)\
                        .then_inc(f_att, 1)

            def place_att(p):
                need(dve, f_wo, 2 * p)
                need(dve, f_attT_ps, p + 1)
                v.tensor_copy(attT.rearrange("p c n -> p (c n)"), bank(0)).then_inc(f_attT, 1)

            def place_xn2(p):
                need(dve, f_h, FC * p)
                need(dve, f_xn2T_ps, p + 1)
                for c in range(DC):
                    last = v.tensor_scalar(xn2T[:, c, :], bank(1, 2 * P, c * 2 * P), g2[:, c:c + 1],
                                           b2v[:, c:c + 1], ALU.mult, ALU.add)
                last.then_inc(f_xn2T, 1)

            def statistics(values, p, side):
                stat, mom, var, _, bn, moms, vars_, _ = side
                for u in range(2):
                    v.bn_stats(stat[:, u, :], values[:, u, :]).then_inc(bn, 1)
                hold(dve, (bn, 2 * p + 2))
                for u in range(2):
                    v.bn_aggr(mom[:, u, :], stat[:, u, :]).then_inc(moms, 1)
                need(dve, moms, 2 * p + 2)
                v.tensor_scalar(var[:, :], mom[:, :, 1], EPS, None, ALU.add).then_inc(vars_, 1)

            def normalised(values, p, side, out, done):
                _, mom, _, inv, _, _, _, invs = side
                need(dve, invs, p + 1)
                for u in range(2):
                    v.tensor_scalar(out[:, u, :], values[:, u, :], mom[:, u, 0:1], inv[:, u:u + 1],
                                    ALU.subtract, ALU.mult).then_inc(done, 1)

            side_a = (ln_a, mom_a, var_a, inv_a, f_bn1, f_mom1, f_var1, f_inv1)
            side_b = (ln_b, mom_b, var_b, inv_b, f_bn2, f_mom2, f_var2, f_inv2)

            def residual(p):
                need(dve, f_half, p)
                dve.wait_ge(f_x, (p + 1) * 16)
                for u in range(2):
                    need(dve, f_wo, 2 * p + u + 1)
                    v.scalar_tensor_tensor(x1[:, u, :], bank(2 + u, D), alpha, x_in[:, u, :],
                                           ALU.mult, ALU.add).then_inc(f_x1a, 1)
                for u in range(2):
                    need(dve, f_x1a, 2 * p + u + 1)
                    v.tensor_tensor(x1[:, u, :], x1[:, u, :], bo_a, ALU.add).then_inc(f_x1, 1)
                need(dve, f_x1, 2 * p + 2)
                statistics(x1, p, side_a)

            def normalise_x1(p):
                need(dve, f_xn2T_ps, p)
                normalised(x1, p, side_a, xn2, f_xn2)

            def sum_y(p, odd):
                need(dve, f_both, p + 1)
                for u in range(2):
                    need(dve, f_ff, 2 * p + u + 1)
                    v.scalar_tensor_tensor(y_sum[:, u, :], bank(6 + u, D), beta, both[odd][:, u, :],
                                           ALU.mult, ALU.add).then_inc(f_y, 1)

            def statistics_y(p):
                need(dve, f_y, 2 * p + 2)
                statistics(y_sum, p, side_b)

            def normalise_y(p, first=False):
                if not first:
                    dve.wait_ge(f_store, p * 16)
                normalised(y_sum, p, side_b, y_out, f_out)

            def pair(p, odd, first=False, ahead=2):
                if ahead >= 1:
                    residual(p + 1)
                if not first:
                    statistics_y(p - 1)
                if ahead >= 1:
                    normalise_x1(p + 1)
                if ahead >= 2:
                    attention(p + 2)
                if not first:
                    normalise_y(p - 1, isinstance(p, int) and p == 1)
                if ahead >= 1:
                    place_xn2(p + 1)
                if ahead >= 2:
                    place_att(p + 2)
                if not first:
                    need(dve, f_out, 2 * p)
                sum_y(p, odd)

            attention(0)
            place_att(0)
            residual(0)
            normalise_x1(0)
            attention(1)
            place_xn2(0)
            place_att(1)
            pair(0, 0, first=True)
            pair(1, 1)
            with dve.Fori(0, (PAIRS - 4) // 2) as two:
                pair(2 * two + 2, 0)
                pair(2 * two + 3, 1)
            for p in range(2 + (PAIRS - 4) // 2 * 2, PAIRS - 2):
                pair(p, p % 2)
            pair(PAIRS - 2, PAIRS % 2, ahead=1)
            pair(PAIRS - 1, 1 - PAIRS % 2, ahead=0)
            statistics_y(PAIRS - 1)
            normalise_y(PAIRS - 1)


def kernel(**inputs):
    import concourse.bacc as bacc
    from concourse.bass_utils import run_bass_kernel_spmd

    a = {k.removeprefix("L0_gnn_"): np.asarray(v) for k, v in inputs.items()}
    n_nodes, D = a["x"].shape
    n_edges = a["src"].shape[0]
    ED, DH = a["We"].shape
    FF = a["W1"].shape[1]
    Z = sizes(n_nodes, n_edges)
    rows, tiles = 2 * Z["pairs"] * P, Z["tile_chunks"] * P

    x = np.zeros((rows, D), a["x"].dtype)
    x[:n_nodes] = a["x"]
    beyond = Z["blocks"] * P
    dst = np.full(tiles * P + 2, beyond, np.int32)
    dst[0] = -1
    dst[1:n_edges + 1] = a["dst"]
    src = np.zeros(tiles * P, np.int32)
    src[:n_edges] = a["src"]
    ew = np.zeros(tiles * P, a["edge_weight"].dtype)
    ew[:n_edges] = a["edge_weight"]
    ef = np.zeros((ED, tiles * P), a["edge_attr_64"].dtype)
    ef[:, :n_edges] = a["edge_attr_64"].T

    def columns(v):
        return v.reshape(-1, P).T

    arrays = {
        "x": x, "dst_rows": dst[1:-1].reshape(tiles, P), "prev_rows": dst[:-2].reshape(tiles, P),
        "next_rows": dst[2:].reshape(tiles, P), "src_rows": src.reshape(tiles, P),
        "w_rows": ew.reshape(tiles, P), "dst_last": columns(dst[1:-1].reshape(tiles, P)[:, P - 1]),
        "efT": ef, "Wq": a["Wq"], "Wk": a["Wk"], "Wv": a["Wv"],
        "b_qkv": np.concatenate([a["bq"], a["bk"], a["bv"]]),
        "cols": np.concatenate([columns(a[k]) for k in ("ln1_g", "ln1_b", "ln2_g", "ln2_b", "b1")], axis=1),
        "alpha": a["alpha"], "beta": a["beta"], "We_be": np.concatenate([a["We"], a["be"][None]]),
        "Wo": a["Wo"], "W1": a["W1"], "W2": a["W2"], "bo": a["bo"], "b2": a["b2"],
    }
    nc = bacc.Bacc("TRN2", target_bir_lowering=False, num_devices=1)
    A, ins = {}, {}
    for name, v in arrays.items():
        v = np.ascontiguousarray(v)
        ins["in_" + name] = v
        A[name] = nc.dram_tensor("in_" + name, v.shape, mybir.dt.from_np(v.dtype), kind="ExternalInput").ap()
    A["out"] = nc.dram_tensor("out", (rows, D), mybir.dt.float32, kind="ExternalOutput").ap()
    graph_layer(nc, A, n_nodes, n_edges, (D, D // DH, ED, FF))
    r = run_bass_kernel_spmd(nc, [ins], core_ids=[0])
    return r.results[0]["out"][:n_nodes]
```

```python
from contextlib import ExitStack

import concourse.bass as bass
from concourse import mybir
import numpy as np

P = 128
ITEM_GROUP = 4
CHUNKS = 16
GROUPS = CHUNKS // ITEM_GROUP
BIG = 1.0e30
EPS = 1.0e-5


def ceil_div(a, b):
    return -(-a // b)


def sizes(n_nodes, n_edges):
    blocks = ceil_div(n_nodes, P)
    tiles = ceil_div(n_edges, P)
    items = tiles + blocks - 1
    steps = 4 * ceil_div(items, 4 * CHUNKS)
    return dict(blocks=blocks, tiles=tiles, items=items, steps=steps, pairs=ceil_div(blocks, 2),
                tile_chunks=ceil_div(max(tiles, steps * CHUNKS) + 1, P),
                col_chunks=ceil_div((steps + 1) * CHUNKS, P))


def graph_layer(nc, A, n_nodes, n_edges, dims):
    D, H, ED, FF = dims
    DH = D // H
    DC = D // P
    FC = FF // P
    ROW = D + H
    GROUP_ROW = (ITEM_GROUP - 1) * ROW + 2 * D
    Z = sizes(n_nodes, n_edges)
    BLOCKS, STEPS, PAIRS = Z["blocks"], Z["steps"], Z["pairs"]
    TCH, CCH = Z["tile_chunks"], Z["col_chunks"]
    COLS = STEPS * CHUNKS
    WIDE = CCH * P
    NTILES = 2 * PAIRS
    LINE = STEPS * P
    NEDGE = BLOCKS - 1
    fp32, bf16, i32 = mybir.dt.float32, mybir.dt.bfloat16, mybir.dt.int32
    ALU, ACT, AX = mybir.AluOpType, mybir.ActivationFunctionType, mybir.AxisListType
    ENG = mybir.EngineType
    ds = bass.ds

    ctx = ExitStack()
    with ctx:
        def sb(name, shape, dt):
            return ctx.enter_context(nc.sbuf_tensor("sb_" + name, shape, dt))

        def sem(name):
            return ctx.enter_context(nc.semaphore(name))

        def carve(region, at, shape, dt):
            n = int(np.prod(shape)) * (2 if dt == bf16 else 4)
            v = region[:, at // 4:(at + n) // 4]
            if dt != fp32:
                v = v.bitcast(dt)
            if len(shape) == 2:
                v = v.rearrange("p (a b) -> p a b", a=shape[0])
            if len(shape) == 3:
                v = v.rearrange("p (a b c) -> p a b c", a=shape[0], b=shape[1])
            return v, at + n

        r_q = sb("r_q", [P, max(NTILES * 3 * D // 2, NTILES * ROW)], fp32)
        r_line = sb("r_line", [P, max(NTILES * D, 2 * LINE)], fp32)
        r_item = sb("r_item", [P, 5 * WIDE], fp32)
        r_kt = sb("r_kt", [P, max(CCH * (2 * P + 2) + 3 * WIDE, GROUPS * GROUP_ROW)], fp32)
        r_w = sb("r_w", [P, max(DC * D + DC * FF, (DC + 1) * 3 * D)], fp32)
        r_tmp = sb("r_tmp", [P, max(4672, LINE // 2 + 4 * P)], fp32)

        q3, _ = carve(r_q, 0, (NTILES, 3, D), bf16)
        sums, _ = carve(r_q, 0, (NTILES, ROW), fp32)
        QB = NTILES * 3 * D * 2
        reach = r_q[:, NTILES * ROW - LINE:NTILES * ROW]
        KEEP = (NTILES * ROW - LINE) // ROW
        x_all, _ = carve(r_line, 0, (NTILES, D), fp32)
        line = r_line[:, 0:LINE]
        fline = r_line[:, LINE:LINE + LINE // 2].bitcast(bf16)
        gline = r_line[:, LINE + LINE // 2:2 * LINE].bitcast(bf16)
        ex_all = r_line[:, LINE:2 * LINE]
        src_item, at = carve(r_item, 0, (WIDE,), i32)
        rel_item, at = carve(r_item, at, (WIDE,), fp32)
        ews_item, at = carve(r_item, at, (WIDE,), fp32)
        off_item, at = carve(r_item, at, (WIDE,), fp32)
        f_item, at = carve(r_item, at, (WIDE,), bf16)
        g_item, at = carve(r_item, at, (WIDE,), bf16)
        kt, _ = carve(r_kt, 0, (GROUPS, GROUP_ROW), fp32)
        g_row, at = carve(r_kt, 0, (CCH, 2 * P + 2), i32)
        g_prev, g_dst, g_next = (g_row[:, :, i:i + P] for i in range(3))
        src_f = r_kt[:, 0:CCH * (2 * P + 2)].rearrange("p (a b) -> p a b", a=CCH)[:, :, P + 2:]
        g_w, at = carve(r_kt, at, (CCH, P), fp32)
        rel_f, at = carve(r_kt, at, (CCH, P), fp32)
        f_f, _ = carve(r_kt, at, (CCH, P), fp32)
        g_f, _ = carve(r_item, 0, (CCH, P), fp32)
        tail = QB - 4 * (2 * WIDE + TCH * NEDGE + COLS)
        assert tail > 0
        icol, at = carve(r_q, tail, (WIDE,), fp32)
        past, at = carve(r_q, at, (WIDE,), fp32)
        valid, _ = carve(r_item, 8 * WIDE, (CCH, P), fp32)
        off_f, _ = carve(r_item, 12 * WIDE, (CCH, P), fp32)
        ended, at = carve(r_q, at, (TCH, NEDGE), fp32)
        tile_rowf, _ = carve(r_q, at, (COLS,), fp32)
        w_qkv, at = carve(r_w, 0, (DC, 3 * D), fp32)
        b_qkv, at = carve(r_w, at, (3 * D,), fp32)
        w_o, at = carve(r_w, 0, (DC, D), fp32)
        w_1, at = carve(r_w, at, (DC, FF), fp32)
        w_2, _ = carve(r_line, 0, (FC, D), fp32)
        xn, at = carve(r_tmp, 0, (2, D), fp32)
        xnT, at = carve(r_tmp, at, (2, DC, P), fp32)
        q32, at = carve(r_tmp, at, (2, D), fp32)
        qrest, at = carve(r_tmp, at, (2, D), fp32)
        kv, at = carve(r_tmp, at, (2, 2 * D), fp32)
        moments, at = carve(r_tmp, at, (NTILES, 2), fp32)
        rstd, at = carve(r_tmp, at, (NTILES,), fp32)
        shift, at = carve(r_tmp, at, (NTILES,), fp32)
        vare, at = carve(r_tmp, at, (NTILES,), fp32)
        efT, at = carve(r_tmp, 0, (CHUNKS, P), fp32)
        hot, at = carve(r_tmp, at, (CHUNKS, P), bf16)
        hotT, at = carve(r_tmp, at, (CHUNKS, P), bf16)
        raw, at = carve(r_tmp, at, (CHUNKS, H), fp32)
        scaled, at = carve(r_tmp, at, (CHUNKS, H), fp32)
        masked, at = carve(r_tmp, at, (CHUNKS, H), fp32)
        dist, at = carve(r_tmp, at, (P,), bf16)
        fwide, at = carve(r_tmp, at, (CHUNKS, H), bf16)
        gwide, at = carve(r_tmp, at, (CHUNKS, H), bf16)
        hot32, at = carve(r_tmp, 0, (CHUNKS, P), fp32)
        dist32, at = carve(r_tmp, at, (P,), fp32)
        junk, at = carve(r_tmp, 0, (LINE,), bf16)
        edge_row, at = carve(r_tmp, at, (2, P), fp32)
        carry_row, at = carve(r_tmp, at, (P + 2 * H,), fp32)
        exslice, _ = carve(r_tmp, 0, (2, 4 * P), fp32)
        att, at = carve(r_kt, 0, (2, D), fp32)
        attT, at = carve(r_kt, at, (DC, 2 * P), fp32)
        x_in, at = carve(r_kt, at, (2, D), fp32)
        x1, at = carve(r_kt, at, (2, D), fp32)
        xn2, at = carve(r_kt, at, (2, D), fp32)
        xn2T, at = carve(r_kt, at, (DC, 2 * P), fp32)
        both_a, at = carve(r_kt, at, (2, D), fp32)
        gelu, at = carve(r_tmp, 0, (FC, 2 * P), fp32)
        y_sum, at = carve(r_tmp, at, (2, D), fp32)
        both_b, at = carve(r_tmp, at, (2, D), fp32)
        both = (both_a, both_b)
        y_out, at = carve(r_tmp, at, (2, D), fp32)
        bo_row, at = carve(r_tmp, at, (D,), fp32)
        b2_row, at = carve(r_tmp, at, (D,), fp32)
        bo_a, at = carve(r_tmp, at, (D,), fp32)
        b2_b, at = carve(r_tmp, at, (D,), fp32)

        ident = sb("ident", [P, P], fp32)
        identb = sb("identb", [P, P], bf16)
        iota = sb("iota", [P, P], fp32)
        iotab = sb("iotab", [P, P], bf16)
        ones = sb("ones", [P, 1], fp32)
        index = sb("index", [P, CHUNKS], i32)
        tile_index = sb("tile_index", [P, CCH], i32)
        b7 = sb("b7", [P, CCH], fp32)
        b128 = sb("b128", [P, CCH], fp32)
        t7 = sb("t7", [P, CCH], fp32)
        last_i = sb("last_i", [P, TCH], i32)
        last_f = sb("last_f", [P, TCH], fp32)
        thr = sb("thr", [P, NEDGE], fp32)
        ends = sb("ends", [P, 1], fp32)
        bcol = sb("bcol", [P, 1], fp32)
        block_row = sb("block_row", [1, COLS + CHUNKS], i32)
        tile_row = sb("tile_row", [1, COLS + CHUNKS], i32)
        halfneg = sb("halfneg", [P, NTILES], fp32)
        cols = sb("cols", [P, 4 * DC + FC + 2], fp32)
        we = sb("we", [ED + 1, DH], fp32)
        flag_sum = sb("flag_sum", [P, 2], fp32)
        carry = sb("carry", [P, 1], fp32)
        warm = sb("warm", [P, 1], fp32)
        den = sb("den", [P, 2, H], fp32)
        ln_a = sb("ln_a", [P, 2, 6], fp32)
        ln_b = sb("ln_b", [P, 2, 6], fp32)
        mom_a = sb("mom_a", [P, 2, 2], fp32)
        mom_b = sb("mom_b", [P, 2, 2], fp32)
        var_a = sb("var_a", [P, 2], fp32)
        var_b = sb("var_b", [P, 2], fp32)
        inv_a = sb("inv_a", [P, 2], fp32)
        inv_b = sb("inv_b", [P, 2], fp32)
        g1, b1v, g2, b2v = (cols[:, i * DC:(i + 1) * DC] for i in range(4))
        bias1 = cols[:, 4 * DC:4 * DC + FC]
        alpha = cols[:, 4 * DC + FC:4 * DC + FC + 1]
        beta = cols[:, 4 * DC + FC + 1:4 * DC + FC + 2]

        ps = ctx.enter_context(nc.psum_tensor("ps", [P, 4096], fp32))

        def bank(i, n=512, off=0):
            return ps[:, i * 512 + off:i * 512 + off + n]

        TABLE = NTILES * P
        k_v_table = nc.dram_tensor("k_v_table", (2 * TABLE, D), fp32).ap()
        kv_table = nc.dram_tensor("kv_table", (NTILES * P, 2 * D), fp32).ap()
        v_kept = nc.dram_tensor("v_kept", (STEPS * GROUPS, P, D), fp32).ap()


        HALF = COLS // 2
        QUADS = STEPS // 4
        AHEAD = min(5, PAIRS // 3)
        MAIN = PAIRS - AHEAD
        SPLIT = max(QUADS // 4 * 8 * P, P)
        FIRST = QUADS // 4 * 2
        cut = [2 * (PAIRS * i // 5) for i in range(6)]

        def hot_ps(g):
            return bank(4, 256).bitcast(bf16).rearrange("p (a b) -> p a b", b=P)

        def ep_ps(g):
            return bank(5 + 2 * (g % 2), ITEM_GROUP * DH)

        def flag_ps(i):
            return bank(6, 64, P + i * 64).bitcast(bf16)

        s_const = sem("consts_made")
        s_credit = sem("credits_given")
        s_held = sem("waits_carried")
        s_load = sem("params_loaded")
        s_last = sem("last_dst_loaded")
        s_x = [sem(f"x_loaded{i}") for i in range(5)]
        s_w = sem("finish_weights_loaded")
        s_w2 = sem("last_weights_loaded")
        gates = [sem(f"gate{i}") for i in range(4)]
        s_step = sem("vector_step")
        s_ended = sem("ended_ready")
        s_ends_ps = sem("ends_summed")
        s_past = sem("past_ready")
        s_item_ps = sem("items_placed")
        s_index_t = sem("tile_index_ready")
        s_tidx = sem("item_rows_ready")
        s_rows = [sem(f"tile_rows_gathered{i}") for i in range(2)]
        s_derived = sem("derived_rows_ready")
        s_rows_T = sem("rows_transposed")
        s_item = sem("item_columns_ready")
        s_bn = sem("tile_stats_ready")
        s_mom = sem("tile_moments_ready")
        s_moms = sem("moments_kept")
        s_vare = sem("variances_ready")
        s_rstd = sem("rstd_ready")
        s_shift0 = sem("scaled_mean_ready")
        s_shift = sem("shift_ready")
        s_xn = sem("xn_ready")
        s_xT_ps = sem("xn_transposed")
        s_xT = sem("xnT_ready")
        s_q_ps = sem("q_projected")
        s_kv_ps = sem("kv_projected")
        s_q32 = sem("q_biased")
        s_q1 = sem("q_part1_ready")
        s_rest1 = sem("q_rest_ready")
        s_q2 = sem("q_part2_ready")
        s_q3 = sem("q_part3_ready")
        s_kv = sem("kv_biased")
        s_kv_out = [sem(f"kv_stored{i}") for i in range(2)]
        s_idx = sem("index_ready")
        s_in = [sem(f"rows_gathered{g}") for g in range(GROUPS)]
        s_keep = [sem(f"v_of_last_item_stored{g}") for g in range(GROUPS)]
        s_back = [sem(f"v_of_last_item_loaded{g}") for g in range(GROUPS)]
        s_ef = [sem(f"edge_features_loaded{g}") for g in range(GROUPS)]
        s_efone = sem("ones_row_ready")
        s_hot = sem("onehot_ready")
        s_dist = sem("distance_ready")
        s_hot_a = sem("last_onehot_of_group_ready")
        s_hot_T = sem("onehot_transposed")
        s_hotT = sem("onehotT_ready")
        s_q_e = sem("q_of_edges_ready")
        s_ep = sem("edge_projection_ready")
        s_added = sem("edge_projection_added")
        s_prod = sem("q_times_k_ready")
        s_raw = sem("scores_raw")
        s_scaled = sem("scores_scaled")
        s_masked = sem("scores_masked")
        s_wide = sem("flags_widened")
        s_flags_T = sem("flags_transposed")
        s_flags = sem("flags_stored")
        s_scores_T = sem("scores_transposed")
        s_scores = sem("scores_stored")
        s_fsum = sem("flags_summed")
        s_scan = sem("chunks_scanned")
        s_edge = sem("chunk_ends_in_a_row")
        s_rows_c = sem("carry_row_ready")
        s_carry = sem("carry_column_ready")
        s_sub = sem("maximum_subtracted")
        s_zero = sem("sums_zeroed")
        s_slice = sem("slice_copied")
        s_slice_T = sem("slice_transposed")
        s_ex = sem("softmax_terms_ready")
        s_hot32 = sem("onehot32_ready")
        s_dist32 = sem("distance32_ready")
        s_hot32_a = sem("last_onehot32_of_group_ready")
        s_wv = sem("v_weighed")
        s_wv_a = sem("v_of_last_item_weighed")
        s_wex = sem("terms_beside_v")
        s_y = sem("item_summed")
        s_acc = sem("item_added")
        f_bias = sem("bias_rows_loaded")
        f_rows = sem("bias_rows_scaled")
        f_x = sem("finish_x_loaded")
        f_den0 = sem("denominators_guarded")
        f_den = sem("denominators_inverted")
        f_att = sem("attention_normalised")
        f_attT_ps = sem("attention_transposed")
        f_attT = sem("attentionT_ready")
        f_wo = sem("attention_projected")
        f_x1a = sem("x1_without_bias")
        f_x1 = sem("x1_ready")
        f_bn1 = sem("x1_stats")
        f_mom1 = sem("x1_moments")
        f_var1 = sem("x1_variance")
        f_inv1 = sem("x1_rstd")
        f_half = sem("x_plus_x1")
        f_both = sem("residuals_ready")
        f_xn2 = sem("xn2_ready")
        f_xn2T_ps = sem("xn2_transposed")
        f_xn2T = sem("xn2T_ready")
        f_h = sem("hidden_ready")
        f_gelu = sem("gelu_ready")
        f_ff = sem("mlp_ready")
        f_y = sem("y_ready")
        f_bn2 = sem("y_stats")
        f_mom2 = sem("y_moments")
        f_var2 = sem("y_variance")
        f_inv2 = sem("y_rstd")
        f_out = sem("out_ready")
        f_store = sem("out_stored")

        credit = {s_q32: 1, s_kv: 1, s_rest1: 2, s_ep: 4, s_added: 2, s_hotT: 2, s_prod: 2, s_q_e: 4,
                  s_hot_T: 4, s_scores_T: 1, s_scores: 2, s_flags_T: 1, s_flags: 1, s_slice_T: 2, s_ex: 2,
                  s_y: 16, s_acc: 8, s_hot_a: 1, f_attT_ps: 1, f_attT: 1, f_x1a: 2, f_xn2T: 1, f_xn2T_ps: 1,
                  f_gelu: 2, f_y: 4, f_half: 1, f_wo: 1, f_h: 1, s_hot32_a: 1}

        def need(eng, semaphore, count):
            eng.wait_ge(semaphore, count + credit.get(semaphore, 0))

        def hold(eng, *needs):
            for semaphore, count in needs:
                need(eng, semaphore, count)
            eng.sem_inc(s_held, 1)

        def gate(eng, i):
            eng.drain().then_inc(gates[i], 1)
            eng.wait_ge(gates[i], 5)

        def load_group(engine, row, s, g, top):
            return nc.values_load_multi_w_load_instructions(
                row[0:1, ds(s * CHUNKS + g * ITEM_GROUP, ITEM_GROUP)], engines=(engine,), min_val=0, max_val=top,
                skip_runtime_bounds_check_because="the prepare stage counts at most BLOCKS - 1 ends, and no "
                                                  "more ends than items, whatever the edges are")[1]

        def tile_of(view, n):
            return view[:, ds(n, 1), :].rearrange("p t d -> p (t d)")

        def part_of(n, part):
            return q3[:, ds(n, 1), part, :].rearrange("p t d -> p (t d)")

        def items_of(g):
            return slice(g * ITEM_GROUP, (g + 1) * ITEM_GROUP)

        def rows_of(g):
            return kt[:, g, 0:ITEM_GROUP * ROW].rearrange("p (a r) -> p a r", r=ROW)[:, :, 0:D]

        def heads_of(g):
            return rows_of(g).rearrange("p a (h d) -> p a h d", h=H)

        block = ctx.enter_context(nc.Block())

        @block.sync
        def _(sp):
            for semaphore, count in credit.items():
                sp.sem_inc(semaphore, count)
            sp.sem_inc(s_credit, 1)

            def load(dst, src):
                sp.dma_start(dst, src).then_inc(s_load, 16)

            sp.dma_start(last_i[:, :], A["dst_last"]).then_inc(s_last, 16)
            xv = A["x"].rearrange("(t p) d -> p t d", p=P)
            for i in range(5):
                sp.dma_start(x_all[:, cut[i]:cut[i + 1], :], xv[:, cut[i]:cut[i + 1], :]).then_inc(s_x[i], 16)
            load(w_qkv[:, :, 0:D], A["Wq"].rearrange("(c p) n -> p c n", p=P))
            load(w_qkv[:, :, D:2 * D], A["Wk"].rearrange("(c p) n -> p c n", p=P))
            load(w_qkv[:, :, 2 * D:3 * D], A["Wv"].rearrange("(c p) n -> p c n", p=P))
            load(b_qkv[:, :], A["b_qkv"].partition_broadcast(P))
            load(cols[:, 0:4 * DC + FC], A["cols"])
            load(alpha, A["alpha"].partition_broadcast(P))
            load(beta, A["beta"].partition_broadcast(P))
            load(we[:, :], A["We_be"])

            kv_both = k_v_table.rearrange("(b t p) d -> t p b d", b=2, p=P)
            kv_kv = kv_table.rearrange("(t p) d -> t p d", p=P)
            with sp.Fori(0, PAIRS) as it:
                for u in range(2):
                    hold(sp, (s_kv, 2 * it + u + 1))
                    sp.dma_start(kv_both[ds(2 * it + u, 1), :, :, :].rearrange("t p b d -> (t p) b d"),
                                 kv[:, u, :].rearrange("p (b d) -> p b d", b=2)).then_inc(s_kv_out[u], 16)
                    sp.dma_start(kv_kv[ds(2 * it + u, 1), :, :].rearrange("t p d -> (t p) d"),
                                 kv[:, u, :]).then_inc(s_kv_out[u], 16)
            for u in range(2):
                sp.wait_ge(s_kv_out[u], 32 * PAIRS)
            gate(sp, 0)

            sp.dma_start(w_o[:, :, :], A["Wo"].rearrange("(c p) n -> p c n", p=P)).then_inc(s_w, 16)
            sp.dma_start(w_1[:, :, :], A["W1"].rearrange("(c p) n -> p c n", p=P)).then_inc(s_w, 16)

            def edge_features(s, g):
                first = load_group(ENG.SP, tile_row, s, g, (TCH * P - 1) * P)
                hold(sp, (s_ep, s * GROUPS + g - 3))
                for i in range(ITEM_GROUP):
                    sp.dma_start(efT[0:ED, g * ITEM_GROUP + i, :], A["efT"][:, ds(first[i], P)])\
                        .then_inc(s_ef[g], 16)

            def keep_v(s, g):
                hold(sp, (s_in[g], (s + 1) * 16 * ITEM_GROUP))
                sp.dma_start(v_kept[ds(s * GROUPS + g, 1), :, :].rearrange("t p d -> (t p) d"),
                             kt[:, g, GROUP_ROW - D:GROUP_ROW]).then_inc(s_keep[g], 16)

            def bring_v(s, g):
                hold(sp, (s_idx, s * GROUPS + (STEPS + 1) * GROUPS + g + 1))
                sp.dma_start(rows_of(g)[:, ITEM_GROUP - 1, :],
                             v_kept[ds(s * GROUPS + g, 1), :, :].rearrange("t p d -> (t p) d"))\
                    .then_inc(s_back[g], 16)

            for g in range(GROUPS):
                edge_features(0, g)
            with sp.Fori(1, STEPS) as s:
                for g in range(GROUPS):
                    edge_features(s, g)
                    keep_v(s - 1, g)
            for g in range(GROUPS):
                keep_v(STEPS - 1, g)
            gate(sp, 1)
            for g in range(GROUPS):
                sp.wait_ge(s_keep[g], 16 * STEPS)
                bring_v(0, g)
            gate(sp, 2)
            sp.dma_start(bo_row[:, :], A["bo"].partition_broadcast(P)).then_inc(f_bias, 16)
            sp.dma_start(b2_row[:, :], A["b2"].partition_broadcast(P)).then_inc(f_bias, 16)
            sp.dma_start(w_2[:, :, :], A["W2"].rearrange("(c p) n -> p c n", p=P)).then_inc(s_w2, 16)
            with sp.Fori(1, STEPS) as s:
                for g in range(GROUPS):
                    bring_v(s, g)
            gate(sp, 3)

            xt = A["x"].rearrange("(t p) d -> p t d", p=P)
            ot = A["out"].rearrange("(t p) d -> p t d", p=P)
            sp.dma_start(x_in[:, :, :], xt[:, 0:2, :]).then_inc(f_x, 16)
            sp.wait_ge(f_both, 1)
            sp.dma_start(x_in[:, :, :], xt[:, 2:4, :]).then_inc(f_x, 16)
            with sp.Fori(0, PAIRS - 2) as it:
                hold(sp, (f_both, it + 2))
                sp.dma_start(x_in[:, :, :], xt[:, ds(2 * it + 4, 2), :]).then_inc(f_x, 16)
                hold(sp, (f_out, 2 * it + 2))
                sp.dma_start(ot[:, ds(2 * it, 2), :], y_out[:, :, :]).then_inc(f_store, 16)
            for p in range(PAIRS - 2, PAIRS):
                sp.wait_ge(f_out, 2 * p + 2)
                sp.dma_start(ot[:, 2 * p:2 * p + 2, :], y_out[:, :, :]).then_inc(f_store, 16)
            sp.wait_ge(f_store, 16 * PAIRS)

        @block.gpsimd
        def _(pool):
            loose = dict(allow_small_or_imprecise_dtypes=True)
            pool.memset(ones[:, :], 1.0).then_inc(s_const, 1)
            pool.memset(ident[:, :], 0.0).then_inc(s_const, 1)
            pool.iota(iota[:, :], [[1, P]], base=0, channel_multiplier=0, **loose).then_inc(s_const, 1)
            pool.iota(iotab[:, :], [[1, P]], base=0, channel_multiplier=0, **loose).then_inc(s_const, 1)
            pool.iota(thr[:, :], [[P, NEDGE]], base=P, channel_multiplier=0, **loose).then_inc(s_const, 1)
            pool.iota(bcol[:, :], [[0, 1]], base=0, channel_multiplier=1, **loose).then_inc(s_const, 1)
            pool.memset(icol[:, COLS:WIDE], 0.0).then_inc(s_const, 1)
            pool.iota(icol[:, 0:COLS], [[1, STEPS], [STEPS, CHUNKS]], base=0, channel_multiplier=0,
                      **loose).then_inc(s_const, 1)
            pool.memset(halfneg[:, :], -0.5).then_inc(s_const, 1)
            pool.wait_ge(s_const, 9)
            pool.affine_select(out=ident[:, :], in_=ident[:, :], compare_op=ALU.not_equal, fill=1.0,
                               base=0, pattern=[[-1, P]], channel_multiplier=1).then_inc(s_const, 1)
            pool.wait_ge(s_const, 10)
            pool.tensor_copy(identb[:, :], ident[:, :]).then_inc(s_const, 1)

            def tile_rows(n, rows, table):
                pool.wait_ge(s_index_t, 1)
                for m in range(CCH):
                    pool.indirect_dma_start(
                        out=rows[:, m, :], out_offset=None, in_=A[table],
                        in_offset=bass.IndirectOffsetOnAxis(ap=tile_index[:, m:m + 1], axis=0))\
                        .then_inc(s_rows[n], 16)

            def root(p):
                hold(pool, (s_vare, p + 1))
                pool.tensor_tensor(rstd[:, ds(2 * p, 2)], vare[:, ds(2 * p, 2)], halfneg[:, 0:2], ALU.pow)\
                    .then_inc(s_rstd, 1)

            def remainders(n, u):
                hold(pool, (s_q1, n + 1))
                pool.tensor_tensor(qrest[:, u, :], q32[:, u, :], part_of(n, 0), ALU.subtract)\
                    .then_inc(s_rest1, 1)
                hold(pool, (s_q2, n + 1))
                pool.tensor_tensor(part_of(n, 2), qrest[:, u, :], part_of(n, 1), ALU.subtract)\
                    .then_inc(s_q3, 1)

            with pool.Fori(0, AHEAD) as p:
                root(p)
            tile_rows(0, g_row, "int_rows")
            tile_rows(1, g_w, "w_rows")
            with pool.Fori(0, MAIN) as p:
                remainders(2 * p, 0)
                root(p + AHEAD)
                remainders(2 * p + 1, 1)
            with pool.Fori(MAIN, PAIRS) as p:
                for u in range(2):
                    remainders(2 * p + u, u)
            gate(pool, 0)

            def gather(out, table, g, i):
                j = g * ITEM_GROUP + i
                pool.indirect_dma_start(
                    out=out, out_offset=None, in_=table,
                    in_offset=bass.IndirectOffsetOnAxis(ap=index[:, j:j + 1], axis=0)).then_inc(s_in[g], 16)

            def gather_k(s, first=False):
                for g in range(GROUPS):
                    hold(pool, (s_idx, s * GROUPS + g + 1))
                    for i in range(ITEM_GROUP - 1):
                        gather(rows_of(g)[:, i, :], k_v_table, g, i)
                    if not first:
                        hold(pool, (s_keep[g], s * 16))
                    gather(kt[:, g, GROUP_ROW - 2 * D:GROUP_ROW], kv_table, g, ITEM_GROUP - 1)

            def gather_v(s):
                for g in range(GROUPS):
                    hold(pool, (s_idx, s * GROUPS + (STEPS + 1) * GROUPS + g + 1))
                    for i in range(ITEM_GROUP - 1):
                        gather(rows_of(g)[:, i, :], k_v_table, g, i)

            gather_k(0, True)
            with pool.Fori(1, STEPS) as s:
                gather_k(s)
            gate(pool, 1)
            gather_v(0)
            pool.memset(sums[:, 0:KEEP, :], 0.0).then_inc(s_zero, 1)
            pool.wait_ge(s_sub, 2)
            pool.memset(sums[:, KEEP:NTILES, :], 0.0).then_inc(s_zero, 1)
            gate(pool, 2)
            with pool.Fori(1, STEPS) as s:
                gather_v(s)
            gate(pool, 3)

            def root1(p):
                hold(pool, (f_var1, p + 1))
                pool.tensor_tensor(inv_a[:, :], var_a[:, :], halfneg[:, 0:2], ALU.pow).then_inc(f_inv1, 1)

            def residuals(p, odd):
                hold(pool, (f_y, 2 * p - 2))
                pool.tensor_tensor(both[odd][:, :, :], x1[:, :, :], x_in[:, :, :], ALU.add).then_inc(f_half, 1)
                hold(pool, (f_half, p + 1))
                pool.tensor_tensor(both[odd][:, :, :], both[odd][:, :, :],
                                   b2_b.unsqueeze(1).to_broadcast([P, 2, D]), ALU.add).then_inc(f_both, 1)

            def root2(p):
                hold(pool, (f_var2, p + 1))
                pool.tensor_tensor(inv_b[:, :], var_b[:, :], halfneg[:, 0:2], ALU.pow).then_inc(f_inv2, 1)

            def roots_of_pair(p, odd):
                root1(p + 1)
                root2(p - 1)
                residuals(p + 1, 1 - odd)

            pool.wait_ge(f_rows, 2)
            for p in range(2):
                root1(p)
                residuals(p, p)
            with pool.Fori(0, (PAIRS - 3) // 2) as two:
                roots_of_pair(2 * two + 1, 1)
                roots_of_pair(2 * two + 2, 0)
            for p in range(1 + (PAIRS - 3) // 2 * 2, PAIRS - 1):
                roots_of_pair(p, p % 2)
            root2(PAIRS - 2)
            root2(PAIRS - 1)

        @block.scalar
        def _(act):
            def mv(out, in_, **kw):
                return nc.scalar.activation(out, in_, ACT.Copy, **kw)

            act.wait_ge(s_credit, 1)
            act.wait_ge(s_shift, 1)
            act.wait_ge(s_load, 16 * 8)

            def normalise(n, u, pair):
                hold(act, (s_xT_ps, n - 1), (s_shift, pair + 1))
                nc.scalar.activation(xn[:, u, :], tile_of(x_all, n), ACT.Identity,
                                     scale=rstd[:, ds(n, 1)], bias=shift[:, ds(n, 1)]).then_inc(s_xn, 1)

            def place_xT(n, u, first=False):
                if first:
                    act.wait_ge(s_xT_ps, n + 1)
                else:
                    hold(act, (s_kv_ps, n - 1), (s_xT_ps, n + 1))
                for c in range(DC):
                    nc.scalar.activation(xnT[:, u, c, :], bank(u, P, c * P), ACT.Identity,
                                         scale=g1[:, c:c + 1], bias=b1v[:, c:c + 1]).then_inc(s_xT, 1)

            def part1(n, u):
                hold(act, (s_q32, n + 1))
                mv(part_of(n, 0), q32[:, u, :]).then_inc(s_q1, 1)

            def part2(n, u):
                hold(act, (s_rest1, n + 1))
                mv(part_of(n, 1), qrest[:, u, :]).then_inc(s_q2, 1)

            for n in range(2):
                nc.scalar.activation(xn[:, n, :], x_all[:, n, :], ACT.Identity, scale=rstd[:, n:n + 1],
                                     bias=shift[:, n:n + 1]).then_inc(s_xn, 1)
            place_xT(0, 0, True)
            place_xT(1, 1, True)
            with act.Fori(0, PAIRS - 1) as it:
                for u in range(2):
                    normalise(2 * it + 2 + u, u, it + 1)
                    part1(2 * it + u, u)
                    part2(2 * it + u, u)
                    place_xT(2 * it + 2 + u, u)
            for u in range(2):
                part1(NTILES - 2 + u, u)
                part2(NTILES - 2 + u, u)
            gate(act, 0)

            def store_scores(s):
                hold(act, (s_scores_T, s + 1))
                mv(line[:, ds(s * P, P)], bank(6, P)).then_inc(s_scores, 1)

            def last_onehot(s, g):
                j = (g + 1) * ITEM_GROUP - 1
                n = s * GROUPS + g
                hold(act, (s_hot_a, n))
                nc.scalar.activation(dist, iotab[:, :], ACT.Abs, scale=-1.0,
                                     bias=rel_item[:, ds(s * CHUNKS + j, 1)]).then_inc(s_dist, 1)
                hold(act, (s_dist, n + 1), (s_hot_T, n - 3))
                nc.scalar.activation(hot[:, j, :], dist, ACT.Relu, scale=-1.0, bias=ones[:, 0:1])\
                    .then_inc(s_hot_a, 1)

            def score_step(s, first=False):
                hold(act, (s_flags_T, s))
                for wide, item in ((fwide, f_item), (gwide, g_item)):
                    mv(wide[:, :, :], item[:, ds(s * CHUNKS, CHUNKS)].unsqueeze(2)
                       .to_broadcast([P, CHUNKS, H])).then_inc(s_wide, 1)
                for g in range(GROUPS):
                    n = s * GROUPS + g
                    hold(act, (s_q_e, n - 3), (s_hot_T, n + 1))
                    mv(hotT[:, items_of(g), :], hot_ps(g)).then_inc(s_hotT, 1)
                    last_onehot(s + (g + 2) // GROUPS, (g + 2) % GROUPS)
                    if g == 0:
                        hold(act, (s_flags_T, s + 1))
                        mv(fline[:, ds(s * P, P)], flag_ps(0)).then_inc(s_flags, 1)
                        mv(gline[:, ds(s * P, P)], flag_ps(1)).then_inc(s_flags, 1)
                if not first:
                    store_scores(s - 1)

            for g in range(2):
                last_onehot(0, g)
            score_step(0, True)
            with act.Fori(1, STEPS) as s:
                score_step(s)
            store_scores(STEPS - 1)
            gate(act, 1)

            nc.scalar.activation(junk, fline, ACT.Copy, accum_out=flag_sum[:, 0:1]).then_inc(s_fsum, 1)
            act.wait_ge(s_fsum, 1)
            nc.scalar.activation(junk, gline, ACT.Copy, accum_out=flag_sum[:, 1:2]).then_inc(s_fsum, 1)
            def exponentials(quad, u):
                hold(act, (s_slice_T, quad - 1))
                nc.scalar.activation(exslice[:, u, :], line[:, ds(quad * 4 * P, 4 * P)], ACT.Exp)\
                    .then_inc(s_slice, 1)

            for half, (a, b) in enumerate(((0, FIRST // 2), (FIRST // 2, QUADS // 2))):
                act.wait_ge(s_sub, half + 1)
                if a < b:
                    with act.Fori(a, b) as two:
                        for u in range(2):
                            exponentials(2 * two + u, u)
            if QUADS % 2:
                exponentials(QUADS - 1, 0)
            gate(act, 2)

            with act.Fori(0, STEPS) as s:
                for g in range(GROUPS):
                    n = s * GROUPS + g
                    j = (g + 1) * ITEM_GROUP - 1
                    hold(act, (s_hot32_a, n))
                    nc.scalar.activation(dist32, iota[:, :], ACT.Abs, scale=-1.0,
                                         bias=rel_item[:, ds(s * CHUNKS + j, 1)]).then_inc(s_dist32, 1)
                    hold(act, (s_dist32, n + 1), (s_y, n * ITEM_GROUP - 12))
                    nc.scalar.activation(hot32[:, j, :], dist32, ACT.Relu, scale=-1.0, bias=ones[:, 0:1])\
                        .then_inc(s_hot32_a, 1)
                    mv(kt[:, g, 0:ITEM_GROUP * ROW].rearrange("p (a r) -> p a r", r=ROW)[:, :, D:ROW],
                       ex_all[:, ds(s * P + g * ITEM_GROUP * H, ITEM_GROUP * H)]
                       .rearrange("p (a h) -> p a h", h=H)).then_inc(s_wex, 1)
                    hold(act, (s_back[g], (s + 1) * 16))
                    for h in range(H):
                        part = rows_of(g)[:, ITEM_GROUP - 1, h * DH:(h + 1) * DH]
                        last = mv(part, part, scale=ex_all[:, ds(s * P + j * H + h, 1)])
                    last.then_inc(s_wv_a, 1)
            gate(act, 3)

            with act.Fori(0, PAIRS) as p:
                nc.scalar.activation(warm[:, :], ones[:, :], ACT.Gelu)
                for f in range(FC):
                    hold(act, (f_h, p * FC + f + 1))
                    nc.scalar.activation(gelu[:, f, :], bank(4 + f % 2, 2 * P), ACT.Gelu,
                                         bias=bias1[:, f:f + 1]).then_inc(f_gelu, 1)

        @block.tensor
        def _(pe):
            mm = nc.tensor.matmul
            tr = nc.tensor.transpose
            pe.wait_ge(s_const, 11)
            pe.wait_ge(s_ended, TCH)
            for c in range(TCH):
                last = mm(bank(6)[0:NEDGE, 0:1], ended[:, c, :], ones[:, 0:1], start=(c == 0), stop=(c == TCH - 1))
            last.then_inc(s_ends_ps, 1)
            pe.wait_ge(s_past, 1)
            for m in range(CCH):
                mm(bank(6, 1, m), past[0:NEDGE, m * P:(m + 1) * P], ones[0:NEDGE, 0:1], start=True, stop=True)
                mm(bank(6, 1, 64 + m), icol[0:1, m * P:(m + 1) * P], ones[0:1, 0:1], start=True, stop=True)
            mm(bank(7)[0:1, 0:HALF], ones[0:NEDGE, 0:1], past[0:NEDGE, 0:HALF], start=True, stop=True)
            mm(bank(5)[0:1, 0:COLS - HALF], ones[0:NEDGE, 0:1], past[0:NEDGE, HALF:COLS], start=True, stop=True)\
                .then_inc(s_item_ps, 1)

            def transpose_x(n, u, first=False):
                if not first:
                    need(pe, s_xT, (n - 1) * DC)
                need(pe, s_xn, n + 1)
                for c in range(DC):
                    last = tr(bank(u, P, c * P), xn[:, u, c * P:(c + 1) * P], ident[:, :])
                last.then_inc(s_xT_ps, 1)

            def project(n, u):
                need(pe, s_xT, n * DC + DC)
                need(pe, s_q32, n - 1) if not (isinstance(n, int) and n < 2) else None
                for c in range(DC):
                    last = mm(bank(2 + u, D), xnT[:, u, c, :], w_qkv[:, c, 0:D],
                              start=(c == 0), stop=(c == DC - 1))
                last.then_inc(s_q_ps, 1)
                need(pe, s_kv, n - 1) if not (isinstance(n, int) and n < 2) else None
                for c in range(DC):
                    last = mm(bank(4 + u), xnT[:, u, c, :], w_qkv[:, c, D:3 * D],
                              start=(c == 0), stop=(c == DC - 1))
                last.then_inc(s_kv_ps, 1)

            pe.wait_ge(s_load, 16 * 8)
            transpose_x(0, 0, True)
            transpose_x(1, 1, True)
            pe.wait_ge(s_tidx, 3)
            project(0, 0)
            with pe.Fori(0, PAIRS - 1) as it:
                transpose_x(2 * it + 2, 0)
                project(2 * it + 1, 1)
                transpose_x(2 * it + 3, 1)
                project(2 * it + 2, 0)
            project(NTILES - 1, 1)
            for n, rows in enumerate((rel_f, f_f, g_f, src_f, g_w, off_f)):
                pe.wait_ge(s_derived, n + 1)
                if n >= 2:
                    pe.wait_ge(s_item, n - 1)
                for m in range(CCH):
                    at = (6 - n % 2 * 6) * 512 + m * P
                    last = tr(ps[:, at:at + P], rows[:, m, :], ident[:, :])
                last.then_inc(s_rows_T, 1)
            gate(pe, 0)

            def transpose_scores(s, flags_stored):
                need(pe, s_flags, flags_stored)
                need(pe, s_scores, s)
                need(pe, s_masked, s + 1)
                tr(bank(6, P), masked.rearrange("p a b -> p (a b)"), ident[:, :]).then_inc(s_scores_T, 1)

            def project_edges(n, g, step):
                need(pe, s_added, n - 1)
                need(pe, s_ef[g], (step + 1) * 16 * ITEM_GROUP)
                for i in range(ITEM_GROUP):
                    last = mm(ep_ps(g)[:, i * DH:(i + 1) * DH], efT[0:ED + 1, g * ITEM_GROUP + i, :],
                              we[:, :], start=True, stop=True)
                last.then_inc(s_ep, 1)

            def transpose_hot(n, g):
                need(pe, s_hotT, n)
                need(pe, s_hot, n + 1)
                need(pe, s_hot_a, n + 1)
                for i in range(ITEM_GROUP):
                    last = tr(hot_ps(g)[:, i, :], hot[:, g * ITEM_GROUP + i, :], identb[:, :])
                last.then_inc(s_hot_T, 1)

            def score_step(s, first=False, final=False):
                for g in range(GROUPS):
                    n = s * GROUPS + g
                    blocks = load_group(ENG.PE, block_row, s, g, BLOCKS - 1)
                    if not (final and g == GROUPS - 1):
                        project_edges(n + 1, (g + 1) % GROUPS, s + (g + 1) // GROUPS)
                    if g == 0:
                        need(pe, s_scores, s - 1)
                        need(pe, s_wide, 2 * s + 2)
                        tr(flag_ps(0), fwide.rearrange("p a b -> p (a b)"), identb[:, :])
                        tr(flag_ps(1), gwide.rearrange("p a b -> p (a b)"), identb[:, :])\
                            .then_inc(s_flags_T, 1)
                    if not (final and g == GROUPS - 1):
                        transpose_hot(n + 1, (g + 1) % GROUPS)
                    if g == 2 and not first:
                        transpose_scores(s - 1, 2 * s + 2)
                    need(pe, s_prod, n - 1)
                    need(pe, s_hotT, n + 1)
                    for i in range(ITEM_GROUP):
                        j = g * ITEM_GROUP + i
                        for part in range(3):
                            last = mm(ps[:, (g % 2) * 1024 + i * D:(g % 2) * 1024 + (i + 1) * D],
                                      hotT[:, j, :], part_of(blocks[i], part), start=(part == 0), stop=(part == 2))
                    last.then_inc(s_q_e, 1)

            pe.wait_ge(s_efone, 1)
            project_edges(0, 0, 0)
            transpose_hot(0, 0)
            score_step(0, True)
            with pe.Fori(1, STEPS - 1) as s:
                score_step(s)
            score_step(STEPS - 1, final=True)
            transpose_scores(STEPS - 1, 2 * STEPS)
            gate(pe, 1)

            for back in range(2):
                pe.wait_ge(s_scan, back + 1)
                pe.wait_ge(s_fsum, back + 1)
                at_end = reach[:, LINE - 1:LINE] if not back else reach[:, 0:1]
                mm(bank(0)[0:1, 0:P], at_end, ident[:, :], start=True, stop=True)
                mm(bank(0)[0:1, P:2 * P], flag_sum[:, back:back + 1], ident[:, :], start=True, stop=True)\
                    .then_inc(s_edge, 1)
                pe.wait_ge(s_rows_c, back + 1)
                row = carry_row[0:1, 0:P] if not back else carry_row[0:1, H:H + P]
                mm(bank(1, 1), row, ones[0:1, 0:1], start=True, stop=True).then_inc(s_carry, 1)
            def transpose_quad(quad, u):
                need(pe, s_ex, quad - 1)
                need(pe, s_slice, quad + 1)
                for i in range(4):
                    last = tr(bank(6 + u, P, i * P), exslice[:, u, i * P:(i + 1) * P], ident[:, :])
                last.then_inc(s_slice_T, 1)

            if QUADS > 1:
                with pe.Fori(0, QUADS // 2) as two:
                    for u in range(2):
                        transpose_quad(2 * two + u, u)
            if QUADS % 2:
                transpose_quad(QUADS - 1, 0)
            gate(pe, 2)

            with pe.Fori(0, STEPS) as s:
                for g in range(GROUPS):
                    n = s * GROUPS + g
                    need(pe, s_hot32, n + 1)
                    need(pe, s_hot32_a, n + 1)
                    need(pe, s_wex, n + 1)
                    need(pe, s_wv, n + 1)
                    for j in range(g * ITEM_GROUP, (g + 1) * ITEM_GROUP):
                        need(pe, s_acc, s * CHUNKS + j - 7)
                        i = j % ITEM_GROUP
                        if i == ITEM_GROUP - 1:
                            need(pe, s_wv_a, n + 1)
                        mm(bank(j % 8, ROW), hot32[:, j, :], kt[:, g, i * ROW:(i + 1) * ROW], start=True, stop=True)\
                            .then_inc(s_y, 1)
            gate(pe, 3)

            def transpose_att(p):
                need(pe, f_attT, p)
                need(pe, f_att, 2 * p + 2)
                for u in range(2):
                    for c in range(DC):
                        last = tr(bank(0, P, c * 2 * P + u * P), att[:, u, c * P:(c + 1) * P], ident[:, :])
                last.then_inc(f_attT_ps, 1)

            def project_att(p):
                for u in range(2):
                    need(pe, f_x1a, 2 * p + u - 1)
                    need(pe, f_attT, p + 1)
                    for c in range(DC):
                        last = mm(bank(2 + u, D), attT[:, c, u * P:(u + 1) * P], w_o[:, c, :],
                                  start=(c == 0), stop=(c == DC - 1))
                    last.then_inc(f_wo, 1)

            def transpose_xn2(p):
                need(pe, f_xn2T, p)
                need(pe, f_xn2, 2 * p + 2)
                for u in range(2):
                    for c in range(DC):
                        last = tr(bank(1, P, c * 2 * P + u * P), xn2[:, u, c * P:(c + 1) * P], ident[:, :])
                last.then_inc(f_xn2T_ps, 1)

            def hidden(p):
                need(pe, f_xn2T, p + 1)
                for f in range(FC):
                    need(pe, f_gelu, p * FC + f - 1)
                    for c in range(DC):
                        last = mm(bank(4 + f % 2, 2 * P), w_1[:, c, f * P:(f + 1) * P], xn2T[:, c, :],
                                  start=(c == 0), stop=(c == DC - 1))
                    last.then_inc(f_h, 1)

            def mlp(p):
                need(pe, f_gelu, (p + 1) * FC)
                for u in range(2):
                    need(pe, f_y, 2 * p + u - 1)
                    for f in range(FC):
                        last = mm(bank(6 + u, D), gelu[:, f, u * P:(u + 1) * P], w_2[:, f, :],
                                  start=(f == 0), stop=(f == FC - 1))
                    last.then_inc(f_ff, 1)

            def pair(p, ahead=2):
                if ahead >= 1:
                    project_att(p + 1)
                hidden(p)
                if ahead >= 1:
                    transpose_xn2(p + 1)
                if ahead >= 2:
                    transpose_att(p + 2)
                mlp(p)

            pe.wait_ge(s_w, 32)
            transpose_att(0)
            project_att(0)
            transpose_xn2(0)
            transpose_att(1)
            pe.wait_ge(s_w2, 16)
            with pe.Fori(0, PAIRS - 2) as p:
                pair(p)
            pair(PAIRS - 2, 1)
            pair(PAIRS - 1, 0)

        @block.vector
        def _(dve):
            v = nc.vector
            steps = [0]

            def step(ins):
                steps[0] += 1
                ins.then_inc(s_step, 1)
                dve.wait_ge(s_step, steps[0])

            dve.wait_ge(s_last, 16)
            dve.wait_ge(s_const, 11)
            step(v.tensor_copy(last_f[:, :], last_i[:, :]))
            for c in range(TCH):
                v.tensor_scalar(ended[:, c, :], thr[:, :], last_f[:, c:c + 1], None, ALU.is_gt)\
                    .then_inc(s_ended, 1)
            dve.wait_ge(s_ends_ps, 1)
            step(v.tensor_tensor(ends[0:NEDGE, :], bank(6)[0:NEDGE, 0:1], bcol[0:NEDGE, :], ALU.add))
            v.tensor_scalar(past[0:NEDGE, :], icol[0:NEDGE, :], ends[0:NEDGE, 0:1], None, ALU.is_gt)\
                .then_inc(s_past, 1)

            def statistics_x(p):
                for u in range(2):
                    v.bn_stats(ln_a[:, u, :], tile_of(x_all, 2 * p + u)).then_inc(s_bn, 1)

            def moments_x(p):
                hold(dve, (s_bn, 2 * p + 2))
                for u in range(2):
                    v.bn_aggr(mom_a[:, u, :], ln_a[:, u, :]).then_inc(s_mom, 1)
                need(dve, s_mom, 2 * p + 2)
                v.tensor_scalar(vare[:, ds(2 * p, 2)], mom_a[:, :, 1], EPS, None, ALU.add).then_inc(s_vare, 1)
                v.tensor_copy(moments[:, ds(2 * p, 2), :], mom_a[:, :, :]).then_inc(s_moms, 1)

            def shift_x(p):
                need(dve, s_moms, p + 1)
                need(dve, s_rstd, p + 1)
                v.tensor_tensor(shift[:, ds(2 * p, 2)], moments[:, ds(2 * p, 2), 0], rstd[:, ds(2 * p, 2)],
                                ALU.mult).then_inc(s_shift0, 1)
                need(dve, s_shift0, p + 1)
                v.tensor_scalar(shift[:, ds(2 * p, 2)], shift[:, ds(2 * p, 2)], -1.0, None, ALU.mult)\
                    .then_inc(s_shift, 1)

            dve.wait_ge(s_x[0], 16)
            dve.wait_ge(s_x[1], 16)
            statistics_x(0)
            moments_x(0)
            with dve.Fori(1, AHEAD) as p:
                statistics_x(p)
                shift_x(p - 1)
                moments_x(p)

            dve.wait_ge(s_item_ps, 1)
            step(v.tensor_copy(b7[:, :], bank(6, CCH)))
            step(v.tensor_tensor(t7[:, :], bank(6, CCH, 64), b7[:, :], ALU.subtract))
            v.tensor_copy(tile_index[:, :], t7[:, :]).then_inc(s_index_t, 1)
            v.tensor_scalar(b128[:, :], b7[:, :], float(P), None, ALU.mult)
            for a, b, source in ((0, HALF, bank(7)), (HALF, COLS, bank(5))):
                v.tensor_copy(block_row[0:1, a:b], source[0:1, 0:b - a])
                v.tensor_tensor(tile_rowf[0:1, a:b], icol[0:1, a:b], source[0:1, 0:b - a], ALU.subtract)\
                    .then_inc(s_tidx, 1)
            dve.wait_ge(s_tidx, 2)
            v.tensor_scalar(tile_row[0:1, 0:COLS], tile_rowf[0:1, :], float(P), None, ALU.mult)\
                .then_inc(s_tidx, 1)

            def biased(n, u, it=None):
                need(dve, s_rest1, n - 1)
                need(dve, s_q_ps, n + 1)
                v.tensor_tensor(q32[:, u, :], bank(2 + u, D), b_qkv[:, 0:D], ALU.add).then_inc(s_q32, 1)
                if it is not None:
                    dve.wait_ge(s_kv_out[u], it * 32)
                need(dve, s_kv_ps, n + 1)
                v.tensor_tensor(kv[:, u, :], bank(4 + u), b_qkv[:, D:3 * D], ALU.add).then_inc(s_kv, 1)

            def pair_and_ahead(p, it=None):
                shift_x(p + AHEAD - 1)
                statistics_x(p + AHEAD)
                biased(2 * p, 0, it)
                moments_x(p + AHEAD)
                biased(2 * p + 1, 1, it)

            dve.wait_ge(s_load, 16 * 8)
            for i in range(2, 5):
                dve.wait_ge(s_x[i], 16)
            pair_and_ahead(0)
            for part in range(3):
                with dve.Fori(1 + (MAIN - 1) * part // 3, 1 + (MAIN - 1) * (part + 1) // 3) as it:
                    pair_and_ahead(it, it)
                if part == 0:
                    dve.wait_ge(s_rows[0], 16 * CCH)
                    step(v.tensor_tensor(f_f, g_prev, g_dst, ALU.not_equal))
                    step(v.tensor_tensor(g_f, g_next, g_dst, ALU.not_equal))
                    step(v.tensor_tensor(rel_f, g_dst, b128[:, :].unsqueeze(2).to_broadcast([P, CCH, P]),
                                         ALU.subtract))
                if part == 1:
                    step(v.tensor_scalar(off_f, rel_f, 0.0, None, ALU.is_ge))
                    step(v.scalar_tensor_tensor(valid, rel_f, float(P), off_f, ALU.is_lt, ALU.mult))
                    step(v.scalar_tensor_tensor(f_f, f_f, -BIG, valid, ALU.mult, ALU.mult))
                    step(v.scalar_tensor_tensor(g_f, g_f, -BIG, valid, ALU.mult, ALU.mult))
                if part == 2:
                    shift_x(PAIRS - 1)
                    dve.wait_ge(s_rows[1], 16 * CCH)
                    step(v.tensor_copy(src_f, g_row[:, :, P + 2:]))
                    step(v.scalar_tensor_tensor(g_w, g_w, float(DH) ** -0.5, valid, ALU.mult, ALU.mult))
                    step(v.tensor_scalar(off_f, valid, BIG, -BIG, ALU.mult, ALU.add))
                    v.tensor_copy(t7[:, 0:1], b7[:, 0:1]).then_inc(s_derived, 6)

            with dve.Fori(MAIN, PAIRS) as it:
                for u in range(2):
                    biased(2 * it + u, u, it)
            for n, column in enumerate((rel_item, f_item, g_item, src_item, ews_item, off_item)):
                dve.wait_ge(s_rows_T, n + 1)
                at = (6 - n % 2 * 6) * 512
                v.tensor_copy(column[:, :], ps[:, at:at + WIDE]).then_inc(s_item, 1)
            dve.wait_ge(s_item, 6)
            gate(dve, 0)

            def indices(s, g):
                v.tensor_copy(index[:, items_of(g)], src_item[:, ds(s * CHUNKS + g * ITEM_GROUP, ITEM_GROUP)])\
                    .then_inc(s_idx, 1)

            def onehots(s, g):
                need(dve, s_hot_T, s * GROUPS + g - 3)
                for j in range(g * ITEM_GROUP, (g + 1) * ITEM_GROUP - 1):
                    last = v.tensor_scalar(hot[:, j, :], iotab[:, :], rel_item[:, ds(s * CHUNKS + j, 1)],
                                           None, ALU.is_equal)
                last.then_inc(s_hot, 1)

            def add_edges(s, g):
                dve.wait_ge(s_in[g], (s + 1) * 16 * ITEM_GROUP)
                need(dve, s_ep, s * GROUPS + g + 1)
                v.tensor_tensor(heads_of(g), heads_of(g),
                                ep_ps(g).rearrange("p (a d) -> p a d", d=DH)
                                .unsqueeze(2).to_broadcast([P, ITEM_GROUP, H, DH]), ALU.add)\
                    .then_inc(s_added, 1)

            def score_step(s, final=False):
                for g in range(GROUPS):
                    n = s * GROUPS + g
                    rows = rows_of(g)
                    need(dve, s_added, n + 1)
                    need(dve, s_q_e, n + 1)
                    v.tensor_tensor(rows, rows, ps[:, (g % 2) * 1024:(g % 2 + 1) * 1024]
                                    .rearrange("p (a d) -> p a d", d=D), ALU.mult).then_inc(s_prod, 1)
                    if not (final and g == GROUPS - 1):
                        add_edges(s + (g + 1) // GROUPS, (g + 1) % GROUPS)
                    need(dve, s_prod, n + 1)
                    v.tensor_reduce(raw[:, items_of(g), :], heads_of(g), AX.X, ALU.add).then_inc(s_raw, 1)
                    if not (final and g >= 1):
                        onehots(s + (g + 3) // GROUPS, (g + 3) % GROUPS)
                    need(dve, s_raw, n + 1)
                    indices(s + 1, g)
                step_cols = ds(s * CHUNKS, CHUNKS)
                v.tensor_tensor(scaled[:, :, :], raw[:, :, :], ews_item[:, step_cols].unsqueeze(2)
                                .to_broadcast([P, CHUNKS, H]), ALU.mult).then_inc(s_scaled, 1)
                need(dve, s_scaled, s + 1)
                need(dve, s_scores_T, s)
                v.tensor_tensor(masked[:, :, :], scaled[:, :, :], off_item[:, step_cols].unsqueeze(2)
                                .to_broadcast([P, CHUNKS, H]), ALU.add).then_inc(s_masked, 1)

            v.memset(efT[ED:ED + 1, :, :], 1.0).then_inc(s_efone, 1)
            for g in range(GROUPS):
                indices(0, g)
            for g in range(3):
                onehots(0, g)
            add_edges(0, 0)
            with dve.Fori(0, STEPS - 1) as s:
                score_step(s)
            score_step(STEPS - 1, True)
            gate(dve, 1)
            step(v.tensor_scalar(src_item[:, :], src_item[:, :], float(TABLE), None, ALU.add))
            for g in range(GROUPS):
                indices(0, g)

            def backwards(view, back):
                return view[:, ::-1] if back else view

            def scan(out, flags, values, start):
                return v.tensor_tensor_scan(out, flags, values, start, ALU.add, ALU.max)

            for back in range(2):
                flags = backwards((fline, gline)[back], back)
                out = backwards(reach, back)
                scan(out, flags, backwards((line, reach)[back], back), -BIG).then_inc(s_scan, 1)
                dve.wait_ge(s_scan, back + 1)
                dve.wait_ge(s_edge, back + 1)
                step(v.tensor_copy(edge_row[0:1, :, :], bank(0)[0:1, 0:2 * P].rearrange("p (a b) -> p a b", a=2)))
                step(v.memset(carry_row[0:1, :], -BIG))
                for h in range(H):
                    ends_h = edge_row[0:1, 0, h:P:H]
                    sums_h = edge_row[0:1, 1, h:P:H]
                    out_h = carry_row[0:1, h:P:H] if back else carry_row[0:1, H + h:H + P:H]
                    last = scan(backwards(out_h, back), backwards(sums_h, back), backwards(ends_h, back), -BIG)
                last.then_inc(s_rows_c, 1)
                dve.wait_ge(s_carry, back + 1)
                step(v.tensor_copy(carry[:, :], bank(1, 1)))
                step(scan(out, flags, out, carry[:, 0:1]))
            for half in range(2):
                a, b = ((0, SPLIT), (SPLIT, LINE))[half]
                v.tensor_tensor(line[:, a:b], line[:, a:b], reach[:, a:b], ALU.subtract).then_inc(s_sub, 1)

            def place_quad(quad, u):
                need(dve, s_slice_T, quad + 1)
                v.tensor_copy(ex_all[:, ds(quad * 4 * P, 4 * P)], bank(6 + u)).then_inc(s_ex, 1)

            if QUADS > 1:
                with dve.Fori(0, QUADS // 2) as two:
                    for u in range(2):
                        place_quad(2 * two + u, u)
            if QUADS % 2:
                place_quad(QUADS - 1, 0)
            need(dve, s_ex, QUADS)
            gate(dve, 2)

            def onehot32(s, g, i):
                j = g * ITEM_GROUP + i
                if i == ITEM_GROUP - 1:
                    return
                if i == 0:
                    need(dve, s_y, s * CHUNKS + j - 12)
                ins = v.tensor_scalar(hot32[:, j, :], iota[:, :], rel_item[:, ds(s * CHUNKS + j, 1)],
                                      None, ALU.is_equal)
                if i == ITEM_GROUP - 2:
                    ins.then_inc(s_hot32, 1)

            def weigh(s, g):
                most = ITEM_GROUP - 1
                ex = ex_all[:, ds(s * P + g * ITEM_GROUP * H, most * H)].rearrange("p (a h) -> p a h", h=H)
                dve.wait_ge(s_in[g], STEPS * 16 * ITEM_GROUP + (s + 1) * 16 * (ITEM_GROUP - 1))
                heads = heads_of(g)[:, 0:most]
                v.tensor_tensor(heads, heads, ex.unsqueeze(3).to_broadcast([P, most, H, DH]),
                                ALU.mult).then_inc(s_wv, 1)

            def sum_step(s, final=False):
                for g in range(GROUPS):
                    if not (final and g == GROUPS - 1):
                        weigh(s + (g + 1) // GROUPS, (g + 1) % GROUPS)
                    blocks = load_group(ENG.DVE, block_row, s, g, BLOCKS - 1)
                    for i in range(ITEM_GROUP):
                        j = g * ITEM_GROUP + i
                        need(dve, s_y, s * CHUNKS + j + 1)
                        need(dve, s_acc, s * CHUNKS + j)
                        v.tensor_tensor(tile_of(sums, blocks[i]), tile_of(sums, blocks[i]),
                                        bank(j % 8, ROW), ALU.add).then_inc(s_acc, 1)
                        if not (final and g >= GROUPS - 2):
                            onehot32(s + (g + 2) // GROUPS, (g + 2) % GROUPS, i)
                    indices(s + 1, g)

            for g in range(2):
                for i in range(ITEM_GROUP):
                    onehot32(0, g, i)
            weigh(0, 0)
            dve.wait_ge(s_zero, 2)
            with dve.Fori(0, STEPS - 1) as s:
                sum_step(s)
            sum_step(STEPS - 1, True)
            dve.wait_ge(f_bias, 32)
            v.tensor_scalar(bo_a, bo_row, alpha, None, ALU.mult).then_inc(f_rows, 1)
            v.tensor_scalar(b2_b, b2_row, beta, None, ALU.mult).then_inc(f_rows, 1)
            need(dve, s_acc, COLS)
            gate(dve, 3)

            dve.wait_ge(f_rows, 2)

            def attention(p):
                v.tensor_scalar(den[:, :, :], sums[:, ds(2 * p, 2), D:ROW], 0.5, None, ALU.max)\
                    .then_inc(f_den0, 1)
                need(dve, f_den0, p + 1)
                v.reciprocal(den[:, :, :], den[:, :, :]).then_inc(f_den, 1)
                need(dve, f_den, p + 1)
                need(dve, f_attT_ps, p)
                for u in range(2):
                    v.tensor_tensor(att[:, u, :].rearrange("p (h d) -> p h d", h=H),
                                    sums[:, ds(2 * p + u, 1), 0:D].rearrange("p t (h d) -> p (t h) d", h=H),
                                    den[:, u, :].unsqueeze(2).to_broadcast([P, H, DH]), ALU.mult)\
                        .then_inc(f_att, 1)

            def place_att(p):
                need(dve, f_wo, 2 * p)
                need(dve, f_attT_ps, p + 1)
                v.tensor_copy(attT.rearrange("p c n -> p (c n)"), bank(0)).then_inc(f_attT, 1)

            def place_xn2(p):
                need(dve, f_h, FC * p)
                need(dve, f_xn2T_ps, p + 1)
                for c in range(DC):
                    last = v.tensor_scalar(xn2T[:, c, :], bank(1, 2 * P, c * 2 * P), g2[:, c:c + 1],
                                           b2v[:, c:c + 1], ALU.mult, ALU.add)
                last.then_inc(f_xn2T, 1)

            def statistics(values, p, side):
                stat, mom, var, _, bn, moms, vars_, _ = side
                for u in range(2):
                    v.bn_stats(stat[:, u, :], values[:, u, :]).then_inc(bn, 1)
                hold(dve, (bn, 2 * p + 2))
                for u in range(2):
                    v.bn_aggr(mom[:, u, :], stat[:, u, :]).then_inc(moms, 1)
                need(dve, moms, 2 * p + 2)
                v.tensor_scalar(var[:, :], mom[:, :, 1], EPS, None, ALU.add).then_inc(vars_, 1)

            def normalised(values, p, side, out, done):
                _, mom, _, inv, _, _, _, invs = side
                need(dve, invs, p + 1)
                for u in range(2):
                    v.tensor_scalar(out[:, u, :], values[:, u, :], mom[:, u, 0:1], inv[:, u:u + 1],
                                    ALU.subtract, ALU.mult).then_inc(done, 1)

            side_a = (ln_a, mom_a, var_a, inv_a, f_bn1, f_mom1, f_var1, f_inv1)
            side_b = (ln_b, mom_b, var_b, inv_b, f_bn2, f_mom2, f_var2, f_inv2)

            def residual(p):
                need(dve, f_half, p)
                dve.wait_ge(f_x, (p + 1) * 16)
                for u in range(2):
                    need(dve, f_wo, 2 * p + u + 1)
                    v.scalar_tensor_tensor(x1[:, u, :], bank(2 + u, D), alpha, x_in[:, u, :],
                                           ALU.mult, ALU.add).then_inc(f_x1a, 1)
                for u in range(2):
                    need(dve, f_x1a, 2 * p + u + 1)
                    v.tensor_tensor(x1[:, u, :], x1[:, u, :], bo_a, ALU.add).then_inc(f_x1, 1)
                need(dve, f_x1, 2 * p + 2)
                statistics(x1, p, side_a)

            def normalise_x1(p):
                need(dve, f_xn2T_ps, p)
                normalised(x1, p, side_a, xn2, f_xn2)

            def sum_y(p, odd):
                need(dve, f_both, p + 1)
                for u in range(2):
                    need(dve, f_ff, 2 * p + u + 1)
                    v.scalar_tensor_tensor(y_sum[:, u, :], bank(6 + u, D), beta, both[odd][:, u, :],
                                           ALU.mult, ALU.add).then_inc(f_y, 1)

            def statistics_y(p):
                need(dve, f_y, 2 * p + 2)
                statistics(y_sum, p, side_b)

            def normalise_y(p, first=False):
                if not first:
                    dve.wait_ge(f_store, p * 16)
                normalised(y_sum, p, side_b, y_out, f_out)

            def pair(p, odd, first=False, ahead=2):
                if ahead >= 1:
                    residual(p + 1)
                if not first:
                    statistics_y(p - 1)
                if ahead >= 1:
                    normalise_x1(p + 1)
                if ahead >= 2:
                    attention(p + 2)
                if not first:
                    normalise_y(p - 1, isinstance(p, int) and p == 1)
                if ahead >= 1:
                    place_xn2(p + 1)
                if ahead >= 2:
                    place_att(p + 2)
                if not first:
                    need(dve, f_out, 2 * p)
                sum_y(p, odd)

            attention(0)
            place_att(0)
            residual(0)
            normalise_x1(0)
            attention(1)
            place_xn2(0)
            place_att(1)
            pair(0, 0, first=True)
            pair(1, 1)
            with dve.Fori(0, (PAIRS - 4) // 2) as two:
                pair(2 * two + 2, 0)
                pair(2 * two + 3, 1)
            for p in range(2 + (PAIRS - 4) // 2 * 2, PAIRS - 2):
                pair(p, p % 2)
            pair(PAIRS - 2, PAIRS % 2, ahead=1)
            pair(PAIRS - 1, 1 - PAIRS % 2, ahead=0)
            statistics_y(PAIRS - 1)
            normalise_y(PAIRS - 1)


def kernel(**inputs):
    import concourse.bacc as bacc
    from concourse.bass_utils import run_bass_kernel_spmd

    a = {k.removeprefix("L0_gnn_"): np.asarray(v) for k, v in inputs.items()}
    n_nodes, D = a["x"].shape
    n_edges = a["src"].shape[0]
    ED, DH = a["We"].shape
    FF = a["W1"].shape[1]
    Z = sizes(n_nodes, n_edges)
    rows, tiles = 2 * Z["pairs"] * P, Z["tile_chunks"] * P

    x = np.zeros((rows, D), a["x"].dtype)
    x[:n_nodes] = a["x"]
    beyond = Z["blocks"] * P
    dst = np.full(tiles * P + 2, beyond, np.int32)
    dst[0] = -1
    dst[1:n_edges + 1] = a["dst"]
    int_rows = np.zeros((tiles, 2 * P + 2), np.int32)
    int_rows[:, 0] = dst[:-2].reshape(tiles, P)[:, 0]
    int_rows[:, 1:P + 1] = dst[1:-1].reshape(tiles, P)
    int_rows[:, P + 1] = dst[2:].reshape(tiles, P)[:, P - 1]
    src = np.zeros(tiles * P, np.int32)
    src[:n_edges] = a["src"]
    int_rows[:, P + 2:] = src.reshape(tiles, P)
    ew = np.zeros(tiles * P, a["edge_weight"].dtype)
    ew[:n_edges] = a["edge_weight"]
    ef = np.zeros((ED, tiles * P), a["edge_attr_64"].dtype)
    ef[:, :n_edges] = a["edge_attr_64"].T

    def columns(v):
        return v.reshape(-1, P).T

    arrays = {
        "x": x, "int_rows": int_rows, "w_rows": ew.reshape(tiles, P),
        "dst_last": columns(dst[1:-1].reshape(tiles, P)[:, P - 1]),
        "efT": ef, "Wq": a["Wq"], "Wk": a["Wk"], "Wv": a["Wv"],
        "b_qkv": np.concatenate([a["bq"], a["bk"], a["bv"]]),
        "cols": np.concatenate([columns(a[k]) for k in ("ln1_g", "ln1_b", "ln2_g", "ln2_b", "b1")], axis=1),
        "alpha": a["alpha"], "beta": a["beta"], "We_be": np.concatenate([a["We"], a["be"][None]]),
        "Wo": a["Wo"], "W1": a["W1"], "W2": a["W2"], "bo": a["bo"], "b2": a["b2"],
    }
    nc = bacc.Bacc("TRN2", target_bir_lowering=False, num_devices=1)
    A, ins = {}, {}
    for name, v in arrays.items():
        v = np.ascontiguousarray(v)
        ins["in_" + name] = v
        A[name] = nc.dram_tensor("in_" + name, v.shape, mybir.dt.from_np(v.dtype), kind="ExternalInput").ap()
    A["out"] = nc.dram_tensor("out", (rows, D), mybir.dt.float32, kind="ExternalOutput").ap()
    graph_layer(nc, A, n_nodes, n_edges, (D, D // DH, ED, FF))
    r = run_bass_kernel_spmd(nc, [ins], core_ids=[0])
    return r.results[0]["out"][:n_nodes]
```
